# Optimizing a Trainium2 kernel written in Bass

```python
import numpy as np
import jax
import jax.numpy as jnp

def _softmax(x, axis=-1):
    return jax.nn.softmax(x, axis=axis)

def _gelu(x):
    return jax.nn.gelu(x, approximate=True)

def _silu(x):
    return jax.nn.silu(x)

def _sigmoid(x):
    return jax.nn.sigmoid(x)

def _layernorm(x, axis=-1, eps=1e-05):
    m = jnp.mean(x, axis=axis, keepdims=True)
    v = jnp.var(x, axis=axis, keepdims=True)
    return (x - m) / jnp.sqrt(v + eps)

def _scatter_add(tgt, idx, src, axis=0):
    return tgt.at[idx].add(src)

def _segment_sum(src, seg, n):
    return jax.ops.segment_sum(src, seg, n)
kernel_name = 'mk_xattn_ffn_d2_seqx_r8_cd7cf1'

def setup_inputs(seed: int=0):
    np.random.seed(seed)
    _w = jnp.asarray

    def _rec_inputs():
        import jax
        import jax.numpy as jnp
        _rk = jax.random.key(seed)
        x = 7.22e-05 + 1 * jax.random.normal(jax.random.fold_in(_rk, 1), (16, 64, 256), jnp.float32)
        _lenS = 64 - jax.random.randint(jax.random.fold_in(_rk, 7), (16,), 0, max(1, 64 // 4) + 1, jnp.int32)
        _lenS2 = 64 - jax.random.randint(jax.random.fold_in(_rk, 8), (16,), 0, max(1, 64 // 4) + 1, jnp.int32)
        _ctx_2048P = jax.random.normal(jax.random.fold_in(_rk, 11), (16, 16, 256), jnp.float32)
        _ctx_2048c = jax.random.dirichlet(jax.random.fold_in(_rk, 511), 0.3 * jnp.ones((16,), jnp.float32), (16, 64))
        _ctx_2048t = jnp.einsum('bsk,bkd->bsd', _ctx_2048c, _ctx_2048P)
        _ctx_2048t = _ctx_2048t * jax.lax.rsqrt(jnp.mean(jnp.square(_ctx_2048t)) + 1e-12) * 0.953939
        ctx_2048 = 4.13588e-05 + 0.999923 * (_ctx_2048t + 0.3 * jax.random.normal(jax.random.fold_in(_rk, 611), (16, 64, 256), jnp.float32))
        return (x, ctx_2048)
    x, ctx_2048 = _rec_inputs()

    def _L0_xattn_setup():
        import jax, jax.numpy as jnp
        import numpy as np
        N, E, T, H = (8, 64, 256, 8)
        key = jax.random.key(seed)
        ks = jax.random.split(key, 6)
        s = 1.0 / np.sqrt(E)
        return {'mask': jax.random.normal(ks[0], (N, E, T), jnp.float32), 'encodings': jax.random.normal(ks[1], (N, E, T), jnp.float32), 'w_in': jax.random.normal(ks[2], (3 * E, E), jnp.float32) * s, 'b_in': jnp.zeros((3 * E,), jnp.float32), 'w_out': jax.random.normal(ks[3], (E, E), jnp.float32) * s, 'b_out': jnp.zeros((E,), jnp.float32), 'w_ct': jax.random.normal(ks[4], (E, E), jnp.float32) * s, 'b_ct': jnp.zeros((E,), jnp.float32), 'local_size': 64}
    _L0_xattn_all = _L0_xattn_setup()
    _L0_xattn_in = {k: v for k, v in _L0_xattn_all.items() if k in ('w_in', 'b_in', 'w_out', 'b_out', 'w_ct', 'b_ct')}
    del _L0_xattn_all

    def _L0_ffn_setup():
        import jax, jax.numpy as jnp
        import numpy as np
        B, L, D = (4, 512, 256)
        DF = 4 * D
        CAPACITY_RATIO = 0.5
        key = jax.random.key(seed)
        ks = jax.random.split(key, 4)
        s = 0.02
        return {'x': jax.random.normal(ks[0], (B, L, D), dtype=jnp.float32), 'w_r': jax.random.normal(ks[1], (D,), dtype=jnp.float32) * s, 'b_r': jnp.zeros((), dtype=jnp.float32), 'w1': jax.random.normal(ks[2], (D, DF), dtype=jnp.float32) * s, 'b1': jnp.zeros((DF,), dtype=jnp.float32), 'w2': jax.random.normal(ks[3], (DF, D), dtype=jnp.float32) * s, 'b2': jnp.zeros((D,), dtype=jnp.float32)}
    _L0_ffn_all = _L0_ffn_setup()
    _L0_ffn_in = {k: v for k, v in _L0_ffn_all.items() if k in ('w_r', 'b_r', 'w1', 'b1', 'w2', 'b2')}
    del _L0_ffn_all

    def _L1_xattn_setup():
        import jax, jax.numpy as jnp
        import numpy as np
        import math
        EMBED = 256
        HEADS = 32
        GROUPS = 8
        GROUP_HEADS = HEADS // GROUPS
        HEAD_DIM = EMBED // HEADS
        B, S = (4, 128)
        key = jax.random.key(seed)
        ks = jax.random.split(key, 8)
        sc = 0.02
        return {'q': jax.random.normal(ks[0], (B, S, EMBED), jnp.float32), 'k': jax.random.normal(ks[1], (B, S, EMBED), jnp.float32), 'v': jax.random.normal(ks[2], (B, S, EMBED), jnp.float32), 'Wq': jax.random.normal(ks[3], (EMBED, EMBED), jnp.float32) * sc, 'Wk': jax.random.normal(ks[4], (GROUPS * HEAD_DIM, EMBED), jnp.float32) * sc, 'Wv': jax.random.normal(ks[5], (GROUPS * HEAD_DIM, EMBED), jnp.float32) * sc, 'Wfc': jax.random.normal(ks[6], (EMBED, EMBED), jnp.float32) * sc, 'bfc': jnp.zeros((EMBED,), jnp.float32)}
    _L1_xattn_all = _L1_xattn_setup()
    _L1_xattn_in = {k: v for k, v in _L1_xattn_all.items() if k in ('Wq', 'Wk', 'Wv', 'Wfc', 'bfc')}
    del _L1_xattn_all

    def _L1_ffn_setup():
        import jax, jax.numpy as jnp
        import numpy as np
        HID = 256
        INTER = 1024
        NEXP = 8
        TOPK = 2
        EPS = 1e-05

        def _mock_fused_moe(x, selected_experts, routing_weights, expert_weight):
            y = jnp.einsum('bsh,hd->bsd', x, expert_weight)
            scale = routing_weights.sum(axis=-1, keepdims=True)
            return y * scale
        key = jax.random.key(seed)
        ks = jax.random.split(key, 6)
        s = lambda fan_in: 1.0 / np.sqrt(fan_in)
        return {'hidden_states': jax.random.normal(ks[0], (4, 512, HID), dtype=jnp.float32), 'gate_w': jax.random.uniform(ks[1], (HID, NEXP), jnp.float32, -s(HID), s(HID)), 'up_w': jax.random.uniform(ks[2], (HID, INTER), jnp.float32, -s(HID), s(HID)), 'down_w': jax.random.uniform(ks[3], (INTER, HID), jnp.float32, -s(INTER), s(INTER)), 'expert_weight': jax.random.normal(ks[4], (HID, HID), dtype=jnp.float32), 'ln_gamma': jnp.ones((HID,), jnp.float32), 'ln_beta': jnp.zeros((HID,), jnp.float32)}
    _L1_ffn_all = _L1_ffn_setup()
    _L1_ffn_in = {k: v for k, v in _L1_ffn_all.items() if k in ('gate_w', 'up_w', 'down_w', 'expert_weight', 'ln_gamma', 'ln_beta')}
    del _L1_ffn_all
    return {'x': x, 'ctx_2048': ctx_2048, 'L0_xattn_w_in': _L0_xattn_in['w_in'], 'L0_xattn_b_in': _L0_xattn_in['b_in'], 'L0_xattn_w_out': _L0_xattn_in['w_out'], 'L0_xattn_b_out': _L0_xattn_in['b_out'], 'L0_xattn_w_ct': _L0_xattn_in['w_ct'], 'L0_xattn_b_ct': _L0_xattn_in['b_ct'], 'L0_ffn_w_r': _L0_ffn_in['w_r'], 'L0_ffn_b_r': _L0_ffn_in['b_r'], 'L0_ffn_w1': _L0_ffn_in['w1'], 'L0_ffn_b1': _L0_ffn_in['b1'], 'L0_ffn_w2': _L0_ffn_in['w2'], 'L0_ffn_b2': _L0_ffn_in['b2'], 'L1_xattn_Wq': _L1_xattn_in['Wq'], 'L1_xattn_Wk': _L1_xattn_in['Wk'], 'L1_xattn_Wv': _L1_xattn_in['Wv'], 'L1_xattn_Wfc': _L1_xattn_in['Wfc'], 'L1_xattn_bfc': _L1_xattn_in['bfc'], 'L1_ffn_gate_w': _L1_ffn_in['gate_w'], 'L1_ffn_up_w': _L1_ffn_in['up_w'], 'L1_ffn_down_w': _L1_ffn_in['down_w'], 'L1_ffn_expert_weight': _L1_ffn_in['expert_weight'], 'L1_ffn_ln_gamma': _L1_ffn_in['ln_gamma'], 'L1_ffn_ln_beta': _L1_ffn_in['ln_beta']}

def reference(x, ctx_2048, L0_xattn_w_in, L0_xattn_b_in, L0_xattn_w_out, L0_xattn_b_out, L0_xattn_w_ct, L0_xattn_b_ct, L0_ffn_w_r, L0_ffn_b_r, L0_ffn_w1, L0_ffn_b1, L0_ffn_w2, L0_ffn_b2, L1_xattn_Wq, L1_xattn_Wk, L1_xattn_Wv, L1_xattn_Wfc, L1_xattn_bfc, L1_ffn_gate_w, L1_ffn_up_w, L1_ffn_down_w, L1_ffn_expert_weight, L1_ffn_ln_gamma, L1_ffn_ln_beta):
    import jax
    import jax.numpy as jnp

    def _L0_xattn_ref(mask, encodings, w_in, b_in, w_out, b_out, w_ct, b_ct, local_size):
        import jax, jax.numpy as jnp
        import numpy as np
        N, E, T, H = (8, 64, 256, 8)
        n, e, t = mask.shape
        d = e // H
        x = jnp.transpose(mask, (0, 2, 1))
        qkv = x @ w_in.T + b_in
        q, k, v = jnp.split(qkv, 3, axis=-1)
        q = q.reshape(n, t, H, d)
        k = k.reshape(n, t, H, d)
        v = v.reshape(n, t, H, d)
        scores = jnp.einsum('bqhd,bkhd->bhqk', q, k) / jnp.sqrt(jnp.asarray(d, q.dtype))
        idx = jnp.arange(t)
        band = jnp.abs(idx[:, None] - idx[None, :]) <= local_size
        neg = jnp.asarray(jnp.finfo(scores.dtype).min, scores.dtype)
        scores = jnp.where(band[None, None], scores, neg)
        attn = jax.nn.softmax(scores, axis=-1)
        o = jnp.einsum('bhqk,bkhd->bqhd', attn, v).reshape(n, t, e)
        o = o @ w_out.T + b_out
        o = jnp.transpose(o, (0, 2, 1))
        y = jax.nn.relu(o) * encodings
        out = jnp.einsum('nit,io->not', y, w_ct) + b_ct[None, :, None]
        return out

    def _L0_ffn_ref(x, w_r, b_r, w1, b1, w2, b2):
        import jax, jax.numpy as jnp
        import numpy as np
        B, L, D = (4, 512, 256)
        DF = 4 * D
        CAPACITY_RATIO = 0.5
        b, l, d = x.shape
        k = int(l * CAPACITY_RATIO)
        scores = jnp.einsum('bld,d->bl', x, w_r) + b_r
        _, idx = jax.lax.top_k(scores, k)
        x_sel = jnp.take_along_axis(x, idx[:, :, None], axis=1)
        h = jax.nn.gelu(jnp.einsum('bkd,df->bkf', x_sel, w1) + b1)
        out_sel = jnp.einsum('bkf,fd->bkd', h, w2) + b2
        batch_ix = jnp.arange(b)[:, None]
        out = jnp.zeros_like(x).at[batch_ix, idx].set(out_sel)
        return out

    def _L1_xattn_ref(q, k, v, Wq, Wk, Wv, Wfc, bfc):
        import jax, jax.numpy as jnp
        import numpy as np
        import math
        EMBED = 256
        HEADS = 32
        GROUPS = 8
        GROUP_HEADS = HEADS // GROUPS
        HEAD_DIM = EMBED // HEADS
        B, S = (4, 128)
        N, S_, _ = q.shape
        qh = (q @ Wq.T).reshape(N, S_, HEADS, HEAD_DIM).transpose(0, 2, 1, 3)
        kh = (k @ Wk.T).reshape(N, S_, GROUPS, HEAD_DIM).transpose(0, 2, 1, 3)
        vh = (v @ Wv.T).reshape(N, S_, GROUPS, HEAD_DIM).transpose(0, 2, 1, 3)
        kh = jnp.repeat(kh, GROUP_HEADS, axis=1)
        vh = jnp.repeat(vh, GROUP_HEADS, axis=1)
        score = jnp.einsum('bhqd,bhkd->bhqk', qh, kh) / math.sqrt(HEAD_DIM)
        attn = jax.nn.softmax(score, axis=-1)
        out = jnp.einsum('bhqk,bhkd->bhqd', attn, vh)
        out = out.transpose(0, 2, 1, 3).reshape(N, S_, EMBED)
        return out @ Wfc.T + bfc

    def _L1_ffn_ref(hidden_states, gate_w, up_w, down_w, expert_weight, ln_gamma, ln_beta):
        import jax, jax.numpy as jnp
        import numpy as np
        HID = 256
        INTER = 1024
        NEXP = 8
        TOPK = 2
        EPS = 1e-05

        def _mock_fused_moe(x, selected_experts, routing_weights, expert_weight):
            y = jnp.einsum('bsh,hd->bsd', x, expert_weight)
            scale = routing_weights.sum(axis=-1, keepdims=True)
            return y * scale
        residuals = hidden_states
        logits = jnp.einsum('bsh,he->bse', hidden_states, gate_w)
        routing_weights, selected_experts = jax.lax.top_k(logits, TOPK)
        h = jnp.einsum('bsh,hi->bsi', residuals, up_w)
        h = jnp.square(jax.nn.relu(h))
        shared_out = jnp.einsum('bsi,ih->bsh', h, down_w)
        moe_out = _mock_fused_moe(hidden_states, selected_experts, routing_weights, expert_weight)
        y = shared_out + moe_out
        mu = y.mean(axis=-1, keepdims=True)
        var = jnp.mean(jnp.square(y - mu), axis=-1, keepdims=True)
        return (y - mu) * jax.lax.rsqrt(var + EPS) * ln_gamma + ln_beta
    x = x + _L0_xattn_ref(_layernorm(x, axis=-1), ctx_2048, L0_xattn_w_in, L0_xattn_b_in, L0_xattn_w_out, L0_xattn_b_out, L0_xattn_w_ct, L0_xattn_b_ct, 64)
    x = x + _L0_ffn_ref(_layernorm(x, axis=-1), L0_ffn_w_r, L0_ffn_b_r, L0_ffn_w1, L0_ffn_b1, L0_ffn_w2, L0_ffn_b2)
    x = x + _L1_xattn_ref(_layernorm(x, axis=-1), ctx_2048, ctx_2048, L1_xattn_Wq, L1_xattn_Wk, L1_xattn_Wv, L1_xattn_Wfc, L1_xattn_bfc)
    x = x + _L1_ffn_ref(_layernorm(x, axis=-1), L1_ffn_gate_w, L1_ffn_up_w, L1_ffn_down_w, L1_ffn_expert_weight, L1_ffn_ln_gamma, L1_ffn_ln_beta)
    return x

_drawn_inputs = setup_inputs


def setup_inputs(seed=0):
    import zlib

    import numpy as np

    out = dict(_drawn_inputs(seed))
    spreads = {'L0_xattn_b_in': (0.0, 0.1),
     'L0_xattn_b_out': (0.0, 0.1),
     'L0_xattn_b_ct': (0.0, 0.1),
     'L0_ffn_b1': (0.0, 0.31),
     'L0_ffn_b2': (0.0, 0.1),
     'L1_xattn_bfc': (0.0, 0.1),
     'L1_ffn_ln_gamma': (1.0, 0.2),
     'L1_ffn_ln_beta': (0.0, 0.1)}
    factors = {'L1_xattn_Wq': 8.0, 'L1_xattn_Wk': 8.0}
    for name, (base, spread) in spreads.items():
        noise = np.random.default_rng([zlib.crc32(name.encode()), seed]).standard_normal(out[name].shape)
        drawn = base * np.exp(spread * noise) if base else spread * noise
        out[name] = jnp.asarray(drawn.astype(out[name].dtype))
    for name, factor in factors.items():
        out[name] = (out[name] * factor).astype(out[name].dtype)
    return out
```

```python
from contextlib import ExitStack

import numpy as np
import concourse.bass as bass
import concourse.mybir as mybir
from concourse.alu_op_type import AluOpType as ALU

F32 = mybir.dt.float32
F32R = mybir.dt.float32r
BF16 = mybir.dt.bfloat16
ACT = mybir.ActivationFunctionType
AX = mybir.AxisListType.X

P = 128
N, E, T = 16, 64, 256
TILES = N * E // P
H0, D0 = 8, 8
BAND = 64
WIN = 192
DF = 1024
FC = DF // P
KEEP = 32
SLOTS = TILES * 2 * KEEP
NEXP = 8
EPS = 1e-5
NEG = -1e30
SCALE = 1.0 / float(np.sqrt(8.0))

UNITS = 16
ST_LAG, PV_LAG = 11, 14
ALL_UNITS = UNITS * TILES


def r32(ap):
    return ap.bitcast(F32R)


def build(nc, a):
    ctx = ExitStack()
    with ctx:
        def sb(name, shape, dt=F32):
            return ctx.enter_context(nc.sbuf_tensor(name, shape, dt))

        def pb(name, shape, dt=F32):
            return ctx.enter_context(nc.psum_tensor(name, shape, dt))

        def sem(name):
            return ctx.enter_context(nc.semaphore(name))

        x = sb("x", [P, TILES, T])
        cx = sb("cx", [P, TILES, T])
        cxT = sb("cxT", [P, 2, N * E])
        ident = sb("ident", [P, P])
        identb = sb("identb", [P, P], BF16)
        band = sb("band", [P, 2, WIN], BF16)
        kmask = sb("kmask", [P, 4])
        cols = sb("cols", [P, 4])
        tri = sb("tri", [P, P])
        blk = sb("blk", [P, P])
        slot = sb("slot", [P, 2 * P])
        w0 = sb("w0", [P, 4, P])
        w0h = sb("w0h", [P, 4, P])
        w0l = sb("w0l", [P, 2, 4, P])
        b0 = sb("b0", [P, 4])
        sb0 = sb("sb0", [P, 4])
        wv0 = sb("wv0", [P, P])
        wo0 = sb("wo0", [P, P])
        wc0 = sb("wc0", [P, P])
        bcol = sb("bcol", [P, 4])
        vecs = sb("vecs", [P, 5, T])
        br = sb("br", [P, 1])
        b1 = sb("b1", [P, FC])
        w1 = sb("w1", [P, 2, DF])
        w2 = sb("w2", [P, FC, T])
        wq1 = sb("wq1", [P, 2, 2, 4, P])
        wk1 = sb("wk1", [P, 2, 2, P])
        wv1 = sb("wv1", [P, 2, 64])
        wf1 = sb("wf1", [P, 2, T])
        up = sb("up", [P, 2, DF])
        down = sb("down", [P, FC, T])
        eg = sb("eg", [P, 2, T + NEXP])
        st6 = sb("st6", [P, 2, 6])
        mv = sb("mv", [P, TILES, 2])
        rstd = sb("rstd", [P, TILES])
        xn = sb("xn", [P, 2, T])
        xs = sb("xs", [P, 2, T])
        hs = sb("hs", [P, 2, 2 * T])
        qp = sb("qp", [P, 2, 2, 2, T])
        kp = sb("kp", [P, 2, 2, T])
        kb = sb("kb", [P, 2, 2, 4, 2, T])
        v0 = sb("v0", [P, 2, 2, 2, 8, 32])
        mw = sb("mw", [P, 2, 4, P])
        ex = sb("ex", [P, 4, 4, WIN])
        osb = sb("osb", [P, 2, 512])
        rc = sb("rc", [P, 2, 32])
        on = sb("on", [P, 2, 2 * P])
        onT = sb("onT", [P, 2, T])
        yr = sb("yr", [P, 2, T])
        sc = sb("sc", [P, TILES])
        rk = sb("rk", [P, TILES])
        cmp = sb("cmp", [P, 3, P])
        exf = ex[:, :, :, :].rearrange("p a b c -> p (a b c)")
        sel = exf[:, 0:1024].rearrange("p (t c) -> p t c", t=TILES)
        selT = exf[:, 1024:2048].rearrange("p (t c) -> p t c", t=TILES)
        osel = exf[:, 2048:3072].rearrange("p (m c) -> p m c", m=4)
        hT = sb("hT", [P, FC, 512])
        xT = sb("xT", [P, 2, N * E])
        xsT = xT[:, :, 0:SLOTS]
        kbf = kb[:, :, :, :, :, :].rearrange("p a b c d e -> p (a b c d e)")
        q1 = kbf[:, 0:3072].rearrange("p (m g b c) -> p m g b c", m=3, g=2, b=2)
        k1 = kbf[:, 3072:6144].rearrange("p (m g b j c) -> p m g b j c", m=3, g=2, b=2, j=4)
        k1p = sb("k1p", [P, T])
        v1 = sb("v1", [P, 3, 2, 4, 32])
        tk = sb("tk", [P, 2, 8])

        S = [pb(f"S{i}", [P, 512]) for i in range(2)]
        ST = [pb(f"ST{i}", [P, 512]) for i in range(2)]
        O = pb("O", [P, 512])
        PJ = pb("PJ", [P, 512])
        MT = pb("MT", [P, 512])
        XB = pb("XB", [P, 512])

        names = ("ld_first ld_w0 ld_small ld_x ld_rest ld_late st_out "
                 "pe_proj pe_v pe_s pe_mt pe_st pe_pv pe_ot pe_bt pe_out pe_wct pe_bias "
                 "act_hs act_v act_mt act_exp act_o act_bt act_relu act_xh act_sb "
                 "dve_w dve_band dve_ln dve_xn dve_xl dve_mix dve_max dve_rc dve_on dve_y dve_x dve_zero "
                 "pool_rstd pool_kb pool_sel pool_zero "
                 "f_ln f_rstd f_xn f_sc f_cmp f_sel fp_sT f_pT fp_pT fp_x fa_x fp_up fa_up fp_dn f_dn fp_sc f_x "
                 "g_ln g_rstd g_xn gp_xT ga_xT gp_k ga_hk g_mk gpool_k gp_v ga_v gp_q ga_hq g_mq gp_s g_max gp_mt ga_mt "
                 "gp_st ga_ex gp_pv ga_o gp_ot g_rc g_on g_y gp_bt ga_bt gp_out g_x "
                 "h_ln h_rstd h_xn hp_xT ha_xT hp_up ha_up h_up hp_dn hp_eg h_tk h_moe h_ln2 h_rstd2 h_y h_out").split()
        s = {n: sem(n) for n in names}
        block = ctx.enter_context(nc.Block())

        def place(T_, l, lag):
            off, r = divmod(l - lag, UNITS)
            return T_ + off, r

        def live(tile, r):
            return 0 <= UNITS * tile + r < ALL_UNITS

        def parts(r):
            return r // 8, (r % 8) // 4, (r % 4) // 2, r % 2

        def xg(t, k):
            return x_norm(t)[:, P * k:P * k + P]

        def x_norm(t):
            return hT[:, t, 0:T]

        def e1(u):
            return ex[:, u % 4, :, :].rearrange("p a b -> p (a b)")[:, 0:512]

        SLOTS_ALL = [(n // UNITS, n % UNITS) for n in range(-UNITS, UNITS * (TILES + 2))]
        PROJ = {5: 0, 7: 1, 9: 2, 11: 3}

        @block.sync
        def _(sp):
            def load(dst, src, name):
                sp.dma_start(dst, src).then_inc(s[name], 16)
            xv = a["x"].rearrange("(t p) c -> p t c", p=P)
            load(x[:, 0, :], xv[:, 0, :], "ld_first")
            load(cols[:, :], a["cols"], "ld_first")
            load(w0[:, :, :], a["w0"], "ld_w0")
            load(b0[:, :], a["b0"], "ld_w0")
            load(kmask[:, :], a["kmask"], "ld_small")
            load(wv0[:, :], a["wv0"], "ld_small")
            load(exf[:, 0:2 * WIN], a["band"], "ld_small")
            load(ident[:, :], a["ident"], "ld_small")
            load(x[:, 1:TILES, :], xv[:, 1:TILES, :], "ld_x")
            load(wo0[:, :], a["wo0"], "ld_rest")
            load(wc0[:, :], a["wc0"], "ld_rest")
            load(bcol[:, :], a["bcol"], "ld_rest")
            load(cx[:, :, :], a["cx"].rearrange("(t p) c -> p t c", p=P), "ld_rest")
            late = [(vecs[:, :, :], a["vecs"][None, :, :].to_broadcast([P, 5, T])), (br[:, :], a["br"][:, :].to_broadcast([P, 1])),
                    (b1[:, :], a["b1"]), (tri[:, :], a["tri"]), (blk[:, :], a["blk"]), (slot[:, :], a["slot"]),
                    (w1[:, :, :], a["w1"].rearrange("(k p) f -> p k f", p=P)),
                    (w2[:, :, :], a["w2"].rearrange("(k p) f -> p k f", p=P)),
                    (wq1[:].rearrange("p a b c d -> p (a b c d)"), a["wq1"]), (wk1[:].rearrange("p a b c -> p (a b c)"), a["wk1"]),
                    (wv1[:, :, :], a["wv1"].rearrange("(k p) f -> p k f", p=P)),
                    (wf1[:, :, :], a["wf1"].rearrange("(k p) f -> p k f", p=P)),
                    (cxT[:, :, :], a["cxT"].rearrange("(k p) f -> p k f", p=P)),
                    (up[:, :, :], a["up"].rearrange("(k p) f -> p k f", p=P)),
                    (down[:, :, :], a["down"].rearrange("(k p) f -> p k f", p=P)),
                    (eg[:, :, 0:T], a["ew"].rearrange("(k p) f -> p k f", p=P)),
                    (eg[:, :, T:T + NEXP], a["gw"].rearrange("(k p) f -> p k f", p=P))]
            assert len(late) == 17
            for dst, src in late:
                load(dst, src, "ld_late")
            ov = a["out"].rearrange("(t p) c -> p t c", p=P)
            for t in range(TILES):
                sp.wait_ge(s["h_out"], t + 1)
                sp.dma_start(ov[:, t, :], x[:, t, :]).then_inc(s["st_out"], 16)
            sp.wait_ge(s["st_out"], 16 * TILES)
        LATE = 16 * 17

        @block.tensor
        def _(pe):
            mm, tr = nc.tensor.matmul, nc.tensor.transpose

            def project(t, n):
                p = t % 2
                if n == 0:
                    pe.wait_ge(s["act_xh"], t + 1)
                    pe.wait_ge(s["dve_xl"], t + 1)
                    if t == 0:
                        pe.wait_ge(s["dve_w"], 4)
                if 4 * t + n >= 1:
                    pe.wait_ge(s["dve_mix"], 4 * t + n)
                if n == 0 and t >= 1:
                    pe.wait_ge(s["act_v"], t)
                for b in range(2):
                    mm(PJ[:, T * b:T * b + T], r32(w0h[:, n, :]), r32(xs[:, b, :]), start=True, stop=False)
                    last = mm(PJ[:, T * b:T * b + T], r32(w0l[:, b, n, :]), r32(xs[:, b, :]), start=False, stop=True)
                last.then_inc(s["pe_proj"], 1)

            def values(t):
                pe.wait_ge(s["dve_mix"], 4 * t + 4)
                if t == 0:
                    pe.wait_ge(s["ld_small"], 64)
                pe.wait_ge(s["dve_xn"], t + 1)
                for c in range(2):
                    last = mm(PJ[:, P * c:P * c + P], xn[:, t % 2, P * c:P * c + P], wv0[:, :], start=True, stop=True)
                last.then_inc(s["pe_v"], 1)

            def slot_(T_, l):
                if T_ >= 0:
                    t, r = T_, l
                    if live(t, r):
                        n = UNITS * t + r
                        b, g, c, w = parts(r)
                        pe.wait_ge(s["pool_kb"], 4 * t + 2 * b + g + 1)
                        if n >= 2:
                            pe.wait_ge(s["dve_max"], n - 1)
                        mv_ = kb[:, t % 2, g, 2 * w:2 * w + 2, b, BAND * c:BAND * c + WIN]
                        out = S[n % 2][:, 0:2 * WIN].rearrange("p (h k) -> p h k", h=2)
                        mm(out, r32(qp[:, t % 2, g, b, P * c:P * c + P]), r32(mv_), start=True, stop=False)
                        mm(out, identb[:, :], band[:, c:c + 1, :].to_broadcast([P, 2, WIN]), start=False, stop=True)\
                            .then_inc(s["pe_s"], 1)
                    if l % 8 == 1:
                        t, r = place(T_, l, 9)
                        if live(t, r):
                            k = 2 * t + r // 8
                            pe.wait_ge(s["dve_max"], UNITS * t + r + 8)
                            if k >= 1:
                                pe.wait_ge(s["act_mt"], k)
                            for gc in range(4):
                                last = tr(MT[:, P * gc:P * gc + P], mw[:, (r // 8), gc, :], ident[:, :])
                            last.then_inc(s["pe_mt"], 1)
                    t, r = place(T_, l, ST_LAG)
                    if live(t, r):
                        n = UNITS * t + r
                        b, g, c, w = parts(r)
                        pe.wait_ge(s["act_mt"], 2 * t + b + 1)
                        if n >= 2:
                            pe.wait_ge(s["act_exp"], n - 1)
                        for h in range(2):
                            last = mm(ST[n % 2][:, WIN * h:WIN * h + WIN], r32(kb[:, t % 2, g, 2 * w + h, b, P * c:P * c + P]),
                                      r32(qp[:, t % 2, g, b, BAND * c:BAND * c + WIN]), start=True, stop=True)
                        last.then_inc(s["pe_st"], 1)
                    t, r = place(T_, l, PV_LAG)
                    if live(t, r):
                        n = UNITS * t + r
                        b, g, c, w = parts(r)
                        pe.wait_ge(s["pool_sel"], n // 2 + 1)
                        pe.wait_ge(s["act_v"], t + 1)
                        if r % 8 == 0 and n >= 8:
                            pe.wait_ge(s["act_o"], 2 * t + b)
                        for h in range(2):
                            j = 2 * w + h
                            last = mm(O[32 * j:32 * j + 32, T * g + BAND * c:T * g + BAND * c + WIN],
                                      v0[:, t % 2, c, b, 4 * g + j, :], ex[:, (n // 2) % 4, j, :],
                                      start=(c == 0), stop=(c == 1), skip_group_check=True)
                        last.then_inc(s["pe_pv"], 1)
                    if l % 8 == 7:
                        t, r = place(T_, l, 23)
                        if live(t, r):
                            k = 2 * t + r // 8
                            pe.wait_ge(s["act_o"], k + 1)
                            if k >= 1:
                                pe.wait_ge(s["dve_on"], k)
                            if k % 2 == 0 and k >= 2:
                                pe.wait_ge(s["dve_x"], k // 2)
                            for c in range(2):
                                for g in range(2):
                                    last = tr(XB[:, T * c + P * g:T * c + P * g + P], osb[:, k % 2, T * g + P * c:T * g + P * c + P], ident[:, :])
                            last.then_inc(s["pe_ot"], 1)
                    t = T_ - 2
                    if 0 <= t < TILES:
                        if l == 1:
                            pe.wait_ge(s["dve_on"], 2 * t + 2)
                            for c in range(2):
                                last = tr(XB[:, P * c:P * c + P], on[:, c, 0:P], ident[:, :])
                            last.then_inc(s["pe_bt"], 1)
                        if l == 3:
                            pe.wait_ge(s["act_bt"], t + 1)
                            mm(XB[:, 0:T], wo0[:, :], onT[:, t % 2, :], start=True, stop=True).then_inc(s["pe_out"], 1)
                        if l == 5:
                            pe.wait_ge(s["dve_y"], t + 1)
                            mm(XB[:, 0:T], wc0[:, :], yr[:, 1, :], start=True, stop=True).then_inc(s["pe_wct"], 1)
                if 0 <= T_ + 1 < TILES:
                    if l in PROJ:
                        project(T_ + 1, PROJ[l])
                    if l == 13:
                        values(T_ + 1)

            pe.wait_ge(s["ld_rest"], 64)
            pe.wait_ge(s["ld_small"], 64)
            mm(XB[:, 0:1], wo0[:, :], bcol[:, 0:1], start=True, stop=True).then_inc(s["pe_bias"], 1)
            for T_, l in SLOTS_ALL:
                if T_ == 0 and l == 0:
                    pe.wait_ge(s["dve_band"], 2)
                if T_ == 1 and l == 7:
                    pe.wait_ge(s["dve_w"], 5)
                slot_(T_, l)

            pe.wait_ge(s["ld_late"], LATE)
            for t in range(TILES):
                pe.wait_ge(s["f_sc"], t + 1)
                if t >= 2:
                    pe.wait_ge(s["f_cmp"], 2 * t - 3)
                tr(S[t % 2][:, 0:P], sc[:, t:t + 1].to_broadcast([P, P]), ident[:, :]).then_inc(s["fp_sT"], 1)
            for t in range(TILES):
                pe.wait_ge(s["f_sel"], t + 1)
                if t >= 2:
                    pe.wait_ge(s["f_pT"], t - 1)
                    pe.wait_ge(s["fa_x"], t - 1)
                tr(ST[t % 2][:, 0:P], sel[:, t, :], ident[:, :]).then_inc(s["fp_pT"], 1)
                o = (t % 2) * 64
                for k in range(2):
                    last = mm((O, PJ)[t % 2][:, 64 * k:64 * k + 64], xg(t, k), sel[:, t, o:o + 64], start=True, stop=True)
                last.then_inc(s["fp_x"], 1)
            FB = [S[0], S[1], MT, XB]
            pe.wait_ge(s["fa_x"], TILES)
            for f in range(FC):
                if f >= 4:
                    pe.wait_ge(s["fa_up"], f - 3)
                for k in range(2):
                    last = mm(FB[f % 4][:, :], w1[:, k, P * f:P * f + P], xsT[:, k, :], start=(k == 0), stop=(k == 1))
                last.then_inc(s["fp_up"], 1)
            for m in range(4):
                for f in range(FC):
                    if m == 0:
                        pe.wait_ge(s["fa_up"], f + 1)
                    last = mm((ST + [O, PJ])[m][:, 0:T], hT[:, f, P * m:P * m + P], w2[:, f, :], start=(f == 0), stop=(f == FC - 1))
                last.then_inc(s["fp_dn"], 1)
            pe.wait_ge(s["f_pT"], TILES)
            for t in range(TILES):
                pe.wait_ge(s["f_dn"], t // 2 + 1)
                if t >= 2:
                    pe.wait_ge(s["f_x"], t - 1)
                mm(S[t % 2][:, 0:T], selT[:, t, :], osel[:, t // 2, :], start=True, stop=True).then_inc(s["fp_sc"], 1)

            def slot1(n):
                t, l = divmod(n, 4)
                u = n
                if 0 <= u < 4 * TILES:
                    t1, l1 = divmod(u, 4)
                    b, g = divmod(l1, 2)
                    pe.wait_ge(s["gpool_k"], t1 + 1)
                    pe.wait_ge(s["g_mq"], 2 * t1 + g + 1)
                    if u >= 2:
                        pe.wait_ge(s["g_max"], u - 1)
                    for ii in range(2):
                        last = mm(S[u % 2][:, T * ii:T * ii + T], r32(q1[:, t1 % 3, g, b, P * ii:P * ii + P]),
                                  r32(k1[:, t1 % 3, g, b, :, :]), start=True, stop=True)
                    last.then_inc(s["gp_s"], 1)
                u = n - 3
                if n % 2 == 1 and 0 <= u < 4 * TILES:
                    k = u // 2
                    pe.wait_ge(s["g_max"], u + 2)
                    if k >= 1:
                        pe.wait_ge(s["ga_mt"], k)
                    for gi in range(4):
                        last = tr(MT[:, P * gi:P * gi + P], mw[:, k % 2, gi, :], ident[:, :])
                    last.then_inc(s["gp_mt"], 1)
                u = n - 5
                if 0 <= u < 4 * TILES:
                    t1, l1 = divmod(u, 4)
                    b, g = divmod(l1, 2)
                    pe.wait_ge(s["ga_mt"], u // 2 + 1)
                    if u >= 2:
                        pe.wait_ge(s["ga_ex"], u - 1)
                    for jp in range(2):
                        last = mm(ST[u % 2][:, T * jp:T * jp + T], r32(k1[:, t1 % 3, g, b, 2 * jp:2 * jp + 2, :]),
                                  r32(q1[:, t1 % 3, g, b, :]), start=True, stop=True)
                    last.then_inc(s["gp_st"], 1)
                u = n - 6
                if 0 <= u < 4 * TILES:
                    t1, l1 = divmod(u, 4)
                    b, g = divmod(l1, 2)
                    pe.wait_ge(s["ga_ex"], u + 1)
                    pe.wait_ge(s["ga_v"], 2 * t1 + 2)
                    if l1 == 0 and t1 >= 1:
                        pe.wait_ge(s["ga_o"], t1)
                    for jp in range(2):
                        pr = 2 * g + jp
                        last = mm(O[32 * pr:32 * pr + 32, T * b:T * b + T], v1[:, t1 % 3, b, pr, :], e1(u)[:, T * jp:T * jp + T],
                                  start=True, stop=True)
                    last.then_inc(s["gp_pv"], 1)
                u = n - 10
                if n % 4 == 2 and 0 <= u < 4 * TILES:
                    t1 = u // 4
                    pe.wait_ge(s["ga_o"], t1 + 1)
                    if t1 >= 1:
                        pe.wait_ge(s["g_x"], t1)
                    for i in range(4):
                        last = tr(XB[:, P * i:P * i + P], osb[:, t1 % 2, P * i:P * i + P], ident[:, :])
                    last.then_inc(s["gp_ot"], 1)
                u = n - 12
                if n % 4 == 0 and 0 <= u < 4 * TILES:
                    t1 = u // 4
                    pe.wait_ge(s["g_on"], t1 + 1)
                    for c in range(2):
                        last = tr(XB[:, P * c:P * c + P], on[:, t1 % 2, P * c:P * c + P], ident[:, :])
                    last.then_inc(s["gp_bt"], 1)
                u = n - 13
                if n % 4 == 1 and 0 <= u < 4 * TILES:
                    t1 = u // 4
                    pe.wait_ge(s["ga_bt"], t1 + 1)
                    for c in range(2):
                        last = mm(XB[:, 256:512], onT[:, t1 % 2, P * c:P * c + P], wf1[:, c, :], start=(c == 0), stop=(c == 1))
                    last.then_inc(s["gp_out"], 1)
                t1 = n // 4 + 1
                if 0 <= t1 < TILES:
                    tk_ = slice(P * t1, P * t1 + P)
                    if n % 4 == 0:
                        pe.wait_ge(s["g_xn"], t1 + 1)
                        if t1 >= 1:
                            pe.wait_ge(s["ga_v"], 2 * t1)
                        for k in range(2):
                            last = tr(PJ[:, P * k:P * k + P], xn[:, t1 % 2, P * k:P * k + P], ident[:, :])
                        last.then_inc(s["gp_xT"], 1)
                        pe.wait_ge(s["ga_xT"], t1 + 1)
                        for g in range(2):
                            for k in range(2):
                                last = mm(PJ[:, P * g:P * g + P], wk1[:, k, g, :], cxT[:, k, tk_], start=(k == 0), stop=(k == 1))
                        last.then_inc(s["gp_k"], 1)
                    if n % 4 in (1, 2):
                        g = n % 4 - 1
                        if g == 0:
                            pe.wait_ge(s["g_mk"], t1 + 1)
                        else:
                            pe.wait_ge(s["g_mq"], 2 * t1 + 1)
                        for i in range(4):
                            for k in range(2):
                                last = mm(PJ[:, P * i:P * i + P], wq1[:, k, g, i, :], xT[:, k, tk_], start=(k == 0), stop=(k == 1))
                        last.then_inc(s["gp_q"], 1)
                    if n % 4 == 3:
                        pe.wait_ge(s["g_mq"], 2 * t1 + 2)
                        for k in range(2):
                            last = mm(PJ[:, 0:64], cxT[:, k, tk_], wv1[:, k, :], start=(k == 0), stop=(k == 1))
                        last.then_inc(s["gp_v"], 1)
            for n in range(-4, 4 * TILES + 14):
                slot1(n)

            for t in range(TILES):
                pe.wait_ge(s["h_xn"], t + 1)
                if t >= 2:
                    pe.wait_ge(s["ha_xT"], t - 1)
                for k in range(2):
                    last = tr((MT, PJ)[t % 2][:, P * k:P * k + P], xn[:, t % 2, P * k:P * k + P], ident[:, :])
                last.then_inc(s["hp_xT"], 1)
            HB = [S[0], S[1], ST[0], ST[1]]
            for half in range(2):
                pe.wait_ge(s["ha_xT"], 4 * half + 4)
                for f in range(FC):
                    m = FC * half + f
                    if m >= 4:
                        pe.wait_ge(s["ha_up"], m - 3)
                    for k in range(2):
                        last = mm(HB[m % 4][:, :], up[:, k, P * f:P * f + P], xT[:, k, 512 * half:512 * half + 512],
                                  start=(k == 0), stop=(k == 1))
                    last.then_inc(s["hp_up"], 1)
                for m in range(4):
                    t = 4 * half + m
                    if t == 0:
                        pe.wait_ge(s["ha_xT"], TILES)
                    if t >= 2:
                        pe.wait_ge(s["h_y"], 4 * t - 7)
                    for k in range(2):
                        last = mm((O, PJ)[t % 2][:, 0:T + NEXP], xT[:, k, P * t:P * t + P], eg[:, k, :], start=(k == 0), stop=(k == 1))
                    last.then_inc(s["hp_eg"], 1)
                    for f in range(FC):
                        if m == 0:
                            pe.wait_ge(s["h_up"], FC * half + f + 1)
                        last = mm((MT, XB)[t % 2][:, 0:T], hT[:, f, P * m:P * m + P], down[:, f, :], start=(f == 0), stop=(f == FC - 1))
                    last.then_inc(s["hp_dn"], 1)

        @block.scalar
        def _(act):
            A = nc.scalar.activation

            def slot_(T_, l):
                if T_ >= 0:
                    t, r = place(T_, l, ST_LAG)
                    if live(t, r):
                        n = UNITS * t + r
                        b, g, c, w = parts(r)
                        act.wait_ge(s["pe_st"], n + 1)
                        if n >= 8:
                            act.wait_ge(s["pe_pv"], (n // 2 - 4) * 2 + 2)
                        A(ex[:, (n // 2) % 4, 2 * w:2 * w + 2, :], ST[n % 2][:, 0:2 * WIN].rearrange("p (h k) -> p h k", h=2),
                          ACT.Exp, scale=SCALE).then_inc(s["act_exp"], 1)
                    if l % 8 == 1:
                        t, r = place(T_, l, 9)
                        if live(t, r):
                            k = 2 * t + r // 8
                            act.wait_ge(s["pe_mt"], k + 1)
                            A(r32(qp[96:128, t % 2, :, r // 8, :].rearrange("p g (c q) -> p c g q", c=2)),
                              MT[96:128, :].rearrange("p (c g q) -> p c g q", c=2, g=2), ACT.Copy, scale=-1.0)\
                                .then_inc(s["act_mt"], 1)
                    if l % 8 == 5:
                        t, r = place(T_, l, 21)
                        if live(t, r):
                            k = 2 * t + r // 8
                            act.wait_ge(s["pe_pv"], 8 * k + 8)
                            if k >= 2:
                                act.wait_ge(s["pe_ot"], k - 1)
                            nc.scalar.copy(osb[:, k % 2, :], O[:, :]).then_inc(s["act_o"], 1)
                    t = T_ - 2
                    if 0 <= t < TILES:
                        if l == 1:
                            act.wait_ge(s["pe_bt"], t + 1)
                            nc.scalar.copy(onT[:, t % 2, :], XB[:, 0:T]).then_inc(s["act_bt"], 1)
                        if l == 3:
                            act.wait_ge(s["pe_out"], t + 1)
                            if t == 0:
                                act.wait_ge(s["dve_w"], 5)
                            if t >= 1:
                                act.wait_ge(s["dve_y"], t)
                            A(yr[:, 0, :], XB[:, 0:T], ACT.Relu, bias=bcol[:, 3:4]).then_inc(s["act_relu"], 1)
                if 0 <= T_ + 1 < TILES:
                    t = T_ + 1
                    if l == 4:
                        act.wait_ge(s["dve_xn"], t + 1)
                        if t >= 1:
                            act.wait_ge(s["pe_proj"], 4 * t)
                        A(r32(xs[0:64, 0, :]), xn[0:64, t % 2, :], ACT.Copy)
                        A(r32(xs[64:128, 1, :]), xn[64:128, t % 2, :], ACT.Copy).then_inc(s["act_xh"], 1)
                    if l in PROJ:
                        n = PROJ[l]
                        m = 4 * t + n
                        act.wait_ge(s["pe_proj"], m + 1)
                        if m == 0:
                            act.wait_ge(s["dve_w"], 4)
                        if m >= 2:
                            act.wait_ge(s["dve_mix"], m - 1)
                        A(r32(hs[:, m % 2, :]), PJ[:, :], ACT.Identity, bias=sb0[:, n:n + 1], scale=cols[:, n % 2:n % 2 + 1])\
                            .then_inc(s["act_hs"], 1)
                    if l == 13:
                        act.wait_ge(s["pe_v"], t + 1)
                        if t >= 2:
                            act.wait_ge(s["pe_pv"], UNITS * (t - 1))
                        nc.scalar.copy(v0[:, t % 2, :, :, :, 0:8].rearrange("p c b h d -> p (c b) h d"),
                                       PJ[:, 0:T].rearrange("p (c h d) -> p c h d", c=4, h=8)).then_inc(s["act_v"], 1)
            act.wait_ge(s["pool_zero"], 2)
            for T_, l in SLOTS_ALL:
                slot_(T_, l)

            for t in range(TILES):
                act.wait_ge(s["fp_pT"], t + 1)
                nc.scalar.copy(selT[:, t, :], ST[t % 2][:, 0:P]).then_inc(s["f_pT"], 1)
                act.wait_ge(s["fp_x"], t + 1)
                nc.scalar.copy(xsT[:, :, 64 * t:64 * t + 64], (O, PJ)[t % 2][:, 0:P].rearrange("p (k c) -> p k c", k=2)).then_inc(s["fa_x"], 1)
            FB = [S[0], S[1], MT, XB]
            act.wait_ge(s["fp_x"], TILES)
            for f in range(FC):
                act.wait_ge(s["fp_up"], f + 1)
                A(hT[:, f, :], FB[f % 4][:, :], ACT.Gelu_apprx_tanh, bias=b1[:, f:f + 1]).then_inc(s["fa_up"], 1)

            def slot1(n):
                u = n - 5
                if 0 <= u < 4 * TILES:
                    act.wait_ge(s["gp_st"], u + 1)
                    if u >= 4:
                        act.wait_ge(s["gp_pv"], u - 3)
                    A(e1(u), ST[u % 2][:, :], ACT.Exp, scale=SCALE).then_inc(s["ga_ex"], 1)
                u = n - 3
                if n % 2 == 1 and 0 <= u < 4 * TILES:
                    k = u // 2
                    t1, b = divmod(k, 2)
                    act.wait_ge(s["gp_mt"], k + 1)
                    A(r32(q1[96:128, t1 % 3, :, b, :]), MT[96:128, :].rearrange("p (g q) -> p g q", g=2), ACT.Copy, scale=-1.0).then_inc(s["ga_mt"], 1)
                u = n - 9
                if n % 4 == 1 and 0 <= u < 4 * TILES:
                    t1 = u // 4
                    act.wait_ge(s["gp_pv"], 4 * t1 + 4)
                    if t1 >= 2:
                        act.wait_ge(s["gp_ot"], t1 - 1)
                    nc.scalar.copy(osb[:, t1 % 2, :].rearrange("p (i b q) -> p b i q", b=2, i=4), O[:, :].rearrange("p (b i q) -> p b i q", b=2, i=4)).then_inc(s["ga_o"], 1)
                u = n - 12
                if n % 4 == 0 and 0 <= u < 4 * TILES:
                    t1 = u // 4
                    act.wait_ge(s["gp_bt"], t1 + 1)
                    nc.scalar.copy(onT[:, t1 % 2, :], XB[:, 0:T]).then_inc(s["ga_bt"], 1)
                t1 = n // 4 + 1
                if 0 <= t1 < TILES:
                    if n % 4 == 0:
                        act.wait_ge(s["gp_xT"], t1 + 1)
                        nc.scalar.copy(xT[:, :, P * t1:P * t1 + P], PJ[:, 0:T].rearrange("p (k c) -> p k c", k=2)).then_inc(s["ga_xT"], 1)
                        act.wait_ge(s["gp_k"], t1 + 1)
                        A(r32(hs[:, 0, 0:T]), PJ[:, 0:T], ACT.Identity, bias=0.0, scale=cols[:, 0:1]).then_inc(s["ga_hk"], 1)
                    if n % 4 in (1, 2):
                        g = n % 4 - 1
                        act.wait_ge(s["gp_q"], 2 * t1 + g + 1)
                        if g == 1:
                            act.wait_ge(s["g_mk"], t1 + 1)
                        A(r32(hs[:, 1 - g, :]), PJ[:, :], ACT.Identity, bias=0.0, scale=cols[:, 1:2]).then_inc(s["ga_hq"], 1)
                    if n % 4 == 3:
                        act.wait_ge(s["gp_v"], t1 + 1)
                        if t1 >= 3:
                            act.wait_ge(s["gp_pv"], 4 * (t1 - 2))
                        for b in range(2):
                            for j2 in range(2):
                                last = nc.scalar.copy(v1[64 * j2:64 * j2 + 64, t1 % 3, b, :, 16 * j2:16 * j2 + 8],
                                                      PJ[64 * b:64 * b + 64, 0:64].rearrange("p (r j d) -> p r j d", r=4, j=2)[:, :, j2, :])
                            last.then_inc(s["ga_v"], 1)
            act.wait_ge(s["pool_zero"], 5)
            for n in range(-4, 4 * TILES + 14):
                slot1(n)

            for t in range(TILES):
                act.wait_ge(s["hp_xT"], t + 1)
                nc.scalar.copy(xT[:, :, P * t:P * t + P], (MT, PJ)[t % 2][:, 0:T].rearrange("p (k c) -> p k c", k=2)).then_inc(s["ha_xT"], 1)
            HB = [S[0], S[1], ST[0], ST[1]]
            for m in range(2 * FC):
                act.wait_ge(s["hp_up"], m + 1)
                if m >= 2:
                    act.wait_ge(s["h_up"], m - 1)
                A(hs[:, m % 2, :], HB[m % 4][:, :], ACT.Relu).then_inc(s["ha_up"], 1)

        @block.gpsimd
        def _(pool):
            G = nc.gpsimd
            G.memset(v0[:, :, :, :, :, :], 0.0).then_inc(s["pool_zero"], 1)
            pool.wait_ge(s["pool_zero"], 1)
            G.memset(v0[:, :, :, :, :, 8:9], 1.0).then_inc(s["pool_zero"], 1)
            pool.wait_ge(s["ld_first"], 32)

            def keys(t, b, g):
                pool.wait_ge(s["dve_mix"], 4 * t + 2 * g + 1)
                if t == 0:
                    pool.wait_ge(s["ld_small"], 64)
                if t >= 2:
                    pool.wait_ge(s["pe_st"], UNITS * (t - 2) + 8 * b + 4 * g + 4)
                G.tensor_tensor(r32(kb[:, t % 2, g, :, b, :]), kp[:, g, b:b + 1, :].to_broadcast([P, 4, T]),
                                kmask[:, :, None].to_broadcast([P, 4, T]), ALU.mult).then_inc(s["pool_kb"], 1)

            KB = {8: (0, 0), 12: (0, 1), 14: (1, 0)}

            def slot_(T_, l):
                t = T_ + 1
                if l == 3 and 0 <= t < TILES:
                    pool.wait_ge(s["dve_ln"], 3 * t + 3)
                    G.tensor_tensor(rstd[:, t:t + 1], mv[:, t, 1:2], cols[:, 2:3], ALU.pow).then_inc(s["pool_rstd"], 1)
                if T_ >= 0:
                    t, r = place(T_, l, ST_LAG + 1)
                    if r % 2 == 0 and live(t, r):
                        n = UNITS * t + r
                        b, g, c, w = parts(r)
                        e = ex[:, (n // 2) % 4, :, :]
                        pool.wait_ge(s["act_exp"], n + 2)
                        if c == 0:
                            G.affine_select(out=e[:, :, 0:64], in_=e[:, :, 0:64], compare_op=ALU.is_ge, fill=0.0, base=BAND,
                                            pattern=[[0, 4], [1, 64]], channel_multiplier=-1)
                            G.affine_select(out=e[:, :, 64:WIN], in_=e[:, :, 64:WIN], compare_op=ALU.is_ge, fill=0.0, base=0,
                                            pattern=[[0, 4], [-1, 128]], channel_multiplier=1).then_inc(s["pool_sel"], 1)
                        else:
                            G.affine_select(out=e[:, :, 0:128], in_=e[:, :, 0:128], compare_op=ALU.is_ge, fill=0.0, base=0,
                                            pattern=[[0, 4], [1, 128]], channel_multiplier=-1)
                            G.affine_select(out=e[:, :, 128:WIN], in_=e[:, :, 128:WIN], compare_op=ALU.is_ge, fill=0.0, base=0,
                                            pattern=[[0, 4], [-1, 64]], channel_multiplier=1).then_inc(s["pool_sel"], 1)
                t = T_ + 1
                if l in KB and 0 <= t < TILES:
                    keys(t, *KB[l])
                if l == 1 and 0 <= T_ < TILES:
                    keys(T_, 1, 1)
            for T_, l in SLOTS_ALL:
                slot_(T_, l)

            pool.wait_ge(s["f_ln"], 17)
            G.tensor_tensor(rstd[:, :], mv[:, :, 1], cols[:, 2:3].to_broadcast([P, TILES]), ALU.pow).then_inc(s["f_rstd"], 1)

            G.memset(v1[:, :, :, :, :], 0.0).then_inc(s["pool_zero"], 1)
            pool.wait_ge(s["pool_zero"], 3)
            for j2 in range(2):
                G.memset(v1[64 * j2:64 * j2 + 64, :, :, :, 16 * j2 + 8:16 * j2 + 9], 1.0).then_inc(s["pool_zero"], 1)
                pool.wait_ge(s["pool_zero"], 4 + j2)
            for t in range(TILES):
                pool.wait_ge(s["g_ln"], 3 * t + 3)
                G.tensor_tensor(rstd[:, t:t + 1], mv[:, t, 1:2], cols[:, 2:3], ALU.pow).then_inc(s["g_rstd"], 1)
                pool.wait_ge(s["g_mk"], t + 1)
                if t >= 3:
                    pool.wait_ge(s["gp_st"], 4 * (t - 2))
                G.tensor_tensor(r32(k1[:, t % 3, :, :, :, :].rearrange("p g b j k -> p (g b) j k")),
                                k1p[:, :].rearrange("p (m k) -> p m k", m=4)[:, :, None, :].to_broadcast([P, 4, 4, 64]),
                                kmask[:, None, :, None].to_broadcast([P, 4, 4, 64]), ALU.mult).then_inc(s["gpool_k"], 1)

            for t in range(TILES):
                pool.wait_ge(s["h_ln"], 3 * t + 3)
                G.tensor_tensor(rstd[:, t:t + 1], mv[:, t, 1:2], cols[:, 2:3], ALU.pow).then_inc(s["h_rstd"], 1)
            for t in range(TILES):
                pool.wait_ge(s["h_ln2"], 3 * t + 3)
                G.tensor_tensor(rstd[:, t:t + 1], mv[:, t, 1:2], cols[:, 2:3], ALU.pow).then_inc(s["h_rstd2"], 1)

        @block.vector
        def _(dve):
            V = nc.vector

            def stats(t, src, name, k):
                V.bn_stats(st6[:, t % 2, :], src).then_inc(s[name], 1)
                dve.wait_ge(s[name], k + 1)
                V.bn_aggr(mv[:, t, :], st6[:, t % 2, :]).then_inc(s[name], 1)
                dve.wait_ge(s[name], k + 2)
                V.tensor_scalar(mv[:, t, 1:2], mv[:, t, 1:2], EPS, None, ALU.add).then_inc(s[name], 1)

            V.memset(w0l[:, :, :, :], 0.0).then_inc(s["dve_zero"], 1)
            V.memset(mw[:, :, :, :], 0.0).then_inc(s["dve_zero"], 1)
            dve.wait_ge(s["ld_w0"], 32)
            dve.wait_ge(s["ld_first"], 32)
            V.tensor_copy(r32(w0h[:, :, :]), w0[:, :, :]).then_inc(s["dve_w"], 1)
            for n in range(4):
                last = V.tensor_tensor(sb0[:, n:n + 1], b0[:, n:n + 1], cols[:, n % 2:n % 2 + 1], ALU.mult)
            last.then_inc(s["dve_w"], 1)
            dve.wait_ge(s["dve_w"], 2)
            dve.wait_ge(s["dve_zero"], 2)
            for b in range(2):
                hp = slice(64 * b, 64 * b + 64)
                V.tensor_tensor(r32(w0l[hp, b, :, :]), w0[hp, :, :], w0h[hp, :, :], ALU.subtract).then_inc(s["dve_w"], 1)

            dve.wait_ge(s["ld_small"], 64)
            V.tensor_copy(band[:, :, :], exf[:, 0:2 * WIN].rearrange("p (c k) -> p c k", c=2)).then_inc(s["dve_band"], 1)
            V.tensor_copy(identb[:, :], ident[:, :]).then_inc(s["dve_band"], 1)

            def slot_(T_, l):
                if T_ >= 0:
                    t, r = T_, l
                    if live(t, r):
                        n = UNITS * t + r
                        b, g, c, w = parts(r)
                        dve.wait_ge(s["pe_s"], n + 1)
                        if r % 8 == 0 and n >= 16:
                            dve.wait_ge(s["pe_mt"], 2 * t + b - 1)
                        V.tensor_reduce(mw[:, b, 2 * c + g, 96 + 2 * w:98 + 2 * w],
                                        S[n % 2][:, 0:2 * WIN].rearrange("p (h k) -> p h k", h=2), AX, ALU.max).then_inc(s["dve_max"], 1)
                    if l % 8 == 0:
                        t, r = place(T_, l, 24)
                        if live(t, r):
                            k = 2 * t + r // 8
                            b = k % 2
                            dve.wait_ge(s["pe_ot"], k + 1)
                            ot = XB[:, :].rearrange("p (c g f) -> p c g f", c=2, f=32)
                            V.reciprocal(rc[:, b, 0:16].rearrange("p (c g) -> p c g", c=2), ot[:, :, :, 8]).then_inc(s["dve_rc"], 1)
                            dve.wait_ge(s["dve_rc"], k + 1)
                            if b == 0 and t >= 1:
                                dve.wait_ge(s["pe_bt"], t)
                            V.tensor_tensor(on[:, :, 64 * b:64 * b + 64].rearrange("p c (g d) -> p c g d", g=8), ot[:, :, :, 0:8],
                                            rc[:, b, 0:16].rearrange("p (c g) -> p c g", c=2)[:, :, :, None].to_broadcast([P, 2, 8, 8]),
                                            ALU.mult).then_inc(s["dve_on"], 1)
                    t = T_ - 2
                    if 0 <= t < TILES:
                        if l == 4:
                            dve.wait_ge(s["act_relu"], t + 1)
                            if t == 0:
                                dve.wait_ge(s["ld_rest"], 64)
                            if t >= 1:
                                dve.wait_ge(s["pe_wct"], t)
                            V.tensor_tensor(yr[:, 1, :], yr[:, 0, :], cx[:, t, :], ALU.mult).then_inc(s["dve_y"], 1)
                        if l == 6:
                            dve.wait_ge(s["pe_wct"], t + 1)
                            V.scalar_tensor_tensor(out=x[:, t, :], in0=XB[:, 0:T], scalar=bcol[:, 2:3], in1=x[:, t, :],
                                                   op0=ALU.add, op1=ALU.add).then_inc(s["dve_x"], 1)
                if T_ == -1 and l == 15:
                    dve.wait_ge(s["pe_bias"], 1)
                    V.tensor_tensor(bcol[:, 3:4], XB[:, 0:1], bcol[:, 1:2], ALU.add).then_inc(s["dve_w"], 1)
                if 0 <= T_ + 1 < TILES:
                    t = T_ + 1
                    if l == 2:
                        if t == 1:
                            dve.wait_ge(s["ld_x"], 16)
                        if t >= 2:
                            dve.wait_ge(s["pe_v"], t - 1)
                        stats(t, x[:, t, :], "dve_ln", 3 * t)
                    if l == 3:
                        dve.wait_ge(s["pool_rstd"], t + 1)
                        V.tensor_scalar(xn[:, t % 2, :], x[:, t, :], mv[:, t, 0:1], rstd[:, t:t + 1], ALU.subtract, ALU.mult)\
                            .then_inc(s["dve_xn"], 1)
                    if l == 4:
                        dve.wait_ge(s["act_xh"], t + 1)
                        V.tensor_tensor(r32(xs[64:128, 0, :]), xn[0:64, t % 2, :], xs[0:64, 0, :], ALU.subtract)
                        V.tensor_tensor(r32(xs[0:64, 1, :]), xn[64:128, t % 2, :], xs[64:128, 1, :], ALU.subtract)\
                            .then_inc(s["dve_xl"], 1)
                    if l in PROJ:
                        n = PROJ[l]
                        m, g = 4 * t + n, n // 2
                        dve.wait_ge(s["act_hs"], m + 1)
                        if t >= 2 and n % 2:
                            dve.wait_ge(s["pe_st"], UNITS * (t - 2) + 8 + 4 * g + 4)
                        if n % 2 == 0 and t >= 1:
                            dve.wait_ge(s["pool_kb"], 4 * (t - 1) + 2 + g + 1)
                        dst = (qp[:, t % 2, g, :, :] if n % 2 else kp[:, g, :, :]).rearrange("p b q -> p (b q)")
                        V.scalar_tensor_tensor(out=r32(dst), in0=PJ[:, :], scalar=b0[:, n:n + 1], in1=hs[:, m % 2, :],
                                               op0=ALU.add, op1=ALU.subtract).then_inc(s["dve_mix"], 1)
            for T_, l in SLOTS_ALL:
                slot_(T_, l)

            for t in range(TILES):
                V.bn_stats(st6[:, t % 2, :], x[:, t, :]).then_inc(s["f_ln"], 1)
                dve.wait_ge(s["f_ln"], 2 * t + 1)
                V.bn_aggr(mv[:, t, :], st6[:, t % 2, :]).then_inc(s["f_ln"], 1)
            dve.wait_ge(s["f_ln"], 16)
            V.tensor_scalar(mv[:, :, 1], mv[:, :, 1], EPS, None, ALU.add).then_inc(s["f_ln"], 1)
            dve.wait_ge(s["f_rstd"], 1)
            dve.wait_ge(s["ld_late"], LATE)
            for t in range(TILES):
                V.tensor_scalar(x_norm(t), x[:, t, :], mv[:, t, 0:1], rstd[:, t:t + 1], ALU.subtract, ALU.mult).then_inc(s["f_xn"], 1)
                dve.wait_ge(s["f_xn"], 2 * t + 1)
                V.tensor_tensor_reduce(out=yr[:, 0, :], in0=x_norm(t), in1=vecs[:, 0, :], scale=1.0, scalar=0.0,
                                       op0=ALU.mult, op1=ALU.add, accum_out=sc[:, t:t + 1]).then_inc(s["f_xn"], 1)
                dve.wait_ge(s["f_xn"], 2 * t + 2)
                V.tensor_scalar(sc[:, t:t + 1], sc[:, t:t + 1], br[:, 0:1], None, ALU.add).then_inc(s["f_sc"], 1)
            for t in range(TILES):
                dve.wait_ge(s["fp_sT"], t + 1)
                if t == 0:
                    dve.wait_ge(s["f_sc"], TILES)
                sT = S[t % 2][:, 0:P]
                V.scalar_tensor_tensor(out=cmp[:, 0, :], in0=sT, scalar=sc[:, t:t + 1], in1=blk[:, :], op0=ALU.is_gt, op1=ALU.mult)
                V.scalar_tensor_tensor(out=cmp[:, 1, :], in0=sT, scalar=sc[:, t:t + 1], in1=tri[:, :], op0=ALU.is_equal, op1=ALU.mult)\
                    .then_inc(s["f_cmp"], 1)
                dve.wait_ge(s["f_cmp"], 2 * t + 1)
                V.tensor_tensor_reduce(out=cmp[:, 2, :], in0=cmp[:, 0, :], in1=cmp[:, 1, :], scale=1.0, scalar=0.0,
                                       op0=ALU.add, op1=ALU.add, accum_out=rk[:, t:t + 1]).then_inc(s["f_cmp"], 1)
                dve.wait_ge(s["f_cmp"], 2 * t + 2)
                V.tensor_scalar(sel[:, t, :], slot[:, P * (t % 2):P * (t % 2) + P], rk[:, t:t + 1], None, ALU.is_equal)\
                    .then_inc(s["f_sel"], 1)
            for m in range(4):
                dve.wait_ge(s["fp_dn"], m + 1)
                V.tensor_tensor(osel[:, m, :], (ST + [O, PJ])[m][:, 0:T], vecs[:, 1, :], ALU.add).then_inc(s["f_dn"], 1)
            for t in range(TILES):
                dve.wait_ge(s["fp_sc"], t + 1)
                V.tensor_tensor(x[:, t, :], S[t % 2][:, 0:T], x[:, t, :], ALU.add).then_inc(s["f_x"], 1)

            def slot1(n):
                u = n
                if 0 <= u < 4 * TILES:
                    k = u // 2
                    g = u % 2
                    dve.wait_ge(s["gp_s"], u + 1)
                    if k >= 2 and g == 0:
                        dve.wait_ge(s["gp_mt"], k - 1)
                    V.tensor_reduce(mw[:, k % 2, 2 * g:2 * g + 2, 96:100], S[u % 2][:, :].rearrange("p (i j k) -> p i j k", i=2, j=4),
                                    AX, ALU.max).then_inc(s["g_max"], 1)
                u = n - 11
                if n % 4 == 3 and 0 <= u < 4 * TILES:
                    t1 = u // 4
                    dve.wait_ge(s["gp_ot"], t1 + 1)
                    ot = XB[:, :].rearrange("p (i g f) -> p i g f", i=4, f=16)
                    rv = rc[:, t1 % 2, :].rearrange("p (i g) -> p i g", i=4)
                    V.reciprocal(rv, ot[:, :, :, 8]).then_inc(s["g_rc"], 1)
                    dve.wait_ge(s["g_rc"], t1 + 1)
                    if t1 >= 2:
                        dve.wait_ge(s["gp_bt"], t1 - 1)
                    V.tensor_tensor(on[:, t1 % 2, :].rearrange("p (g i d) -> p i g d", g=8, i=4), ot[:, :, :, 0:8],
                                    rv[:, :, :, None].to_broadcast([P, 4, 8, 8]), ALU.mult).then_inc(s["g_on"], 1)
                u = n - 14
                if n % 4 == 2 and 0 <= u < 4 * TILES:
                    t1 = u // 4
                    dve.wait_ge(s["gp_out"], t1 + 1)
                    V.tensor_tensor(yr[:, t1 % 2, :], XB[:, 256:512], x[:, t1, :], ALU.add).then_inc(s["g_y"], 1)
                    dve.wait_ge(s["g_y"], t1 + 1)
                    V.tensor_tensor(x[:, t1, :], yr[:, t1 % 2, :], vecs[:, 2, :], ALU.add).then_inc(s["g_x"], 1)
                t1 = n // 4 + 1
                if 0 <= t1 < TILES:
                    if n % 4 == 0:
                        dve.wait_ge(s["ga_hk"], t1 + 1)
                        if t1 >= 1:
                            dve.wait_ge(s["gpool_k"], t1)
                        V.scalar_tensor_tensor(out=r32(k1p[:, :]), in0=PJ[:, 0:T], scalar=kone(), in1=hs[:, 0, 0:T],
                                               op0=ALU.add, op1=ALU.subtract).then_inc(s["g_mk"], 1)
                    if n % 4 in (1, 2):
                        g = n % 4 - 1
                        dve.wait_ge(s["ga_hq"], 2 * t1 + g + 1)
                        if t1 >= 3:
                            dve.wait_ge(s["gp_st"], 4 * (t1 - 2))
                        V.tensor_tensor(r32(q1[:, t1 % 3, g, :, :].rearrange("p b (i q) -> p i b q", i=4)),
                                        PJ[:, :].rearrange("p (i b q) -> p i b q", i=4, b=2),
                                        hs[:, 1 - g, :].rearrange("p (i b q) -> p i b q", i=4, b=2), ALU.subtract).then_inc(s["g_mq"], 1)

            def kone():
                return cols[:, 3:4]

            def norm1(t):
                if t >= 2:
                    dve.wait_ge(s["gp_xT"], t - 1)
                stats(t, x[:, t, :], "g_ln", 3 * t)
                dve.wait_ge(s["g_rstd"], t + 1)
                V.tensor_scalar(xn[:, t % 2, :], x[:, t, :], mv[:, t, 0:1], rstd[:, t:t + 1], ALU.subtract, ALU.mult)\
                    .then_inc(s["g_xn"], 1)
            dve.wait_ge(s["f_x"], TILES)
            norm1(0)
            for n in range(-4, 4 * TILES + 14):
                slot1(n)
                if n % 4 == 3 and 0 <= n // 4 + 2 < TILES + 0 and n // 4 + 2 >= 1:
                    norm1(n // 4 + 2)

            for t in range(TILES):
                dve.wait_ge(s["g_x"], TILES)
                if t >= 2:
                    dve.wait_ge(s["hp_xT"], t - 1)
                stats(t, x[:, t, :], "h_ln", 3 * t)
                dve.wait_ge(s["h_rstd"], t + 1)
                V.tensor_scalar(xn[:, t % 2, :], x[:, t, :], mv[:, t, 0:1], rstd[:, t:t + 1], ALU.subtract, ALU.mult)\
                    .then_inc(s["h_xn"], 1)
            for half in range(2):
                for f in range(FC):
                    m = FC * half + f
                    dve.wait_ge(s["ha_up"], m + 1)
                    V.tensor_tensor(hT[:, f, :], hs[:, m % 2, :], hs[:, m % 2, :], ALU.mult).then_inc(s["h_up"], 1)
                for m in range(4):
                    t = 4 * half + m
                    dve.wait_ge(s["hp_eg"], t + 1)
                    gp = (O, PJ)[t % 2]
                    V.max(out=tk[:, t % 2, :], in_=gp[:, T:T + NEXP]).then_inc(s["h_tk"], 1)
                    dve.wait_ge(s["h_tk"], 2 * t + 1)
                    V.tensor_tensor(rk[:, t:t + 1], tk[:, t % 2, 0:1], tk[:, t % 2, 1:2], ALU.add).then_inc(s["h_tk"], 1)
                    dve.wait_ge(s["h_tk"], 2 * t + 2)
                    dve.wait_ge(s["hp_dn"], t + 1)
                    V.tensor_scalar(yr[:, 0, :], gp[:, 0:T], rk[:, t:t + 1], None, ALU.mult).then_inc(s["h_moe"], 1)
                    dve.wait_ge(s["h_moe"], t + 1)
                    V.tensor_tensor(yr[:, 1, :], (MT, XB)[t % 2][:, 0:T], yr[:, 0, :], ALU.add).then_inc(s["h_y"], 1)
                    dve.wait_ge(s["h_y"], 4 * t + 1)
                    stats(t, yr[:, 1, :], "h_ln2", 3 * t)
                    dve.wait_ge(s["h_rstd2"], t + 1)
                    V.tensor_scalar(yr[:, 0, :], yr[:, 1, :], mv[:, t, 0:1], rstd[:, t:t + 1], ALU.subtract, ALU.mult).then_inc(s["h_y"], 1)
                    dve.wait_ge(s["h_y"], 4 * t + 2)
                    V.tensor_tensor(yr[:, 1, :], yr[:, 0, :], vecs[:, 3, :], ALU.mult).then_inc(s["h_y"], 1)
                    dve.wait_ge(s["h_y"], 4 * t + 3)
                    V.tensor_tensor(yr[:, 0, :], yr[:, 1, :], vecs[:, 4, :], ALU.add).then_inc(s["h_y"], 1)
                    dve.wait_ge(s["h_y"], 4 * t + 4)
                    V.tensor_tensor(x[:, t, :], yr[:, 0, :], x[:, t, :], ALU.add).then_inc(s["h_out"], 1)


def constants():
    i = np.arange(P)
    ident = np.eye(P, dtype=np.float32)
    c = {"ident": ident}
    band = np.zeros((P, 2, WIN), np.float32)
    for ch in range(2):
        q = P * ch + i[:, None]
        k = BAND * ch + np.arange(WIN)[None, :]
        band[:, ch] = np.where(np.abs(q - k) <= BAND, 0.0, NEG)
    c["band"] = band.reshape(P, 2 * WIN)
    kmask = np.zeros((P, 4), np.float32)
    for r in range(3):
        for j in range(4):
            kmask[32 * r + 8 * j:32 * r + 8 * j + 8, j] = 1
    for j in range(4):
        kmask[96 + j, j] = 1
    c["kmask"] = kmask
    cols = np.zeros((P, 4), np.float32)
    cols[32:64, 0] = 1
    cols[64:96, 1] = 1
    cols[:, 2] = -0.5
    cols[96:128, 3] = 1
    c["cols"] = cols
    same = (i[:, None] // 64) == (i[None, :] // 64)
    c["blk"] = same.astype(np.float32)
    c["tri"] = (same & (i[None, :] < i[:, None])).astype(np.float32)
    slot = np.full((P, 2, 2, 2, KEEP), -1, np.float32)
    for par in range(2):
        for b in range(2):
            slot[64 * b:64 * b + 64, par, par, b] = np.arange(KEEP)
    c["slot"] = slot.reshape(P, 2 * P)
    return c


def kernel(**inputs):
    import concourse.bacc as bacc
    from concourse.bass_utils import run_bass_kernel_spmd

    f = {k: np.asarray(v) for k, v in inputs.items()}
    arr = constants()
    arr["x"] = f["x"].reshape(N * E, T)
    arr["cx"] = f["ctx_2048"].reshape(N * E, T)
    arr["cxT"] = np.ascontiguousarray(arr["cx"].T)
    w_in, b_in = f["L0_xattn_w_in"], f["L0_xattn_b_in"]
    w0 = np.zeros((P, 4, 4, 32), np.float32)
    b0 = np.zeros((4, 32, 4), np.float32)
    for n, (typ, g) in enumerate(((1, 0), (0, 0), (1, 1), (0, 1))):
        rows = slice(64 * typ + 32 * g, 64 * typ + 32 * g + 32)
        for r in range(3):
            w0[0:64, n, r] = w_in[rows].T
            w0[64:128, n, r] = w_in[rows].T
            b0[r, :, n] = b_in[rows]
        if typ:
            b0[3, :, n] = 1
    arr["w0"] = w0.reshape(P, 4, P)
    arr["b0"] = b0.reshape(P, 4)

    def twice(w):
        out = np.zeros((P, P), np.float32)
        out[0:64, 0:64] = w
        out[64:128, 64:128] = w
        return out
    arr["wv0"] = twice(w_in[128:192].T)
    arr["wo0"] = twice(f["L0_xattn_w_out"].T)
    arr["wc0"] = twice(f["L0_xattn_w_ct"])
    bcol = np.zeros((P, 4), np.float32)
    for k, v in enumerate((b_in[128:192], f["L0_xattn_b_out"], f["L0_xattn_b_ct"])):
        bcol[0:64, k] = v
        bcol[64:128, k] = v
    arr["bcol"] = bcol
    arr["vecs"] = np.stack([f["L0_ffn_w_r"], f["L0_ffn_b2"], f["L1_xattn_bfc"], f["L1_ffn_ln_gamma"], f["L1_ffn_ln_beta"]])
    arr["br"] = f["L0_ffn_b_r"].reshape(1, 1)
    arr["b1"] = np.ascontiguousarray(f["L0_ffn_b1"].reshape(FC, P).T)
    arr["w1"], arr["w2"] = f["L0_ffn_w1"], f["L0_ffn_w2"]
    wq = f["L1_xattn_Wq"].reshape(2, 4, 4, 8, 2, P)
    wq1 = np.zeros((P, 2, 2, 4, 4, 4, 8), np.float32)
    wk = f["L1_xattn_Wk"].reshape(2, 4, 8, 2, P)
    wk1 = np.zeros((P, 2, 2, 4, 4, 8), np.float32)
    for r in range(3):
        wq1[:, :, :, :, r] = wq.transpose(5, 4, 0, 2, 1, 3)
        wk1[:, :, :, r] = wk.transpose(4, 3, 0, 1, 2)
    arr["wq1"] = wq1.reshape(P, -1)
    arr["wk1"] = wk1.reshape(P, -1)
    arr["wv1"] = np.ascontiguousarray(f["L1_xattn_Wv"].T)
    arr["wf1"] = np.ascontiguousarray(f["L1_xattn_Wfc"].T)
    arr["up"], arr["down"] = f["L1_ffn_up_w"], f["L1_ffn_down_w"]
    arr["ew"], arr["gw"] = f["L1_ffn_expert_weight"], f["L1_ffn_gate_w"]

    nc = bacc.Bacc("TRN2", target_bir_lowering=False, num_devices=1)
    aps, feed = {}, {}
    for name, v in arr.items():
        v = np.ascontiguousarray(v)
        feed[f"in_{name}"] = v
        aps[name] = nc.dram_tensor(f"in_{name}", v.shape, mybir.dt.from_np(v.dtype), kind="ExternalInput").ap()
    aps["out"] = nc.dram_tensor("out_0", (N * E, T), F32, kind="ExternalOutput").ap()
    build(nc, aps)
    res = run_bass_kernel_spmd(nc, [feed], core_ids=[0])
    return res.results[0]["out_0"].reshape(N, E, T)
```

```python
from contextlib import ExitStack

import numpy as np
import concourse.bass as bass
import concourse.mybir as mybir
from concourse.alu_op_type import AluOpType as ALU

F32 = mybir.dt.float32
F32R = mybir.dt.float32r
BF16 = mybir.dt.bfloat16
ACT = mybir.ActivationFunctionType
AX = mybir.AxisListType.X

P = 128
N, E, T = 16, 64, 256
TILES = N * E // P
H0, D0 = 8, 8
BAND = 64
WIN = 192
DF = 1024
FC = DF // P
KEEP = 32
SLOTS = TILES * 2 * KEEP
NEXP = 8
EPS = 1e-5
NEG = -1e30
SCALE = 1.0 / float(np.sqrt(8.0))

UNITS = 16
ST_LAG, PV_LAG = 11, 16
ALL_UNITS = UNITS * TILES


def r32(ap):
    return ap.bitcast(F32R)


def build(nc, a):
    ctx = ExitStack()
    with ctx:
        def sb(name, shape, dt=F32):
            return ctx.enter_context(nc.sbuf_tensor(name, shape, dt))

        def pb(name, shape, dt=F32):
            return ctx.enter_context(nc.psum_tensor(name, shape, dt))

        def sem(name):
            return ctx.enter_context(nc.semaphore(name))

        x = sb("x", [P, TILES, T])
        cx = sb("cx", [P, TILES, T])
        cxT = sb("cxT", [P, 2, N * E])
        ident = sb("ident", [P, P])
        identb = sb("identb", [P, P], BF16)
        band = sb("band", [P, 2, WIN], BF16)
        kmask = sb("kmask", [P, 4])
        cols = sb("cols", [P, 4])
        tri = sb("tri", [P, P])
        blk = sb("blk", [P, P])
        slot = sb("slot", [P, 2 * P])
        w0 = sb("w0", [P, 4, P])
        w0h = sb("w0h", [P, 4, P])
        w0l = sb("w0l", [P, 2, 4, P])
        b0 = sb("b0", [P, 4])
        sb0 = sb("sb0", [P, 4])
        wv0 = sb("wv0", [P, P])
        wo0 = sb("wo0", [P, P])
        wc0 = sb("wc0", [P, P])
        bcol = sb("bcol", [P, 4])
        vecs = sb("vecs", [P, 5, T])
        br = sb("br", [P, 1])
        b1 = sb("b1", [P, FC])
        w1 = sb("w1", [P, 2, DF])
        w2 = sb("w2", [P, FC, T])
        wq1 = sb("wq1", [P, 2, T])
        spread = sb("spread", [P, 2, 4, P])
        wk1 = sb("wk1", [P, 2, 2, P])
        wv1 = sb("wv1", [P, 2, 64])
        wf1 = sb("wf1", [P, 2, T])
        up = sb("up", [P, 2, DF])
        down = sb("down", [P, FC, T])
        eg = sb("eg", [P, 2, T + NEXP])
        st6 = sb("st6", [P, 2, 6])
        mv = sb("mv", [P, TILES, 2])
        rstd = sb("rstd", [P, TILES])
        xn = sb("xn", [P, 2, T])
        xs = sb("xs", [P, 2, T])
        hs = sb("hs", [P, 2, 2 * T])
        qk = sb("qk", [P, 10240])
        qp = qk[:, 8192:10240].rearrange("p (m g b q) -> p m g b q", m=2, g=2, b=2)
        kp = sb("kp", [P, 2, 2, T])
        kb = qk[:, 0:8192].rearrange("p (m g j b k) -> p m g j b k", m=2, g=2, j=4, b=2)
        v0 = sb("v0", [P, 2, 2, 2, 8, 32])
        mw = sb("mw", [P, 2, 4, P])
        ex = sb("ex", [P, 4, 4, WIN])
        osb = sb("osb", [P, 2, 512])
        rc = sb("rc", [P, 2, 32])
        on = sb("on", [P, 2, 2 * P])
        onT = sb("onT", [P, 2, T])
        yr = sb("yr", [P, 2, T])
        sc = sb("sc", [P, TILES])
        rk = sb("rk", [P, TILES])
        cmp = sb("cmp", [P, 3, P])
        exf = ex[:, :, :, :].rearrange("p a b c -> p (a b c)")
        sel = sb("sel", [P, 2, P])
        osel = exf[:, 0:1024].rearrange("p (m c) -> p m c", m=4)
        hT = sb("hT", [P, FC, 512])
        xT = sb("xT", [P, 2, N * E])
        xsT = xT[:, :, 0:SLOTS]
        q1 = qk[:, 0:6144].rearrange("p (m g t b i q) -> p m g t b i q", m=3, g=2, t=2, b=2, i=4)
        k1 = qk[:, 6144:10240].rearrange("p (m g b j k) -> p m g b j k", m=4, g=2, b=2, j=4)
        k1p = kp[:, 0, :, :].rearrange("p b k -> p (b k)")
        k1h = xs[:, :, :].rearrange("p a k -> p (a k)")
        v1 = sb("v1", [P, 6, 2, 4, 32])
        tk = sb("tk", [P, 2, 8])

        S = [pb(f"S{i}", [P, 512]) for i in range(2)]
        ST = [pb(f"ST{i}", [P, 512]) for i in range(2)]
        O = pb("O", [P, 512])
        PJ = pb("PJ", [P, 512])
        MT = pb("MT", [P, 512])
        XB = pb("XB", [P, 512])

        names = ("ld_first ld_w0 ld_small ld_x1 ld_x ld_rest ld_late st_out "
                 "pe_proj pe_v pe_s pe_mt pe_st pe_pv pe_ot pe_bt pe_out pe_wct pe_bias "
                 "act_hs act_v act_mt act_exp act_o act_bt act_relu act_xh act_sb "
                 "dve_w dve_band dve_ln dve_xn dve_xl dve_mix dve_max dve_rc dve_on dve_x dve_zero "
                 "pool_var pool_rstd pool_mw dve_y pool_kb pool_sel pool_zero act_kb dve_spread ld_sel "
                 "f_ln f_rstd f_xn f_sc f_cmp f_sel fp_sT fp_x fa_x fp_up fa_up fp_dn f_dn fp_sc f_x "
                 "g_ln g_rstd g_xn gp_xT ga_xT gp_k ga_hk g_mk gpool_k gp_v ga_v gp_q ga_hq g_lq gp_e ga_q g_q gp_s g_max gp_mt ga_mt "
                 "gp_st ga_ex gp_pv ga_o gp_ot g_rc g_on g_y gp_bt ga_bt gp_out g_x "
                 "h_ln h_rstd h_xn hp_xT ha_xT hp_up ha_up h_up hp_dn hp_eg h_tk h_moe h_ln2 h_rstd2 h_y h_out").split()
        s = {n: sem(n) for n in names}
        block = ctx.enter_context(nc.Block())

        def place(T_, l, lag):
            off, r = divmod(l - lag, UNITS)
            return T_ + off, r

        def live(tile, r):
            return 0 <= UNITS * tile + r < ALL_UNITS

        def parts(r):
            return r // 8, (r % 8) // 4, (r % 4) // 2, r % 2

        def xg(t, k):
            return x_norm(t)[:, P * k:P * k + P]

        def proj_bank(t, n):
            return (PJ, S[1], S[0], ST[0])[n] if t == 0 else PJ

        def value_bank(t):
            return ST[1] if t == 0 else PJ

        def x_norm(t):
            return hT[:, t, 256:512]

        def selT(t):
            return xT[:, t // 4, SLOTS + P * (t % 4):SLOTS + P * (t % 4) + P]

        def up_bank(f):
            return S[f % 2][:, 0:T]

        def e1(u):
            return ex[:, u % 4, :, :].rearrange("p a b -> p (a b)")[:, 0:512]

        def q1f(t, g, b):
            return q1[:, (t // 2) % 3, g, t % 2, b, :, :].rearrange("p i q -> p (i q)")

        def relu(m):
            return cxT[:, m % 2, 0:512]

        def stacked(p, i):
            return r32(q1[:, p % 3, :, :, :, i, :].rearrange("p g t b q -> p g (t b) q"))

        def down_bank(c):
            return (O, PJ, ST[0], ST[1])[c][:, 0:T]

        def scatter_bank(t):
            return (XB, (ST[0], O)[t // 4])[t % 2][:, 0:T]

        def at(n, first, step, count):
            q, r = divmod(n - first, step)
            return q if r == 0 and 0 <= q < count else None

        PAIRS = TILES // 2
        SLOTS1 = range(-20, 52)
        SLOTS_ALL = [(n // UNITS, n % UNITS) for n in range(-2 * UNITS, UNITS * (TILES + 2) + 9)]
        PROJ = {3: 0, 6: 1, 9: 2, 12: 3}
        KB = {5: (0, 0), 9: (0, 1), 14: (1, 0)}
        KA = {11: 0, 12: 1, 15: 2, 18: 3}

        def tail(T_, l):
            n = UNITS * (T_ - TILES) + l - ST_LAG
            if 0 <= n < FC:
                return "up", n
            if FC <= n < 2 * FC:
                return "down", n - FC
            if 2 * FC <= n < 2 * FC + 4:
                return "scatter", n - 2 * FC
            return "", 0

        @block.sync
        def _(sp):
            def load(dst, src, name):
                sp.dma_start(dst, src).then_inc(s[name], 16)
            xv = a["x"].rearrange("(t p) c -> p t c", p=P)
            load(x[:, 0, :], xv[:, 0, :], "ld_first")
            load(cols[:, :], a["cols"], "ld_first")
            load(exf[:, 0:2 * WIN], a["band"], "ld_small")
            load(ident[:, :], a["ident"], "ld_small")
            load(x[:, 1, :], xv[:, 1, :], "ld_x1")
            load(x[:, 2:TILES, :], xv[:, 2:TILES, :], "ld_x")
            load(wo0[:, :], a["wo0"], "ld_rest")
            load(wc0[:, :], a["wc0"], "ld_rest")
            load(bcol[:, :], a["bcol"], "ld_rest")
            load(cx[:, :, :], a["cx"].rearrange("(t p) c -> p t c", p=P), "ld_rest")
            load(vecs[:, :, :], a["vecs"][None, :, :].to_broadcast([P, 5, T]), "ld_sel")
            load(br[:, :], a["br"][:, :].to_broadcast([P, 1]), "ld_sel")
            load(tri[:, :], a["tri"], "ld_sel")
            load(blk[:, :], a["blk"], "ld_sel")
            load(slot[:, :], a["slot"], "ld_sel")
            load(hT[:, 0:2, :].rearrange("p a b -> p (a b)"), a["spread"], "ld_sel")
            late = [(b1[:, :], a["b1"]),
                    (w1[:, :, :], a["w1"].rearrange("(k p) f -> p k f", p=P)),
                    (w2[:, :, :], a["w2"].rearrange("(k p) f -> p k f", p=P)),
                    (wq1[:, :, :], a["wq1"].rearrange("(k p) f -> p k f", p=P)), (wk1[:].rearrange("p a b c -> p (a b c)"), a["wk1"]),
                    (wv1[:, :, :], a["wv1"].rearrange("(k p) f -> p k f", p=P)),
                    (wf1[:, :, :], a["wf1"].rearrange("(k p) f -> p k f", p=P)),
                    (cxT[:, :, :], a["cxT"].rearrange("(k p) f -> p k f", p=P)),
                    (up[:, :, :], a["up"].rearrange("(k p) f -> p k f", p=P)),
                    (down[:, :, :], a["down"].rearrange("(k p) f -> p k f", p=P)),
                    (eg[:, :, 0:T], a["ew"].rearrange("(k p) f -> p k f", p=P)),
                    (eg[:, :, T:T + NEXP], a["gw"].rearrange("(k p) f -> p k f", p=P))]
            assert len(late) == 12
            for dst, src in late:
                load(dst, src, "ld_late")
            ov = a["out"].rearrange("(t p) c -> p t c", p=P)
            for t in range(TILES):
                sp.wait_ge(s["h_out"], t + 1)
                sp.dma_start(ov[:, t, :], x[:, t, :]).then_inc(s["st_out"], 16)
            sp.wait_ge(s["st_out"], 16 * TILES)
        LATE = 16 * 12

        @block.tensor
        def _(pe):
            mm, tr = nc.tensor.matmul, nc.tensor.transpose

            def project(t, n):
                if n == 0:
                    pe.wait_ge(s["act_xh"], t + 1)
                    pe.wait_ge(s["dve_xl"], t + 1)
                    if t == 0:
                        pe.wait_ge(s["dve_w"], 4)
                bank = proj_bank(t, n)
                if t >= 1:
                    pe.wait_ge(s["dve_mix"], 4 * t + n)
                if n == 0 and t >= 1:
                    pe.wait_ge(s["act_v"], t)
                for b in range(2):
                    mm(bank[:, T * b:T * b + T], r32(w0h[:, n, :]), r32(xs[:, b, :]), start=True, stop=False)
                    last = mm(bank[:, T * b:T * b + T], r32(w0l[:, b, n, :]), r32(xs[:, b, :]), start=False, stop=True)
                last.then_inc(s["pe_proj"], 1)

            def values(t):
                if t >= 1:
                    pe.wait_ge(s["dve_mix"], 4 * t + 4)
                if t == 0:
                    pe.wait_ge(s["ld_small"], 64)
                pe.wait_ge(s["dve_xn"], t + 1)
                for c in range(2):
                    last = mm(value_bank(t)[:, P * c:P * c + P], xn[:, t % 2, P * c:P * c + P], wv0[:, :], start=True, stop=True)
                last.then_inc(s["pe_v"], 1)

            def slot_(T_, l):
                t, r = T_, l
                if live(t, r):
                    n = UNITS * t + r
                    b, g, c, w = parts(r)
                    if (b, g) == (1, 1):
                        pe.wait_ge(s["act_kb"], t + 1)
                    else:
                        pe.wait_ge(s["pool_kb"], 3 * t + 1 + g + 2 * b)
                    if r in (0, 4):
                        pe.wait_ge(s["dve_mix"], 4 * t + 3 + g)
                    if n >= 2:
                        pe.wait_ge(s["dve_max"], n - 1)
                    mv_ = kb[:, t % 2, g, 2 * w:2 * w + 2, b, BAND * c:BAND * c + WIN]
                    out = S[n % 2][:, 0:2 * WIN].rearrange("p (h k) -> p h k", h=2)
                    mm(out, r32(qp[:, t % 2, g, b, P * c:P * c + P]), r32(mv_), start=True, stop=False)
                    mm(out, identb[:, :], band[:, c:c + 1, :].to_broadcast([P, 2, WIN]), start=False, stop=True)\
                        .then_inc(s["pe_s"], 1)
                t, r = place(T_, l, 9)
                if l % 8 == 1 and live(t, r):
                    k = 2 * t + r // 8
                    pe.wait_ge(s["dve_max"], UNITS * t + r + 8)
                    if k >= 1:
                        pe.wait_ge(s["act_mt"], k)
                    if l == 9 and T_ >= 3:
                        pe.wait_ge(s["fa_x"], T_ - 2)
                    for gc in range(4):
                        last = tr(MT[:, P * gc:P * gc + P], mw[:, (r // 8), gc, :], ident[:, :])
                    last.then_inc(s["pe_mt"], 1)
                t, r = place(T_, l, ST_LAG)
                if live(t, r):
                    n = UNITS * t + r
                    b, g, c, w = parts(r)
                    pe.wait_ge(s["act_mt"], 2 * t + b + 1)
                    if n >= 2:
                        pe.wait_ge(s["act_exp"], n - 1)
                    if n < 2:
                        pe.wait_ge(*((s["dve_mix"], 4), (s["act_v"], 1))[n])
                    for h in range(2):
                        last = mm(ST[n % 2][:, WIN * h:WIN * h + WIN], r32(kb[:, t % 2, g, 2 * w + h, b, P * c:P * c + P]),
                                  r32(qp[:, t % 2, g, b, BAND * c:BAND * c + WIN]), start=True, stop=True)
                    last.then_inc(s["pe_st"], 1)
                for t, r in {0: (), 1: (place(T_, l, PV_LAG + 1), place(T_, l, PV_LAG))}.get(l % 8, (place(T_, l, PV_LAG),)):
                    if not live(t, r):
                        continue
                    n = UNITS * t + r
                    b, g, c, w = parts(r)
                    pe.wait_ge(s["pool_sel"], n // 2 + 1)
                    pe.wait_ge(s["act_v"], t + 1)
                    if r % 8 == 0 and n >= 8:
                        pe.wait_ge(s["act_o"], n // 8)
                    for h in range(2):
                        j = 2 * w + h
                        last = mm(O[32 * j:32 * j + 32, T * g + BAND * c:T * g + BAND * c + WIN],
                                  v0[:, t % 2, c, b, 4 * g + j, :], ex[:, (n // 2) % 4, j, :],
                                  start=(c == 0), stop=(c == 1), skip_group_check=True)
                    last.then_inc(s["pe_pv"], 1)
                t, r = place(T_, l, 26)
                if l % 8 == 2 and live(t, r):
                    k = 2 * t + r // 8
                    pe.wait_ge(s["act_o"], k + 1)
                    if k >= 1:
                        pe.wait_ge(s["dve_on"], k)
                    if k % 2 == 0 and k >= 2:
                        pe.wait_ge(s["dve_x"], k // 2)
                    for c in range(2):
                        for g in range(2):
                            last = tr(XB[:, T * c + P * g:T * c + P * g + P], osb[:, k % 2, T * g + P * c:T * g + P * c + P], ident[:, :])
                    last.then_inc(s["pe_ot"], 1)
                t = T_ - 2
                if 0 <= t < TILES:
                    if l == 4:
                        pe.wait_ge(s["dve_on"], 2 * t + 2)
                        for c in range(2):
                            last = tr(XB[:, P * c:P * c + P], on[:, c, 0:P], ident[:, :])
                        last.then_inc(s["pe_bt"], 1)
                    if l == 5:
                        pe.wait_ge(s["act_bt"], t + 1)
                        mm(XB[:, 0:T], wo0[:, :], onT[:, t % 2, :], start=True, stop=True).then_inc(s["pe_out"], 1)
                    if l == 7:
                        pe.wait_ge(s["dve_y"], t + 1)
                        mm(XB[:, 0:T], wc0[:, :], yr[:, 1, :], start=True, stop=True).then_inc(s["pe_wct"], 1)
                t = T_ - 3
                if l == 2 and 0 <= t < TILES:
                    pe.wait_ge(s["f_sc"], t + 1)
                    pe.wait_ge(s["act_mt"], min(2 * T_, 2 * TILES))
                    if t >= 1:
                        pe.wait_ge(s["fa_x"], t)
                    tr(MT[:, 0:P], sc[:, t:t + 1].to_broadcast([P, P]), ident[:, :]).then_inc(s["fp_sT"], 1)
                if l == 6 and 0 <= t < TILES:
                    pe.wait_ge(s["f_sel"], t + 1)
                    tr(MT[:, 0:P], sel[:, t % 2, :], ident[:, :])
                    o = (t % 2) * 64
                    for k in range(2):
                        last = mm(MT[:, P + 64 * k:P + 64 * k + 64], xg(t, k), sel[:, t % 2, o:o + 64], start=True, stop=True)
                    last.then_inc(s["fp_x"], 1)
                if T_ + 1 >= 0 and T_ + 1 < TILES:
                    if l in PROJ:
                        project(T_ + 1, PROJ[l])
                    if l == 15:
                        values(T_ + 1)
                kind, n = tail(T_, l)
                if kind == "up":
                    ffn_up(0, n)
                if kind == "down":
                    for i in (2 * n, 2 * n + 1):
                        ffn_down(0, i // FC, i % FC)
                if kind == "scatter":
                    scatter(n)

            def ffn_up(half, f):
                m = FC * half + f
                if m == 0:
                    pe.wait_ge(s["ld_late"], LATE)
                    pe.wait_ge(s["dve_max"], ALL_UNITS)
                if f == 0:
                    pe.wait_ge(s["fa_x"], 4 * half + 4)
                if m >= 2:
                    pe.wait_ge(s["fa_up"], m - 1)
                for k in range(2):
                    last = mm(up_bank(f), w1[:, k, P * f:P * f + P], xsT[:, k, T * half:T * half + T], start=(k == 0), stop=(k == 1))
                last.then_inc(s["fp_up"], 1)

            def ffn_down(half, m, f):
                if (half, m, f) == (0, 0, 0):
                    pe.wait_ge(s["act_o"], 2 * TILES)
                    pe.wait_ge(s["act_v"], TILES)
                if (half, m, f) == (1, 0, 0):
                    pe.wait_ge(s["f_x"], 4)
                if m == 0:
                    pe.wait_ge(s["fa_up"], FC * half + f + 1)
                c = 2 * half + m
                last = mm(down_bank(c), hT[:, f, P * c:P * c + P], w2[:, f, :], start=(f == 0), stop=(f == FC - 1))
                if f == FC - 1:
                    last.then_inc(s["fp_dn"], 1)

            def scatter(t):
                pe.wait_ge(s["f_dn"], t // 2 + 1)
                if t == 0:
                    pe.wait_ge(s["dve_x"], TILES)
                    pe.wait_ge(s["act_exp"], ALL_UNITS)
                if t == 5:
                    pe.wait_ge(s["f_dn"], 1)
                elif t >= 2:
                    pe.wait_ge(s["f_x"], t - 1)
                mm(scatter_bank(t), selT(t), osel[:, t // 2, :], start=True, stop=True).then_inc(s["fp_sc"], 1)

            for T_, l in SLOTS_ALL:
                if T_ == 0 and l == 0:
                    pe.wait_ge(s["dve_band"], 2)
                if T_ == 1 and l == 0:
                    pe.wait_ge(s["ld_rest"], 64)
                    mm(XB[:, 0:1], wo0[:, :], bcol[:, 0:1], start=True, stop=True).then_inc(s["pe_bias"], 1)
                if T_ == 1 and l == 10:
                    pe.wait_ge(s["dve_w"], 5)
                slot_(T_, l)

            def slot1(n):
                f = at(n, -20, 1, FC)
                if f is not None:
                    ffn_up(1, f)
                i = at(n, -12, 1, FC)
                if i is not None:
                    for j in (2 * i, 2 * i + 1):
                        ffn_down(1, j // FC, j % FC)
                t = at(n, -4, 1, 4)
                if t is not None:
                    scatter(4 + t)
                u = at(n, 0, 1, 4 * TILES)
                if u is not None:
                    t, l = divmod(u, 4)
                    b, g = divmod(l, 2)
                    if l == 0:
                        pe.wait_ge(s["gpool_k"], t + 1)
                        pe.wait_ge(s["ga_q"], 2 * (t // 2) + 2)
                        pe.wait_ge(s["g_q"], 2 * (t // 2) + 2)
                    if u == 0:
                        pe.wait_ge(s["fa_up"], 2 * FC)
                    if u >= 2:
                        pe.wait_ge(s["g_max"], u - 1)
                    for ii in range(2):
                        last = mm(S[u % 2][:, T * ii:T * ii + T], r32(q1[:, (t // 2) % 3, g, t % 2, b, 2 * ii:2 * ii + 2, :]),
                                  r32(k1[:, t % 4, g, b, :, :]), start=True, stop=True)
                    last.then_inc(s["gp_s"], 1)
                k = at(n, 3, 2, 2 * TILES)
                if k is not None:
                    pe.wait_ge(s["g_max"], 2 * k + 2)
                    e = at(n - 1, -8, 2, 4 * PAIRS)
                    if e is not None:
                        pe.wait_ge(s["ga_q" if e % 2 == 0 else "g_q"], e // 2 + 1)
                    if k >= 1:
                        pe.wait_ge(s["ga_mt"], k)
                    for gi in range(4):
                        last = tr(MT[:, P * gi:P * gi + P], mw[:, k % 2, gi, :], ident[:, :])
                    last.then_inc(s["gp_mt"], 1)
                u = at(n, 5, 1, 4 * TILES)
                if u is not None:
                    t, l = divmod(u, 4)
                    b, g = divmod(l, 2)
                    pe.wait_ge(s["ga_mt"], u // 2 + 1)
                    if u < 2:
                        pe.wait_ge(s["f_dn"], 3 + u)
                    if u >= 2:
                        pe.wait_ge(s["ga_ex"], u - 1)
                    for jp in range(2):
                        last = mm(ST[u % 2][:, T * jp:T * jp + T], r32(k1[:, t % 4, g, b, 2 * jp:2 * jp + 2, :]),
                                  r32(q1f(t, g, b)), start=True, stop=True)
                    last.then_inc(s["gp_st"], 1)
                t = at(n, 11, 4, TILES)
                if t is not None:
                    pe.wait_ge(s["ga_o"], t + 1)
                    if t == 0:
                        pe.wait_ge(s["f_x"], TILES)
                    if t >= 1:
                        pe.wait_ge(s["g_x"], t)
                    for i in range(4):
                        last = tr(XB[:, P * i:P * i + P], osb[:, t % 2, P * i:P * i + P], ident[:, :])
                    last.then_inc(s["gp_ot"], 1)
                th = at(n, 20, 4, TILES)
                t = at(n, 12, 4, TILES)
                if t is not None:
                    pe.wait_ge(s["g_on"], t + 1)
                if th is not None:
                    pe.wait_ge(s["h_xn"], th + 1)
                    if th == TILES - 2:
                        pe.wait_ge(s["g_x"], TILES)
                    if th == TILES - 1:
                        pe.wait_ge(s["ha_xT"], th)
                    for k in range(2):
                        last = tr(XB[:, T + P * k:T + P * k + P], xn[:, th % 2, P * k:P * k + P], ident[:, :])
                    last.then_inc(s["hp_xT"], 1)
                if t is not None:
                    for c in range(2):
                        last = tr(XB[:, P * c:P * c + P], on[:, t % 2, P * c:P * c + P], ident[:, :])
                    last.then_inc(s["gp_bt"], 1)
                t = at(n, 13, 4, TILES)
                if t is not None:
                    pe.wait_ge(s["ga_bt"], t + 1)
                    if t >= 2:
                        pe.wait_ge(s["ha_xT"], t - 1)
                    for c in range(2):
                        last = mm(XB[:, T:2 * T], onT[:, t % 2, P * c:P * c + P], wf1[:, c, :], start=(c == 0), stop=(c == 1))
                    last.then_inc(s["gp_out"], 1)
                p = at(n, -13, 8, PAIRS)
                if p is not None:
                    pe.wait_ge(s["g_xn"], 2 * p + 2)
                    if p == 0:
                        pe.wait_ge(s["f_dn"], 2)
                    else:
                        pe.wait_ge(s["ga_v"], p)
                    for k in range(2):
                        for tt in range(2):
                            last = tr(PJ[:, T * k + P * tt:T * k + P * tt + P], xn[:, tt, P * k:P * k + P], ident[:, :])
                    last.then_inc(s["gp_xT"], 1)
                for g in range(2):
                    p = at(n, -11 + g, 8, PAIRS)
                    if p is not None:
                        pe.wait_ge(s["ga_xT"], p + 1)
                        for k in range(2):
                            last = mm(PJ[:, T * g:T * g + T], wq1[:, k, P * g:P * g + P], xT[:, k, T * p:T * p + T], start=(k == 0), stop=(k == 1))
                        last.then_inc(s["gp_q"], 1)
                p = at(n, -8, 8, PAIRS)
                if p is not None:
                    pe.wait_ge(s["ga_hq"], p + 1)
                    pe.wait_ge(s["g_lq"], p + 1)
                    for g in range(2):
                        for k in range(2):
                            last = mm(PJ[:, T * g:T * g + T], wk1[:, k, g, :], cxT[:, k, T * p:T * p + T], start=(k == 0), stop=(k == 1))
                    last.then_inc(s["gp_k"], 1)
                e = at(n, -8, 2, 4 * PAIRS)
                if e is not None:
                    pe.wait_ge(s["g_lq"], e // 4 + 1)
                    if e == 0:
                        pe.wait_ge(s["dve_spread"], 1)
                    k = at(n, 4, 2, 2 * TILES)
                    if k is not None:
                        pe.wait_ge(s["ga_mt"], k + 1)
                    elif e >= 1:
                        pe.wait_ge(s["ga_q" if e % 2 else "g_q"], (e - 1) // 2 + 1)
                    for part in range(2):
                        last = mm(MT[:, :], r32(spread[:, part, e % 4, :]), r32(hs[:, part, :]), start=(part == 0), stop=(part == 1))
                    last.then_inc(s["gp_e"], 1)
                p = at(n, -6, 8, PAIRS)
                if p is not None:
                    pe.wait_ge(s["g_mk"], p + 1)
                    for tt in range(2):
                        for k in range(2):
                            last = mm(PJ[:, 64 * tt:64 * tt + 64], cxT[:, k, P * (2 * p + tt):P * (2 * p + tt) + P], wv1[:, k, :],
                                      start=(k == 0), stop=(k == 1))
                    last.then_inc(s["gp_v"], 1)
                u = at(n, 6, 1, 4 * TILES)
                if u is not None:
                    t, l = divmod(u, 4)
                    b, g = divmod(l, 2)
                    pe.wait_ge(s["ga_ex"], u + 1)
                    pe.wait_ge(s["ga_v"], t // 2 + 1)
                    if l == 0 and t >= 1:
                        pe.wait_ge(s["ga_o"], t)
                    for jp in range(2):
                        pr = 2 * g + jp
                        last = mm(O[32 * pr:32 * pr + 32, T * b:T * b + T], v1[:, t % 6, b, pr, :], e1(u)[:, T * jp:T * jp + T],
                                  start=True, stop=True)
                    last.then_inc(s["gp_pv"], 1)
                f = at(n, 34, 1, FC)
                if f is not None:
                    moe_up(0, f)
                i = at(n, 42, 1, FC)
                if i is not None:
                    moe_down(i // 2, 4 * (i % 2), 4 * (i % 2) + 4)

            def moe_up(half, f):
                m = FC * half + f
                if m == 0:
                    pe.wait_ge(s["g_max"], 4 * TILES)
                if f == 0:
                    pe.wait_ge(s["ha_xT"], 4 * half + 4)
                if m >= 2:
                    pe.wait_ge(s["ha_up"], m - 1)
                for k in range(2):
                    last = mm(S[m % 2][:, :], up[:, k, P * f:P * f + P], xT[:, k, 512 * half:512 * half + 512],
                              start=(k == 0), stop=(k == 1))
                last.then_inc(s["hp_up"], 1)

            def moe_down(t, f0, f1):
                half, m = divmod(t, 4)
                if f0 == 0:
                    if t == 0:
                        pe.wait_ge(s["ga_o"], TILES)
                        pe.wait_ge(s["ga_ex"], 4 * TILES)
                    if t == 1:
                        pe.wait_ge(s["ga_v"], PAIRS)
                    if t >= 2:
                        pe.wait_ge(s["h_y"], 4 * t - 7)
                    for k in range(2):
                        last = mm((O, PJ)[t % 2][:, 0:T + NEXP], xT[:, k, P * t:P * t + P], eg[:, k, :], start=(k == 0), stop=(k == 1))
                    last.then_inc(s["hp_eg"], 1)
                for f in range(f0, f1):
                    if m == 0:
                        pe.wait_ge(s["h_up"], FC * half + f + 1)
                    last = mm(ST[t % 2][:, 0:T], hT[:, f, P * m:P * m + P], down[:, f, :], start=(f == 0), stop=(f == FC - 1))
                if f1 == FC:
                    last.then_inc(s["hp_dn"], 1)

            for n in SLOTS1:
                slot1(n)

            for f in range(FC):
                moe_up(1, f)
            for t in range(4, TILES):
                moe_down(t, 0, FC)

        @block.scalar
        def _(act):
            A = nc.scalar.activation

            def load(dst, src, name):
                act.dma_start(dst, src).then_inc(s[name], 16)
            load(w0[:, :, :], a["w0"], "ld_w0")
            load(b0[:, :], a["b0"], "ld_w0")
            load(kmask[:, :], a["kmask"], "ld_small")
            load(wv0[:, :], a["wv0"], "ld_small")

            def slot_(T_, l):
                t = T_ - 2
                if 0 <= t < TILES:
                    if l == 5:
                        act.wait_ge(s["pe_bt"], t + 1)
                        nc.scalar.copy(onT[:, t % 2, :], XB[:, 0:T]).then_inc(s["act_bt"], 1)
                    if l == 6:
                        act.wait_ge(s["pe_out"], t + 1)
                        if t == 0:
                            act.wait_ge(s["dve_w"], 5)
                        if t >= 1:
                            act.wait_ge(s["dve_y"], t)
                        A(yr[:, 0, :], XB[:, 0:T], ACT.Relu, bias=bcol[:, 3:4]).then_inc(s["act_relu"], 1)
                t = T_ - 3
                if l == 8 and 0 <= t < TILES:
                    act.wait_ge(s["fp_x"], t + 1)
                    nc.scalar.copy(selT(t), MT[:, 0:P])
                    nc.scalar.copy(xsT[:, :, 64 * t:64 * t + 64], MT[:, P:2 * P].rearrange("p (k c) -> p k c", k=2)).then_inc(s["fa_x"], 1)
                t, r = place(T_, l, 24)
                if l % 8 == 0 and live(t, r):
                    k = 2 * t + r // 8
                    act.wait_ge(s["pe_pv"], 8 * k + 8)
                    if k >= 2:
                        act.wait_ge(s["pe_ot"], k - 1)
                    nc.scalar.copy(osb[:, k % 2, :], O[:, :]).then_inc(s["act_o"], 1)
                t = T_ + 1
                if 0 <= t < TILES:
                    if l - 1 in PROJ:
                        n = PROJ[l - 1]
                        m = 4 * t + n
                        act.wait_ge(s["pe_proj"], m + 1)
                        if m == 0:
                            act.wait_ge(s["dve_w"], 4)
                        if m >= 2:
                            act.wait_ge(s["dve_mix"], m - 1)
                        A(r32(hs[:, m % 2, :]), proj_bank(t, n)[:, :], ACT.Identity, bias=sb0[:, n:n + 1], scale=cols[:, n // 2:n // 2 + 1])\
                            .then_inc(s["act_hs"], 1)
                for t, j in ((T_ + 1, KA.get(l)), (T_, KA.get(l + UNITS))):
                    if j is not None and 0 <= t < TILES:
                        if j == 0:
                            act.wait_ge(s["dve_mix"], 4 * t + 2)
                            if t == 0:
                                act.wait_ge(s["ld_small"], 64)
                            if t >= 2:
                                act.wait_ge(s["pe_st"], UNITS * (t - 1))
                        last = A(r32(kb[:, t % 2, 1, j, 1, :]), kp[:, 1, 1, :], ACT.Copy, scale=kmask[:, j:j + 1])
                        if j == 3:
                            last.then_inc(s["act_kb"], 1)
                if l == 0 and 0 <= T_ < TILES:
                    t = T_
                    act.wait_ge(s["pe_v"], t + 1)
                    if t >= 2:
                        act.wait_ge(s["pe_pv"], UNITS * (t - 1))
                    nc.scalar.copy(v0[:, t % 2, :, :, :, 0:8].rearrange("p c b h d -> p (c b) h d"),
                                   value_bank(t)[:, 0:T].rearrange("p (c h d) -> p c h d", c=4, h=8)).then_inc(s["act_v"], 1)
                t = T_ + 2
                if l == 14 and 0 <= t < TILES:
                    act.wait_ge(s["dve_xn"], t + 1)
                    if t >= 1:
                        act.wait_ge(s["pe_proj"], 4 * t)
                    A(r32(xs[0:64, 0, :]), xn[0:64, t % 2, :], ACT.Copy)
                    A(r32(xs[64:128, 1, :]), xn[64:128, t % 2, :], ACT.Copy).then_inc(s["act_xh"], 1)
                t, r = place(T_, l, ST_LAG)
                if live(t, r):
                    n = UNITS * t + r
                    b, g, c, w = parts(r)
                    act.wait_ge(s["pe_st"], n + 1)
                    if n >= 8:
                        act.wait_ge(s["pe_pv"], (n // 2 - 4) * 2 + 2)
                    A(ex[:, (n // 2) % 4, 2 * w:2 * w + 2, :], ST[n % 2][:, 0:2 * WIN].rearrange("p (h k) -> p h k", h=2),
                      ACT.Exp, scale=SCALE).then_inc(s["act_exp"], 1)
                t, r = place(T_, l, 9)
                if l % 8 == 1 and live(t, r):
                    k = 2 * t + r // 8
                    act.wait_ge(s["pe_mt"], k + 1)
                    A(r32(qp[96:128, t % 2, :, r // 8, :].rearrange("p g (c q) -> p c g q", c=2)),
                      MT[96:128, :].rearrange("p (c g q) -> p c g q", c=2, g=2), ACT.Copy, scale=-1.0)\
                        .then_inc(s["act_mt"], 1)
                kind, n = tail(T_, l)
                if kind == "up":
                    gelu(0, n)

            def gelu(half, f):
                act.wait_ge(s["fp_up"], FC * half + f + 1)
                A(hT[:, f, T * half:T * half + T], up_bank(f), ACT.Gelu_apprx_tanh, bias=b1[:, f:f + 1]).then_inc(s["fa_up"], 1)

            act.wait_ge(s["pool_zero"], 1)
            A(rc[:, 0, 0:1], v0[:, 0, 0, 0, 0, 0:1], ACT.Exp)
            act.wait_ge(s["pool_zero"], 2)
            for T_, l in SLOTS_ALL:
                slot_(T_, l)

            def slot1(n):
                f = at(n, -20, 1, FC)
                if f is not None:
                    if f == 0:
                        act.wait_ge(s["fp_x"], TILES)
                    gelu(1, f)
                k = at(n, 4, 2, 2 * TILES)
                if k is not None:
                    t, b = divmod(k, 2)
                    act.wait_ge(s["gp_mt"], k + 1)
                    A(r32(q1[96:128, (t // 2) % 3, :, t % 2, b, :, :]), MT[96:128, :].rearrange("p (g i q) -> p g i q", g=2, i=4),
                      ACT.Copy, scale=-1.0).then_inc(s["ga_mt"], 1)
                t = at(n, 10, 4, TILES)
                if t is not None:
                    act.wait_ge(s["gp_pv"], 4 * t + 4)
                    if t >= 2:
                        act.wait_ge(s["gp_ot"], t - 1)
                    nc.scalar.copy(osb[:, t % 2, :].rearrange("p (i b q) -> p b i q", b=2, i=4),
                                   O[:, :].rearrange("p (b i q) -> p b i q", b=2, i=4)).then_inc(s["ga_o"], 1)
                t = at(n, 13, 4, TILES)
                if t is not None:
                    act.wait_ge(s["gp_bt"], t + 1)
                    nc.scalar.copy(onT[:, t % 2, :], XB[:, 0:T]).then_inc(s["ga_bt"], 1)
                t = at(n, 21, 4, TILES)
                if t is not None:
                    act.wait_ge(s["hp_xT"], t + 1)
                    nc.scalar.copy(xT[:, :, P * t:P * t + P], XB[:, T:2 * T].rearrange("p (k c) -> p k c", k=2)).then_inc(s["ha_xT"], 1)
                p = at(n, -12, 8, PAIRS)
                if p is not None:
                    act.wait_ge(s["gp_xT"], p + 1)
                    act.wait_ge(*((s["fp_up"], 2 * FC) if p < 2 else (s["fp_sc"], TILES)))
                    nc.scalar.copy(xT[:, :, T * p:T * p + T], PJ[:, :].rearrange("p (k c) -> p k c", k=2)).then_inc(s["ga_xT"], 1)
                p = at(n, -9, 8, PAIRS)
                if p is not None:
                    act.wait_ge(s["gp_q"], 2 * p + 2)
                    if p >= 1:
                        act.wait_ge(s["gp_e"], 4 * p)
                    A(r32(hs[:, 0, :]), PJ[:, :], ACT.Copy).then_inc(s["ga_hq"], 1)
                p = at(n, -7, 8, PAIRS)
                if p is not None:
                    act.wait_ge(s["gp_k"], p + 1)
                    if p >= 1:
                        act.wait_ge(s["g_mk"], p)
                    A(r32(k1h), PJ[:, :], ACT.Identity, bias=0.0, scale=cols[:, 0:1]).then_inc(s["ga_hk"], 1)
                for i in (0, 2):
                    p = at(n, -7 + 2 * i, 8, PAIRS)
                    if p is not None:
                        act.wait_ge(s["gp_e"], 4 * p + i + 1)
                        if p >= 3:
                            act.wait_ge(s["gp_st"], 8 * (p - 2))
                        A(stacked(p, i), MT[:, :].rearrange("p (g t q) -> p g t q", g=2, t=4), ACT.Copy).then_inc(s["ga_q"], 1)
                p = at(n, -5, 8, PAIRS)
                if p is not None:
                    act.wait_ge(s["gp_v"], p + 1)
                    if p >= 3:
                        act.wait_ge(s["gp_pv"], 8 * (p - 2))
                    for b in range(2):
                        for j2 in range(2):
                            last = nc.scalar.copy(v1[64 * j2:64 * j2 + 64, (2 * p) % 6:(2 * p) % 6 + 2, b, :, 16 * j2:16 * j2 + 8],
                                                  PJ[64 * b:64 * b + 64, 0:128].rearrange("p (t r j d) -> p t r j d", t=2, r=4, j=2)[:, :, :, j2, :])
                    last.then_inc(s["ga_v"], 1)
                f = at(n, 35, 1, FC)
                if f is not None:
                    moe_relu(f)
                u = at(n, 5, 1, 4 * TILES)
                if u is not None:
                    act.wait_ge(s["gp_st"], u + 1)
                    if u >= 4:
                        act.wait_ge(s["gp_pv"], u - 3)
                    A(e1(u), ST[u % 2][:, :], ACT.Exp, scale=SCALE).then_inc(s["ga_ex"], 1)

            def moe_relu(m):
                act.wait_ge(s["hp_up"], m + 1)
                if m >= 2:
                    act.wait_ge(s["h_up"], m - 1)
                A(relu(m), S[m % 2][:, :], ACT.Relu).then_inc(s["ha_up"], 1)

            act.wait_ge(s["pool_zero"], 5)
            for n in SLOTS1:
                slot1(n)

            for m in range(FC, 2 * FC):
                moe_relu(m)

        @block.gpsimd
        def _(pool):
            G = nc.gpsimd
            G.memset(v0[:, :, :, :, :, :], 0.0).then_inc(s["pool_zero"], 1)
            pool.wait_ge(s["pool_zero"], 1)
            G.memset(v0[:, :, :, :, :, 8:9], 1.0).then_inc(s["pool_zero"], 1)
            G.memset(mw[:, :, :, :], 0.0).then_inc(s["pool_mw"], 1)
            pool.wait_ge(s["ld_first"], 32)

            variances = []

            def inv_std(t, ready, k, done):
                pool.wait_ge(s[ready], k)
                G.tensor_scalar(rstd[:, t:t + 1], mv[:, t, 1:2], EPS, None, ALU.add).then_inc(s["pool_var"], 1)
                variances.append(t)
                pool.wait_ge(s["pool_var"], len(variances))
                G.tensor_tensor(rstd[:, t:t + 1], rstd[:, t:t + 1], cols[:, 2:3], ALU.pow).then_inc(s[done], 1)

            def keys(t, b, g):
                pool.wait_ge(s["dve_mix"], 4 * t + g + 1)
                if t == 0 and (b, g) == (0, 0):
                    pool.wait_ge(s["ld_small"], 64)
                if t >= 2:
                    pool.wait_ge(s["pe_st"], UNITS * (t - 2) + 8 * b + 4 * g + 4)
                G.tensor_tensor(r32(kb[:, t % 2, g, :, b, :]), kp[:, g, b:b + 1, :].to_broadcast([P, 4, T]),
                                kmask[:, :, None].to_broadcast([P, 4, T]), ALU.mult).then_inc(s["pool_kb"], 1)

            def slot_(T_, l):
                t = T_ + 2
                if l == 3 and 0 <= t < TILES:
                    inv_std(t, "dve_ln", 2 * t + 2, "pool_rstd")
                t = T_ - 2
                if l == 13 and 0 <= t < TILES:
                    inv_std(t, "f_ln", 2 * t + 2, "f_rstd")
                if T_ >= 0:
                    t, r = place(T_, l, ST_LAG + 1)
                    if r % 2 == 0 and live(t, r):
                        n = UNITS * t + r
                        b, g, c, w = parts(r)
                        e = ex[:, (n // 2) % 4, :, :]
                        pool.wait_ge(s["act_exp"], n + 2)
                        if c == 0:
                            G.affine_select(out=e[:, :, 0:64], in_=e[:, :, 0:64], compare_op=ALU.is_ge, fill=0.0, base=BAND,
                                            pattern=[[0, 4], [1, 64]], channel_multiplier=-1)
                            G.affine_select(out=e[:, :, 64:WIN], in_=e[:, :, 64:WIN], compare_op=ALU.is_ge, fill=0.0, base=0,
                                            pattern=[[0, 4], [-1, 128]], channel_multiplier=1).then_inc(s["pool_sel"], 1)
                        else:
                            G.affine_select(out=e[:, :, 0:128], in_=e[:, :, 0:128], compare_op=ALU.is_ge, fill=0.0, base=0,
                                            pattern=[[0, 4], [1, 128]], channel_multiplier=-1)
                            G.affine_select(out=e[:, :, 128:WIN], in_=e[:, :, 128:WIN], compare_op=ALU.is_ge, fill=0.0, base=0,
                                            pattern=[[0, 4], [-1, 64]], channel_multiplier=1).then_inc(s["pool_sel"], 1)
                t = T_ + 1
                if l in KB and 0 <= t < TILES:
                    keys(t, *KB[l])
            for T_, l in SLOTS_ALL:
                slot_(T_, l)

            G.memset(v1[:, :, :, :, :], 0.0).then_inc(s["pool_zero"], 1)
            pool.wait_ge(s["pool_zero"], 3)
            for j2 in range(2):
                G.memset(v1[64 * j2:64 * j2 + 64, :, :, :, 16 * j2 + 8:16 * j2 + 9], 1.0).then_inc(s["pool_zero"], 1)
                pool.wait_ge(s["pool_zero"], 4 + j2)
            def slot1(n):
                for tt in range(2):
                    p = at(n, -17 + 2 * tt, 8, PAIRS)
                    if p is not None:
                        inv_std(2 * p + tt, "g_ln", 2 * (2 * p + tt) + 2, "g_rstd")
                t = at(n, 16, 4, TILES)
                if t is not None:
                    inv_std(t, "h_ln", 2 * t + 2, "h_rstd")
                for tt in range(2):
                    p = at(n, -6 + 2 * tt, 8, PAIRS)
                    if p is not None:
                        t = 2 * p + tt
                        pool.wait_ge(s["g_mk"], p + 1)
                        if t == 0:
                            pool.wait_ge(s["pe_st"], ALL_UNITS)
                        if t >= 4:
                            pool.wait_ge(s["gp_st"], 4 * (t - 3))
                        for g in range(2):
                            last = G.tensor_tensor(r32(k1[:, t % 4, g, :, :, :]),
                                                   k1p.rearrange("p (g t b k) -> p g t b k", g=2, t=2, b=2)[:, g, tt, :, None, :].to_broadcast([P, 2, 4, 64]),
                                                   kmask[:, None, :, None].to_broadcast([P, 2, 4, 64]), ALU.mult)
                        last.then_inc(s["gpool_k"], 1)
            for n in SLOTS1:
                slot1(n)

            for t in range(TILES):
                inv_std(t, "h_ln2", 2 * t + 2, "h_rstd2")

        @block.vector
        def _(dve):
            V = nc.vector

            def stats(t, src, name, k):
                V.bn_stats(st6[:, t % 2, :], src).then_inc(s[name], 1)
                dve.wait_ge(s[name], k + 1)
                V.bn_aggr(mv[:, t, :], st6[:, t % 2, :]).then_inc(s[name], 1)

            V.memset(w0l[:, :, :, :], 0.0).then_inc(s["dve_zero"], 1)
            dve.wait_ge(s["ld_first"], 32)
            stats(0, x[:, 0, :], "dve_ln", 0)
            dve.wait_ge(s["ld_w0"], 32)
            V.tensor_copy(r32(w0h[:, :, :]), w0[:, :, :]).then_inc(s["dve_w"], 1)
            for n in range(4):
                last = V.tensor_tensor(sb0[:, n:n + 1], b0[:, n:n + 1], cols[:, n // 2:n // 2 + 1], ALU.mult)
            last.then_inc(s["dve_w"], 1)
            dve.wait_ge(s["dve_w"], 2)
            dve.wait_ge(s["dve_zero"], 1)
            for b in range(2):
                hp = slice(64 * b, 64 * b + 64)
                V.tensor_tensor(r32(w0l[hp, b, :, :]), w0[hp, :, :], w0h[hp, :, :], ALU.subtract).then_inc(s["dve_w"], 1)

            dve.wait_ge(s["ld_small"], 64)
            V.tensor_copy(band[:, :, :], exf[:, 0:2 * WIN].rearrange("p (c k) -> p c k", c=2)).then_inc(s["dve_band"], 1)
            V.tensor_copy(identb[:, :], ident[:, :]).then_inc(s["dve_band"], 1)

            def slot_(T_, l):
                t, r = T_, l
                if live(t, r):
                    n = UNITS * t + r
                    b, g, c, w = parts(r)
                    dve.wait_ge(s["pe_s"], n + 1)
                    if n == 0:
                        dve.wait_ge(s["pool_mw"], 1)
                    if r % 8 == 0 and n >= 16:
                        dve.wait_ge(s["pe_mt"], 2 * t + b - 1)
                    V.tensor_reduce(mw[:, b, 2 * c + g, 96 + 2 * w:98 + 2 * w],
                                    S[n % 2][:, 0:2 * WIN].rearrange("p (h k) -> p h k", h=2), AX, ALU.max).then_inc(s["dve_max"], 1)
                t, r = place(T_, l, 27)
                if l % 8 == 3 and live(t, r):
                    k = 2 * t + r // 8
                    b = k % 2
                    dve.wait_ge(s["pe_ot"], k + 1)
                    ot = XB[:, :].rearrange("p (c g f) -> p c g f", c=2, f=32)
                    V.reciprocal(rc[:, b, 0:16].rearrange("p (c g) -> p c g", c=2), ot[:, :, :, 8]).then_inc(s["dve_rc"], 1)
                    dve.wait_ge(s["dve_rc"], k + 1)
                    if b == 0 and t >= 1:
                        dve.wait_ge(s["pe_bt"], t)
                    V.tensor_tensor(on[:, :, 64 * b:64 * b + 64].rearrange("p c (g d) -> p c g d", g=8), ot[:, :, :, 0:8],
                                    rc[:, b, 0:16].rearrange("p (c g) -> p c g", c=2)[:, :, :, None].to_broadcast([P, 2, 8, 8]),
                                    ALU.mult).then_inc(s["dve_on"], 1)
                t = T_ - 2
                if 0 <= t < TILES:
                    if l == 6:
                        dve.wait_ge(s["act_relu"], t + 1)
                        if t == 0:
                            dve.wait_ge(s["ld_rest"], 64)
                        if t >= 1:
                            dve.wait_ge(s["pe_wct"], t)
                        V.tensor_tensor(yr[:, 1, :], yr[:, 0, :], cx[:, t, :], ALU.mult).then_inc(s["dve_y"], 1)
                    if l == 8:
                        dve.wait_ge(s["pe_wct"], t + 1)
                        V.scalar_tensor_tensor(out=x[:, t, :], in0=XB[:, 0:T], scalar=bcol[:, 2:3], in1=x[:, t, :],
                                               op0=ALU.add, op1=ALU.add).then_inc(s["dve_x"], 1)
                    if l == 12:
                        dve.wait_ge(s["dve_x"], t + 1)
                        stats(t, x[:, t, :], "f_ln", 2 * t)
                    if l == 15:
                        dve.wait_ge(s["f_rstd"], t + 1)
                        if t == 0:
                            dve.wait_ge(s["ld_sel"], 96)
                            V.tensor_copy(r32(spread[:, :, :, :].rearrange("p a b c -> p (a b c)")), hT[:, 0:2, :].rearrange("p a b -> p (a b)"))\
                                .then_inc(s["dve_spread"], 1)
                            dve.wait_ge(s["dve_spread"], 1)
                        V.tensor_scalar(x_norm(t), x[:, t, :], mv[:, t, 0:1], rstd[:, t:t + 1], ALU.subtract, ALU.mult).then_inc(s["f_xn"], 1)
                t = T_ - 3
                if 0 <= t < TILES:
                    if l == 0:
                        dve.wait_ge(s["f_xn"], 2 * t + 1)
                        V.tensor_tensor_reduce(out=cmp[:, 0:2, :].rearrange("p a b -> p (a b)"), in0=x_norm(t), in1=vecs[:, 0, :], scale=1.0,
                                               scalar=0.0, op0=ALU.mult, op1=ALU.add, accum_out=sc[:, t:t + 1]).then_inc(s["f_xn"], 1)
                        dve.wait_ge(s["f_xn"], 2 * t + 2)
                        V.tensor_scalar(sc[:, t:t + 1], sc[:, t:t + 1], br[:, 0:1], None, ALU.add).then_inc(s["f_sc"], 1)
                if l == 5 and 0 <= t < TILES:
                    dve.wait_ge(s["fp_sT"], t + 1)
                    V.scalar_tensor_tensor(out=cmp[:, 0, :], in0=MT[:, 0:P], scalar=sc[:, t:t + 1], in1=blk[:, :], op0=ALU.is_gt, op1=ALU.mult,
                                           accum_out=rk[:, 0:1])
                    V.scalar_tensor_tensor(out=cmp[:, 1, :], in0=MT[:, 0:P], scalar=sc[:, t:t + 1], in1=tri[:, :], op0=ALU.is_equal, op1=ALU.mult,
                                           accum_out=rk[:, 1:2]).then_inc(s["f_cmp"], 1)
                    dve.wait_ge(s["f_cmp"], t + 1)
                    if t >= 2:
                        dve.wait_ge(s["fp_x"], t - 1)
                    V.tensor_scalar(sel[:, t % 2, :], slot[:, P * (t % 2):P * (t % 2) + P], rk[:, 0:1], rk[:, 1:2], ALU.subtract, ALU.is_equal)\
                        .then_inc(s["f_sel"], 1)
                if T_ == 1 and l == 2:
                    dve.wait_ge(s["pe_bias"], 1)
                    V.tensor_tensor(bcol[:, 3:4], XB[:, 0:1], bcol[:, 1:2], ALU.add).then_inc(s["dve_w"], 1)
                t = T_ + 2
                if 0 <= t < TILES:
                    if l == 2 and t >= 1:
                        if t == 1:
                            dve.wait_ge(s["ld_x1"], 16)
                        if t == 2:
                            dve.wait_ge(s["ld_x"], 16)
                        stats(t, x[:, t, :], "dve_ln", 2 * t)
                    if l == 9:
                        dve.wait_ge(s["pool_rstd"], t + 1)
                        if t >= 2:
                            dve.wait_ge(s["pe_v"], t - 1)
                        V.tensor_scalar(xn[:, t % 2, :], x[:, t, :], mv[:, t, 0:1], rstd[:, t:t + 1], ALU.subtract, ALU.mult)\
                            .then_inc(s["dve_xn"], 1)
                t = T_ + 1
                if l == 1 and 0 <= t < TILES:
                    dve.wait_ge(s["act_xh"], t + 1)
                    V.tensor_tensor(r32(xs[64:128, 0, :]), xn[0:64, t % 2, :], xs[0:64, 0, :], ALU.subtract)
                    V.tensor_tensor(r32(xs[0:64, 1, :]), xn[64:128, t % 2, :], xs[64:128, 1, :], ALU.subtract)\
                        .then_inc(s["dve_xl"], 1)
                t = T_ + 1
                if l - 1 in PROJ and 0 <= t < TILES:
                    n = PROJ[l - 1]
                    m, g = 4 * t + n, n % 2
                    dve.wait_ge(s["act_hs"], m + 1)
                    if n < 2 and t >= 1:
                        dve.wait_ge(s["pool_kb"], 3 * t)
                        if g == 1:
                            dve.wait_ge(s["act_kb"], t)
                    if n >= 2 and t >= 2:
                        dve.wait_ge(s["pe_st"], UNITS * (t - 2) + 8 + 4 * g + 4)
                    dst = (qp[:, t % 2, g, :, :] if n >= 2 else kp[:, g, :, :]).rearrange("p b q -> p (b q)")
                    V.scalar_tensor_tensor(out=r32(dst), in0=proj_bank(t, n)[:, :], scalar=b0[:, n:n + 1], in1=hs[:, m % 2, :],
                                           op0=ALU.add, op1=ALU.subtract).then_inc(s["dve_mix"], 1)
                kind, n = tail(T_, l)
                if kind == "scatter" and n % 2 == 0:
                    ffn_out(n // 2)
                kind, n = tail(*place(T_, l, 1))
                if kind == "scatter":
                    ffn_add(n)

            def ffn_out(c):
                dve.wait_ge(s["fp_dn"], c + 1)
                V.tensor_tensor(osel[:, c, :], down_bank(c), vecs[:, 1, :], ALU.add).then_inc(s["f_dn"], 1)

            def ffn_add(t):
                dve.wait_ge(s["fp_sc"], t + 1)
                V.tensor_tensor(x[:, t, :], scatter_bank(t), x[:, t, :], ALU.add).then_inc(s["f_x"], 1)

            for T_, l in SLOTS_ALL:
                slot_(T_, l)

            def slot1(n):
                c = at(n, -8, 4, 2)
                if c is not None:
                    ffn_out(2 + c)
                t = at(n, -3, 1, 4)
                if t is not None:
                    ffn_add(4 + t)
                p = at(n, -9, 8, PAIRS)
                if p is not None:
                    dve.wait_ge(s["ga_hq"], p + 1)
                    V.tensor_tensor(r32(hs[:, 1, :]), PJ[:, :], hs[:, 0, :], ALU.subtract).then_inc(s["g_lq"], 1)
                p = at(n, -7, 8, PAIRS)
                if p is not None:
                    dve.wait_ge(s["ga_hk"], p + 1)
                    if p >= 1:
                        dve.wait_ge(s["gpool_k"], 2 * p)
                    V.scalar_tensor_tensor(out=r32(k1p), in0=PJ[:, :], scalar=cols[:, 3:4], in1=k1h,
                                           op0=ALU.add, op1=ALU.subtract).then_inc(s["g_mk"], 1)
                for i in (1, 3):
                    p = at(n, -7 + 2 * i, 8, PAIRS)
                    if p is not None:
                        dve.wait_ge(s["gp_e"], 4 * p + i + 1)
                        if p >= 3:
                            dve.wait_ge(s["gp_st"], 8 * (p - 2))
                        V.tensor_copy(stacked(p, i), MT[:, :].rearrange("p (g t q) -> p g t q", g=2, t=4)).then_inc(s["g_q"], 1)
                t = at(n, 14, 4, TILES)
                if t is not None:
                    dve.wait_ge(s["gp_out"], t + 1)
                    V.tensor_tensor(yr[:, t % 2, :], XB[:, T:2 * T], x[:, t, :], ALU.add).then_inc(s["g_y"], 1)
                    dve.wait_ge(s["g_y"], t + 1)
                    V.tensor_tensor(x[:, t, :], yr[:, t % 2, :], vecs[:, 2, :], ALU.add).then_inc(s["g_x"], 1)
                u = at(n, 0, 1, 4 * TILES)
                if u is not None:
                    k, g = divmod(u, 2)
                    dve.wait_ge(s["gp_s"], u + 1)
                    if k >= 2 and g == 0:
                        dve.wait_ge(s["gp_mt"], k - 1)
                    V.tensor_reduce(mw[:, k % 2, 2 * g:2 * g + 2, 96:100], S[u % 2][:, :].rearrange("p (i j k) -> p i j k", i=2, j=4),
                                    AX, ALU.max).then_inc(s["g_max"], 1)
                t = at(n, 11, 4, TILES)
                if t is not None:
                    dve.wait_ge(s["gp_ot"], t + 1)
                    ot = XB[:, :].rearrange("p (i g f) -> p i g f", i=4, f=16)
                    rv = rc[:, t % 2, :].rearrange("p (i g) -> p i g", i=4)
                    V.reciprocal(rv, ot[:, :, :, 8]).then_inc(s["g_rc"], 1)
                    dve.wait_ge(s["g_rc"], t + 1)
                    if t >= 2:
                        dve.wait_ge(s["gp_bt"], t - 1)
                    V.tensor_tensor(on[:, t % 2, :].rearrange("p (g i d) -> p i g d", g=8, i=4), ot[:, :, :, 0:8],
                                    rv[:, :, :, None].to_broadcast([P, 4, 8, 8]), ALU.mult).then_inc(s["g_on"], 1)
                for tt in range(2):
                    p = at(n, -18 + 2 * tt, 8, PAIRS)
                    if p is not None:
                        t = 2 * p + tt
                        dve.wait_ge(s["f_x"], t + 1)
                        stats(t, x[:, t, :], "g_ln", 2 * t)
                    p = at(n, -17 + 2 * tt, 8, PAIRS)
                    if p is not None:
                        t = 2 * p + tt
                        dve.wait_ge(s["g_rstd"], t + 1)
                        if p >= 1:
                            dve.wait_ge(s["gp_xT"], p)
                        normalise(xn[:, tt, :], t, "g_xn")
                t = at(n, 15, 4, TILES)
                if t is not None:
                    dve.wait_ge(s["g_x"], t + 1)
                    stats(t, x[:, t, :], "h_ln", 2 * t)
                t = at(n, 16, 4, TILES)
                if t is not None:
                    dve.wait_ge(s["h_rstd"], t + 1)
                    if t >= 2:
                        dve.wait_ge(s["hp_xT"], t - 1)
                    elif t == 0:
                        dve.wait_ge(s["gp_xT"], PAIRS)
                    normalise(xn[:, t % 2, :], t, "h_xn")
                f = at(n, 35, 1, FC)
                if f is not None:
                    moe_square(f)
                t = at(n, 44, 2, 4)
                if t is not None:
                    moe_out(t)

            def normalise(dst, t, name):
                V.tensor_scalar(dst, x[:, t, :], mv[:, t, 0:1], rstd[:, t:t + 1], ALU.subtract, ALU.mult).then_inc(s[name], 1)

            def moe_square(m):
                dve.wait_ge(s["ha_up"], m + 1)
                if m == FC:
                    dve.wait_ge(s["hp_dn"], 4)
                V.tensor_tensor(hT[:, m % FC, :], relu(m), relu(m), ALU.mult).then_inc(s["h_up"], 1)

            def moe_out(t):
                dve.wait_ge(s["hp_eg"], t + 1)
                gp = (O, PJ)[t % 2]
                V.max(out=tk[:, t % 2, :], in_=gp[:, T:T + NEXP]).then_inc(s["h_tk"], 1)
                dve.wait_ge(s["h_tk"], 2 * t + 1)
                V.tensor_tensor(rk[:, t:t + 1], tk[:, t % 2, 0:1], tk[:, t % 2, 1:2], ALU.add).then_inc(s["h_tk"], 1)
                dve.wait_ge(s["h_tk"], 2 * t + 2)
                dve.wait_ge(s["hp_dn"], t + 1)
                V.tensor_scalar(yr[:, 0, :], gp[:, 0:T], rk[:, t:t + 1], None, ALU.mult).then_inc(s["h_moe"], 1)
                dve.wait_ge(s["h_moe"], t + 1)
                V.tensor_tensor(yr[:, 1, :], ST[t % 2][:, 0:T], yr[:, 0, :], ALU.add).then_inc(s["h_y"], 1)
                dve.wait_ge(s["h_y"], 4 * t + 1)
                stats(t, yr[:, 1, :], "h_ln2", 2 * t)
                dve.wait_ge(s["h_rstd2"], t + 1)
                V.tensor_scalar(yr[:, 0, :], yr[:, 1, :], mv[:, t, 0:1], rstd[:, t:t + 1], ALU.subtract, ALU.mult).then_inc(s["h_y"], 1)
                dve.wait_ge(s["h_y"], 4 * t + 2)
                V.tensor_tensor(yr[:, 1, :], yr[:, 0, :], vecs[:, 3, :], ALU.mult).then_inc(s["h_y"], 1)
                dve.wait_ge(s["h_y"], 4 * t + 3)
                V.tensor_tensor(yr[:, 0, :], yr[:, 1, :], vecs[:, 4, :], ALU.add).then_inc(s["h_y"], 1)
                dve.wait_ge(s["h_y"], 4 * t + 4)
                V.tensor_tensor(x[:, t, :], yr[:, 0, :], x[:, t, :], ALU.add).then_inc(s["h_out"], 1)

            for n in SLOTS1:
                slot1(n)

            for m in range(FC, 2 * FC):
                moe_square(m)
            for t in range(4, TILES):
                moe_out(t)


def constants():
    i = np.arange(P)
    ident = np.eye(P, dtype=np.float32)
    c = {"ident": ident}
    band = np.zeros((P, 2, WIN), np.float32)
    for ch in range(2):
        q = P * ch + i[:, None]
        k = BAND * ch + np.arange(WIN)[None, :]
        band[:, ch] = np.where(np.abs(q - k) <= BAND, 0.0, NEG)
    c["band"] = band.reshape(P, 2 * WIN)
    kmask = np.zeros((P, 4), np.float32)
    for r in range(3):
        for j in range(4):
            kmask[32 * r + 8 * j:32 * r + 8 * j + 8, j] = 1
    for j in range(4):
        kmask[96 + j, j] = 1
    c["kmask"] = kmask
    cols = np.zeros((P, 4), np.float32)
    cols[32:64, 0] = 1
    cols[64:96, 1] = 1
    cols[:, 2] = -0.5
    cols[96:128, 3] = 1
    c["cols"] = cols
    same = (i[:, None] // 64) == (i[None, :] // 64)
    c["blk"] = same.astype(np.float32)
    c["tri"] = (same & (i[None, :] < i[:, None])).astype(np.float32)
    slot = np.full((P, 2, 2, 2, KEEP), -1, np.float32)
    for par in range(2):
        for b in range(2):
            slot[64 * b:64 * b + 64, par, par, b] = np.arange(KEEP)
    c["slot"] = slot.reshape(P, 2 * P)
    spread = np.zeros((4, 4, 8, 2, 4, 4, 4, 8), np.float32)
    for j in range(4):
        for i in range(4):
            for d in range(8):
                for r in range(3):
                    spread[j, i, d, r // 2, i, r, j, d] = 1
    c["spread"] = spread.reshape(P, -1)
    return c


def kernel(**inputs):
    import concourse.bacc as bacc
    from concourse.bass_utils import run_bass_kernel_spmd

    f = {k: np.asarray(v) for k, v in inputs.items()}
    arr = constants()
    arr["x"] = f["x"].reshape(N * E, T)
    arr["cx"] = f["ctx_2048"].reshape(N * E, T)
    arr["cxT"] = np.ascontiguousarray(arr["cx"].T)
    w_in, b_in = f["L0_xattn_w_in"], f["L0_xattn_b_in"]
    w0 = np.zeros((P, 4, 4, 32), np.float32)
    b0 = np.zeros((4, 32, 4), np.float32)
    for n, (typ, g) in enumerate(((1, 0), (1, 1), (0, 0), (0, 1))):
        rows = slice(64 * typ + 32 * g, 64 * typ + 32 * g + 32)
        for r in range(3):
            w0[0:64, n, r] = w_in[rows].T
            w0[64:128, n, r] = w_in[rows].T
            b0[r, :, n] = b_in[rows]
        if typ:
            b0[3, :, n] = 1
    arr["w0"] = w0.reshape(P, 4, P)
    arr["b0"] = b0.reshape(P, 4)

    def twice(w):
        out = np.zeros((P, P), np.float32)
        out[0:64, 0:64] = w
        out[64:128, 64:128] = w
        return out
    arr["wv0"] = twice(w_in[128:192].T)
    arr["wo0"] = twice(f["L0_xattn_w_out"].T)
    arr["wc0"] = twice(f["L0_xattn_w_ct"])
    bcol = np.zeros((P, 4), np.float32)
    for k, v in enumerate((b_in[128:192], f["L0_xattn_b_out"], f["L0_xattn_b_ct"])):
        bcol[0:64, k] = v
        bcol[64:128, k] = v
    arr["bcol"] = bcol
    arr["vecs"] = np.stack([f["L0_ffn_w_r"], f["L0_ffn_b2"], f["L1_xattn_bfc"], f["L1_ffn_ln_gamma"], f["L1_ffn_ln_beta"]])
    arr["br"] = f["L0_ffn_b_r"].reshape(1, 1)
    arr["b1"] = np.ascontiguousarray(f["L0_ffn_b1"].reshape(FC, P).T)
    arr["w1"], arr["w2"] = f["L0_ffn_w1"], f["L0_ffn_w2"]
    arr["wq1"] = np.ascontiguousarray(f["L1_xattn_Wq"].T)
    wk = f["L1_xattn_Wk"].reshape(2, 4, 8, 2, P)
    wk1 = np.zeros((P, 2, 2, 4, 4, 8), np.float32)
    for r in range(3):
        wk1[:, :, :, r] = wk.transpose(4, 3, 0, 1, 2)
    arr["wk1"] = wk1.reshape(P, -1)
    arr["wv1"] = np.ascontiguousarray(f["L1_xattn_Wv"].T)
    arr["wf1"] = np.ascontiguousarray(f["L1_xattn_Wfc"].T)
    arr["up"], arr["down"] = f["L1_ffn_up_w"], f["L1_ffn_down_w"]
    arr["ew"], arr["gw"] = f["L1_ffn_expert_weight"], f["L1_ffn_gate_w"]

    nc = bacc.Bacc("TRN2", target_bir_lowering=False, num_devices=1)
    aps, feed = {}, {}
    for name, v in arr.items():
        v = np.ascontiguousarray(v)
        feed[f"in_{name}"] = v
        aps[name] = nc.dram_tensor(f"in_{name}", v.shape, mybir.dt.from_np(v.dtype), kind="ExternalInput").ap()
    aps["out"] = nc.dram_tensor("out_0", (N * E, T), F32, kind="ExternalOutput").ap()
    build(nc, aps)
    res = run_bass_kernel_spmd(nc, [feed], core_ids=[0])
    return res.results[0]["out_0"].reshape(N, E, T)
```

```python
from contextlib import ExitStack

import numpy as np
import concourse.bass as bass
import concourse.mybir as mybir
from concourse.alu_op_type import AluOpType as ALU

F32 = mybir.dt.float32
F32R = mybir.dt.float32r
BF16 = mybir.dt.bfloat16
ACT = mybir.ActivationFunctionType
AX = mybir.AxisListType.X

P = 128
N, E, T = 16, 64, 256
TILES = N * E // P
H0, D0 = 8, 8
BAND = 64
WIN = 192
DF = 1024
FC = DF // P
KEEP = 32
SLOTS = TILES * 2 * KEEP
NEXP = 8
EPS = 1e-5
NEG = -1e30
SCALE = 1.0 / float(np.sqrt(8.0))

UNITS = 16
ST_LAG, PV_LAG = 11, 16
ALL_UNITS = UNITS * TILES


def r32(ap):
    return ap.bitcast(F32R)


def build(nc, a):
    ctx = ExitStack()
    with ctx:
        def sb(name, shape, dt=F32):
            return ctx.enter_context(nc.sbuf_tensor(name, shape, dt))

        def pb(name, shape, dt=F32):
            return ctx.enter_context(nc.psum_tensor(name, shape, dt))

        def sem(name):
            return ctx.enter_context(nc.semaphore(name))

        x = sb("x", [P, TILES, T])
        cx = sb("cx", [P, TILES, T])
        cxT = sb("cxT", [P, 2, N * E])
        ident = sb("ident", [P, P])
        band = sb("band", [P, 2, WIN], BF16)
        masked = sb("masked", [P, 2, 2, WIN], BF16)
        kmask = sb("kmask", [P, 4])
        cols = sb("cols", [P, 4])
        tri = sb("tri", [P, P])
        blk = sb("blk", [P, P])
        slot = sb("slot", [P, 2 * P])
        w0 = sb("w0", [P, 4, P])
        w0h = sb("w0h", [P, 4, P])
        w0l = sb("w0l", [P, 2, 4, P])
        b0 = sb("b0", [P, 4])
        sb0 = sb("sb0", [P, 4])
        wv0 = sb("wv0", [P, P])
        wo0 = sb("wo0", [P, P])
        wc0 = sb("wc0", [P, P])
        bcol = sb("bcol", [P, 4])
        vecs = sb("vecs", [P, 5, T])
        br = sb("br", [P, 1])
        b1 = sb("b1", [P, FC])
        w1 = sb("w1", [P, 2, DF])
        w2 = sb("w2", [P, FC, T])
        wq1 = sb("wq1", [P, 2, T])
        spread = sb("spread", [P, 2, 4, P])
        wk1 = sb("wk1", [P, 2, 2, P])
        wv1 = sb("wv1", [P, 2, 64])
        wf1 = sb("wf1", [P, 2, T])
        up = sb("up", [P, 2, DF])
        down = sb("down", [P, FC, T])
        eg = sb("eg", [P, 2, T + NEXP])
        st6 = sb("st6", [P, 2, 6])
        mv = sb("mv", [P, TILES, 2])
        rstd = sb("rstd", [P, TILES])
        xn = sb("xn", [P, 2, T])
        xs = sb("xs", [P, 2, T])
        hs = sb("hs", [P, 2, 2 * T])
        qk = sb("qk", [P, 10240])
        qp = qk[:, 8192:10240].rearrange("p (m g b q) -> p m g b q", m=2, g=2, b=2)
        kp = sb("kp", [P, 2, 2, T])
        kb = qk[:, 0:8192].rearrange("p (m g j b k) -> p m g j b k", m=2, g=2, j=4, b=2)
        v0 = sb("v0", [P, 2, 2, 2, 8, 32])
        mw = sb("mw", [P, 2, 4, P])
        ex = sb("ex", [P, 4, 4, WIN])
        osb = sb("osb", [P, 2, 512])
        rc = sb("rc", [P, 2, 32])
        on = sb("on", [P, 2, 2 * P])
        onT = sb("onT", [P, 2, T])
        yr = sb("yr", [P, 2, T])
        sc = sb("sc", [P, TILES])
        rk = sb("rk", [P, TILES])
        cmp = sb("cmp", [P, 3, P])
        exf = ex[:, :, :, :].rearrange("p a b c -> p (a b c)")
        sel = sb("sel", [P, 2, P])
        osel = exf[:, 0:1024].rearrange("p (m c) -> p m c", m=4)
        hT = sb("hT", [P, FC, 512])
        xT = sb("xT", [P, 2, N * E])
        xsT = xT[:, :, 0:SLOTS]
        q1 = qk[:, 0:6144].rearrange("p (m g t b i q) -> p m g t b i q", m=3, g=2, t=2, b=2, i=4)
        k1 = qk[:, 6144:10240].rearrange("p (m g b j k) -> p m g b j k", m=4, g=2, b=2, j=4)
        k1p = kp[:, 0, :, :].rearrange("p b k -> p (b k)")
        k1h = xs[:, :, :].rearrange("p a k -> p (a k)")
        v1 = sb("v1", [P, 6, 2, 4, 32])
        xq = [qk[:, 2048 * (1 - h):2048 * (2 - h)].rearrange("p (t a k c) -> p t a k c", t=4, a=2, k=2) for h in range(2)]
        up2 = qk[:, 4096:8192].rearrange("p (a k f) -> p a k f", a=2, k=2)
        eg2 = qk[:, 8192:8192 + 4 * (T + NEXP)].rearrange("p (a k f) -> p a k f", a=2, k=2)
        tk = sb("tk", [P, 2, 8])
        warm = sb("warm", [P, 1])

        S = [pb(f"S{i}", [P, 512]) for i in range(2)]
        ST = [pb(f"ST{i}", [P, 512]) for i in range(2)]
        O = pb("O", [P, 512])
        PJ = pb("PJ", [P, 512])
        MT = pb("MT", [P, 512])
        XB = pb("XB", [P, 512])

        names = ("ld_first ld_w0 ld_small ld_x1 ld_x ld_rest ld_late st_out "
                 "pe_proj pe_v pe_s pe_mt pe_st pe_pv pe_ot pe_bt pe_out pe_wct pe_bias "
                 "act_hs act_v act_mt act_exp act_o act_bt act_relu act_xh act_sb "
                 "dve_w dve_band dve_ln dve_xn dve_xl dve_mix dve_max dve_rc dve_on dve_x dve_zero "
                 "pool_var pool_rstd pool_mw dve_y pool_kb pool_sel pool_zero act_kb dve_spread ld_sel "
                 "f_ln f_rstd f_xn f_sc f_cmp f_sel fp_sT fp_x fa_x fp_up fa_up fp_dn f_dn fp_sc f_x "
                 "g_ln g_rstd g_xn gp_xT ga_xT gp_k ga_hk g_mk gpool_k gp_v ga_v gp_q ga_hq g_lq gp_e ga_q g_q gp_s g_max gp_mt ga_mt "
                 "gp_st ga_ex gp_pv ga_o gp_ot g_rc g_on g_y gp_bt ga_bt gp_out g_x "
                 "h_ln h_rstd h_xn hp_xT ha_xT hl_xT ha_w hpool_w hpool_up h_xb hp_up ha_up h_up hp_dn hp_eg h_tk h_moe h_ln2 h_rstd2 h_y h_out").split()
        s = {n: sem(n) for n in names}
        block = ctx.enter_context(nc.Block())

        def place(T_, l, lag):
            off, r = divmod(l - lag, UNITS)
            return T_ + off, r

        def live(tile, r):
            return 0 <= UNITS * tile + r < ALL_UNITS

        def parts(r):
            return r // 8, (r % 8) // 4, (r % 4) // 2, r % 2

        def xg(t, k):
            return x_norm(t)[:, P * k:P * k + P]

        def proj_bank(t, n):
            return (PJ, S[1], S[0], ST[0])[n] if t == 0 else PJ

        def value_bank(t):
            return ST[1] if t == 0 else PJ

        def x_norm(t):
            return hT[:, t, 256:512]

        def selT(t):
            return xT[:, t // 4, SLOTS + P * (t % 4):SLOTS + P * (t % 4) + P]

        def up_bank(f):
            return S[f % 2][:, 0:T]

        def e1(u):
            return ex[:, u % 4, :, :].rearrange("p a b -> p (a b)")[:, 0:512]

        def q1f(t, g, b):
            return q1[:, (t // 2) % 3, g, t % 2, b, :, :].rearrange("p i q -> p (i q)")

        def spread_at(n):
            for i, first in enumerate(SPREAD):
                p = at(n, first, 8, PAIRS)
                if p is not None:
                    return 4 * p + i
            return None

        def spread_read(e):
            p, i = divmod(e, 4)
            return (s["ga_q"], 2 * p + 1 + i // 2) if i in (0, 3) else (s["g_q"], 2 * p + i)

        def relu(m):
            return cxT[:, m % 2, 0:512]

        def stacked(p, i):
            return r32(q1[:, p % 3, :, :, :, i, :].rearrange("p g t b q -> p g (t b) q"))

        def down_bank(c):
            return (O, PJ, ST[0], ST[1])[c][:, 0:T]

        def scatter_bank(t):
            return (XB, (ST[0], O)[t // 4])[t % 2][:, 0:T]

        def at(n, first, step, count):
            q, r = divmod(n - first, step)
            return q if r == 0 and 0 <= q < count else None

        MOE_OUT = {46: 0, 48: 1, 53: 2}
        PARTS = [(k, a, b) for k in range(2) for a, b in ((0, 0), (0, 1), (1, 0))]
        SCATTER1 = {-3: (4,), -2: (5,), 4: (6, 7)}
        PAIRS = TILES // 2
        SPREAD = (-7, -6, -4, -2)
        SLOTS1 = range(-18, 54)
        SLOTS_ALL = [(n // UNITS, n % UNITS) for n in range(-2 * UNITS, UNITS * (TILES + 2) + 9)]
        PROJ = {3: 0, 6: 1, 9: 2, 12: 3}
        KB = {5: (0, 0), 9: (0, 1), 14: (1, 0)}
        KA = {11: 0, 12: 1, 15: 2, 18: 3}

        def tail(T_, l):
            n = UNITS * (T_ - TILES) + l - ST_LAG
            if 0 <= n < FC:
                return "up", n
            if FC <= n < 2 * FC:
                return "down", n - FC
            if 2 * FC + 7 <= n < 2 * FC + 11:
                return "scatter", n - 2 * FC - 7
            return "", 0

        @block.sync
        def _(sp):
            def load(dst, src, name):
                sp.dma_start(dst, src).then_inc(s[name], 16)
            xv = a["x"].rearrange("(t p) c -> p t c", p=P)
            load(x[:, 0, :], xv[:, 0, :], "ld_first")
            load(cols[:, :], a["cols"], "ld_first")
            load(exf[:, 0:2 * WIN], a["band"], "ld_small")
            load(ident[:, :], a["ident"], "ld_small")
            load(x[:, 1, :], xv[:, 1, :], "ld_x1")
            load(x[:, 2:TILES, :], xv[:, 2:TILES, :], "ld_x")
            load(wo0[:, :], a["wo0"], "ld_rest")
            load(wc0[:, :], a["wc0"], "ld_rest")
            load(bcol[:, :], a["bcol"], "ld_rest")
            load(cx[:, :, :], a["cx"].rearrange("(t p) c -> p t c", p=P), "ld_rest")
            load(vecs[:, :, :], a["vecs"][None, :, :].to_broadcast([P, 5, T]), "ld_sel")
            load(br[:, :], a["br"][:, :].to_broadcast([P, 1]), "ld_sel")
            load(tri[:, :], a["tri"], "ld_sel")
            load(blk[:, :], a["blk"], "ld_sel")
            load(slot[:, :], a["slot"], "ld_sel")
            load(hT[:, 0:2, :].rearrange("p a b -> p (a b)"), a["spread"], "ld_sel")
            late = [(b1[:, :], a["b1"]),
                    (w1[:, :, :], a["w1"].rearrange("(k p) f -> p k f", p=P)),
                    (w2[:, :, :], a["w2"].rearrange("(k p) f -> p k f", p=P)),
                    (wq1[:, :, :], a["wq1"].rearrange("(k p) f -> p k f", p=P)), (wk1[:].rearrange("p a b c -> p (a b c)"), a["wk1"]),
                    (wv1[:, :, :], a["wv1"].rearrange("(k p) f -> p k f", p=P)),
                    (wf1[:, :, :], a["wf1"].rearrange("(k p) f -> p k f", p=P)),
                    (cxT[:, :, :], a["cxT"].rearrange("(k p) f -> p k f", p=P)),
                    (up[:, :, :], a["up"].rearrange("(k p) f -> p k f", p=P)),
                    (down[:, :, :], a["down"].rearrange("(k p) f -> p k f", p=P)),
                    (eg[:, :, 0:T], a["ew"].rearrange("(k p) f -> p k f", p=P)),
                    (eg[:, :, T:T + NEXP], a["gw"].rearrange("(k p) f -> p k f", p=P))]
            assert len(late) == 12
            for dst, src in late:
                load(dst, src, "ld_late")
            ov = a["out"].rearrange("(t p) c -> p t c", p=P)
            for t in range(TILES):
                sp.wait_ge(s["h_out"], t + 1)
                sp.dma_start(ov[:, t, :], x[:, t, :]).then_inc(s["st_out"], 16)
            sp.wait_ge(s["st_out"], 16 * TILES)
        LATE = 16 * 12

        @block.tensor
        def _(pe):
            mm, tr = nc.tensor.matmul, nc.tensor.transpose

            def project(t, n):
                if n == 0:
                    pe.wait_ge(s["act_xh"], t + 1)
                    pe.wait_ge(s["dve_xl"], t + 1)
                    if t == 0:
                        pe.wait_ge(s["dve_w"], 4)
                bank = proj_bank(t, n)
                if t >= 1:
                    pe.wait_ge(s["dve_mix"], 4 * t + n)
                if n == 0 and t >= 1:
                    pe.wait_ge(s["act_v"], t)
                for b in range(2):
                    mm(bank[:, T * b:T * b + T], r32(w0h[:, n, :]), r32(xs[:, b, :]), start=True, stop=False)
                    last = mm(bank[:, T * b:T * b + T], r32(w0l[:, b, n, :]), r32(xs[:, b, :]), start=False, stop=True)
                last.then_inc(s["pe_proj"], 1)

            def values(t):
                if t >= 1:
                    pe.wait_ge(s["dve_mix"], 4 * t + 4)
                if t == 0:
                    pe.wait_ge(s["ld_small"], 64)
                pe.wait_ge(s["dve_xn"], t + 1)
                for c in range(2):
                    last = mm(value_bank(t)[:, P * c:P * c + P], xn[:, t % 2, P * c:P * c + P], wv0[:, :], start=True, stop=True)
                last.then_inc(s["pe_v"], 1)

            def slot_(T_, l):
                t, r = T_, l
                if live(t, r):
                    n = UNITS * t + r
                    b, g, c, w = parts(r)
                    if (b, g) == (1, 1):
                        pe.wait_ge(s["act_kb"], t + 1)
                    else:
                        pe.wait_ge(s["pool_kb"], 3 * t + 1 + g + 2 * b)
                    if r in (0, 4):
                        pe.wait_ge(s["dve_mix"], 4 * t + 3 + g)
                    if n >= 2:
                        pe.wait_ge(s["dve_max"], n - 1)
                    mv_ = kb[:, t % 2, g, 2 * w:2 * w + 2, b, BAND * c:BAND * c + WIN]
                    out = S[n % 2][:, 0:2 * WIN].rearrange("p (h k) -> p h k", h=2)
                    mm(out, r32(qp[:, t % 2, g, b, P * c:P * c + P]), r32(mv_), start=True, stop=True).then_inc(s["pe_s"], 1)
                t, r = place(T_, l, 9)
                if l % 8 == 1 and live(t, r):
                    k = 2 * t + r // 8
                    pe.wait_ge(s["dve_max"], UNITS * t + r + 8)
                    if k >= 1:
                        pe.wait_ge(s["act_mt"], k)
                    if l == 9 and T_ >= 3:
                        pe.wait_ge(s["fa_x"], T_ - 2)
                    for gc in range(4):
                        last = tr(MT[:, P * gc:P * gc + P], mw[:, (r // 8), gc, :], ident[:, :])
                    last.then_inc(s["pe_mt"], 1)
                t, r = place(T_, l, ST_LAG)
                if live(t, r):
                    n = UNITS * t + r
                    b, g, c, w = parts(r)
                    pe.wait_ge(s["act_mt"], 2 * t + b + 1)
                    if n >= 2:
                        pe.wait_ge(s["act_exp"], n - 1)
                    if n < 2:
                        pe.wait_ge(*((s["dve_mix"], 4), (s["act_v"], 1))[n])
                    for h in range(2):
                        last = mm(ST[n % 2][:, WIN * h:WIN * h + WIN], r32(kb[:, t % 2, g, 2 * w + h, b, P * c:P * c + P]),
                                  r32(qp[:, t % 2, g, b, BAND * c:BAND * c + WIN]), start=True, stop=True)
                    last.then_inc(s["pe_st"], 1)
                for t, r in {0: (), 1: (place(T_, l, PV_LAG + 1), place(T_, l, PV_LAG))}.get(l % 8, (place(T_, l, PV_LAG),)):
                    if not live(t, r):
                        continue
                    n = UNITS * t + r
                    b, g, c, w = parts(r)
                    pe.wait_ge(s["pool_sel"], n // 2 + 1)
                    pe.wait_ge(s["act_v"], t + 1)
                    if r % 8 == 0 and n >= 8:
                        pe.wait_ge(s["act_o"], n // 8)
                    for h in range(2):
                        j = 2 * w + h
                        last = mm(O[32 * j:32 * j + 32, T * g + BAND * c:T * g + BAND * c + WIN],
                                  v0[:, t % 2, c, b, 4 * g + j, :], ex[:, (n // 2) % 4, j, :],
                                  start=(c == 0), stop=(c == 1), skip_group_check=True)
                    last.then_inc(s["pe_pv"], 1)
                t, r = place(T_, l, 26)
                if l % 8 == 2 and live(t, r):
                    k = 2 * t + r // 8
                    pe.wait_ge(s["act_o"], k + 1)
                    if k >= 1:
                        pe.wait_ge(s["dve_on"], k)
                    if k % 2 == 0 and k >= 2:
                        pe.wait_ge(s["dve_x"], k // 2)
                    for c in range(2):
                        for g in range(2):
                            last = tr(XB[:, T * c + P * g:T * c + P * g + P], osb[:, k % 2, T * g + P * c:T * g + P * c + P], ident[:, :])
                    last.then_inc(s["pe_ot"], 1)
                t = T_ - 2
                if 0 <= t < TILES:
                    if l == 4:
                        pe.wait_ge(s["dve_on"], 2 * t + 2)
                        for c in range(2):
                            last = tr(XB[:, P * c:P * c + P], on[:, c, 0:P], ident[:, :])
                        last.then_inc(s["pe_bt"], 1)
                    if l == 5:
                        pe.wait_ge(s["act_bt"], t + 1)
                        mm(XB[:, 0:T], wo0[:, :], onT[:, t % 2, :], start=True, stop=True).then_inc(s["pe_out"], 1)
                    if l == 7:
                        pe.wait_ge(s["dve_y"], t + 1)
                        mm(XB[:, 0:T], wc0[:, :], yr[:, 1, :], start=True, stop=True).then_inc(s["pe_wct"], 1)
                t = T_ - 3
                if l == 2 and 0 <= t < TILES:
                    pe.wait_ge(s["f_sc"], t + 1)
                    pe.wait_ge(s["act_mt"], min(2 * T_, 2 * TILES))
                    if t >= 1:
                        pe.wait_ge(s["fa_x"], t)
                    tr(MT[:, 0:P], sc[:, t:t + 1].to_broadcast([P, P]), ident[:, :]).then_inc(s["fp_sT"], 1)
                if l == 6 and 0 <= t < TILES:
                    pe.wait_ge(s["f_sel"], t + 1)
                    tr(MT[:, 0:P], sel[:, t % 2, :], ident[:, :])
                    o = (t % 2) * 64
                    for k in range(2):
                        last = mm(MT[:, P + 64 * k:P + 64 * k + 64], xg(t, k), sel[:, t % 2, o:o + 64], start=True, stop=True)
                    last.then_inc(s["fp_x"], 1)
                if T_ + 1 >= 0 and T_ + 1 < TILES:
                    if l in PROJ:
                        project(T_ + 1, PROJ[l])
                    if l == 15:
                        values(T_ + 1)
                if (T_, l) == (TILES + 2, 1):
                    keys1(0)
                if (T_, l) == (TILES + 2, 7):
                    values1(0)
                kind, n = tail(T_, l)
                if kind == "up":
                    ffn_up(0, n)
                if kind == "down":
                    for i in (2 * n, 2 * n + 1):
                        ffn_down(0, i // FC, i % FC)
                if kind == "scatter":
                    scatter(n)

            def keys1(p):
                if p == 0:
                    pe.wait_ge(s["ld_late"], LATE)
                    pe.wait_ge(s["f_dn"], 2)
                else:
                    pe.wait_ge(s["ga_hq"], p + 1)
                    pe.wait_ge(s["g_lq"], p + 1)
                for g in range(2):
                    for k in range(2):
                        last = mm(PJ[:, T * g:T * g + T], wk1[:, k, g, :], cxT[:, k, T * p:T * p + T], start=(k == 0), stop=(k == 1))
                last.then_inc(s["gp_k"], 1)

            def values1(p):
                pe.wait_ge(s["g_mk"], p + 1)
                for tt in range(2):
                    for k in range(2):
                        last = mm(PJ[:, 64 * tt:64 * tt + 64], cxT[:, k, P * (2 * p + tt):P * (2 * p + tt) + P], wv1[:, k, :],
                                  start=(k == 0), stop=(k == 1))
                last.then_inc(s["gp_v"], 1)

            def ffn_up(half, f):
                m = FC * half + f
                if m == 0:
                    pe.wait_ge(s["ld_late"], LATE)
                    pe.wait_ge(s["dve_max"], ALL_UNITS)
                if f == 0:
                    pe.wait_ge(s["fa_x"], 4 * half + 4)
                if m >= 2:
                    pe.wait_ge(s["fa_up"], m - 1)
                for k in range(2):
                    last = mm(up_bank(f), w1[:, k, P * f:P * f + P], xsT[:, k, T * half:T * half + T], start=(k == 0), stop=(k == 1))
                last.then_inc(s["fp_up"], 1)

            def ffn_down(half, m, f):
                if (half, m, f) == (0, 0, 0):
                    pe.wait_ge(s["act_o"], 2 * TILES)
                    pe.wait_ge(s["act_v"], TILES)
                if (half, m, f) == (1, 0, 0):
                    pe.wait_ge(s["f_x"], 4)
                if m == 0:
                    pe.wait_ge(s["fa_up"], FC * half + f + 1)
                c = 2 * half + m
                last = mm(down_bank(c), hT[:, f, P * c:P * c + P], w2[:, f, :], start=(f == 0), stop=(f == FC - 1))
                if f == FC - 1:
                    last.then_inc(s["fp_dn"], 1)

            def scatter(t):
                pe.wait_ge(s["f_dn"], t // 2 + 1)
                if t == 0:
                    pe.wait_ge(s["dve_x"], TILES)
                    pe.wait_ge(s["act_exp"], ALL_UNITS)
                if t == 5:
                    pe.wait_ge(s["f_dn"], 1)
                elif t >= 2:
                    pe.wait_ge(s["f_x"], t - 1)
                mm(scatter_bank(t), selT(t), osel[:, t // 2, :], start=True, stop=True).then_inc(s["fp_sc"], 1)

            for T_, l in SLOTS_ALL:
                if T_ == 1 and l == 0:
                    pe.wait_ge(s["ld_rest"], 64)
                    mm(XB[:, 0:1], wo0[:, :], bcol[:, 0:1], start=True, stop=True).then_inc(s["pe_bias"], 1)
                if T_ == 1 and l == 10:
                    pe.wait_ge(s["dve_w"], 5)
                slot_(T_, l)

            def slot1(n):
                f = at(n, -16, 1, FC)
                if f is not None:
                    ffn_up(1, f)
                i = at(n, -8, 1, 4)
                if i is not None:
                    ffn_down(1, 0, 2 * i)
                    ffn_down(1, 0, 2 * i + 1)
                f = at(n, -4, 1, FC)
                if f is not None:
                    ffn_down(1, 1, f)
                for t in SCATTER1.get(n, ()):
                    scatter(t)
                u = at(n, 0, 1, 4 * TILES)
                if u is not None:
                    t, l = divmod(u, 4)
                    b, g = divmod(l, 2)
                    if l == 0:
                        pe.wait_ge(s["ga_q"], 2 * (t // 2) + 2)
                        pe.wait_ge(s["g_q"], 2 * (t // 2) + 2)
                    if l < 2:
                        pe.wait_ge(s["gpool_k"], 2 * t + l + 1)
                    if u == 0:
                        pe.wait_ge(s["fa_up"], 2 * FC)
                    if u >= 1:
                        pe.wait_ge(s["g_max"], u)
                    for ii in range(2):
                        last = mm(S[0][:, T * ii:T * ii + T], r32(q1[:, (t // 2) % 3, g, t % 2, b, 2 * ii:2 * ii + 2, :]),
                                  r32(k1[:, t % 4, g, b, :, :]), start=True, stop=True)
                    last.then_inc(s["gp_s"], 1)
                u = at(n, 5, 1, 4 * TILES)
                if u is not None:
                    t, l = divmod(u, 4)
                    b, g = divmod(l, 2)
                    pe.wait_ge(s["ga_mt"], u // 2 + 1)
                    if u < 2:
                        pe.wait_ge(s["f_dn"], 3 + u)
                    if u >= 2:
                        pe.wait_ge(s["ga_ex"], u - 1)
                    for jp in range(2):
                        last = mm(ST[u % 2][:, T * jp:T * jp + T], r32(k1[:, t % 4, g, b, 2 * jp:2 * jp + 2, :]),
                                  r32(q1f(t, g, b)), start=True, stop=True)
                    last.then_inc(s["gp_st"], 1)
                t = at(n, 12, 4, TILES)
                if t is not None:
                    pe.wait_ge(s["ga_o"], t + 1)
                    if t == 0:
                        pe.wait_ge(s["f_x"], TILES)
                    if t >= 1:
                        pe.wait_ge(s["g_x"], t)
                    for i in range(4):
                        last = tr(XB[:, P * i:P * i + P], osb[:, t % 2, P * i:P * i + P], ident[:, :])
                    last.then_inc(s["gp_ot"], 1)
                p = at(n, -13, 8, PAIRS)
                if p is not None:
                    pe.wait_ge(s["g_xn"], 2 * p + 2)
                    pe.wait_ge(s["ga_v"], max(p, 1))
                    if p >= 1:
                        pe.wait_ge(s["ga_hq"], p)
                        pe.wait_ge(s["g_lq"], p)
                    for k in range(2):
                        for tt in range(2):
                            last = tr(PJ[:, T * k + P * tt:T * k + P * tt + P], xn[:, tt, P * k:P * k + P], ident[:, :])
                    last.then_inc(s["gp_xT"], 1)
                for g in range(2):
                    p = at(n, -11 + g, 8, PAIRS)
                    if p is not None:
                        pe.wait_ge(s["ga_xT"], p + 1)
                        for k in range(2):
                            last = mm(PJ[:, T * g:T * g + T], wq1[:, k, P * g:P * g + P], xT[:, k, T * p:T * p + T], start=(k == 0), stop=(k == 1))
                        last.then_inc(s["gp_q"], 1)
                p = at(n, -8, 8, PAIRS)
                if p:
                    keys1(p)
                p = at(n, -6, 8, PAIRS)
                if p:
                    values1(p)
                t = at(n, 13, 4, TILES)
                if t is not None:
                    pe.wait_ge(s["g_on"], t + 1)
                    for c in range(2):
                        last = tr(XB[:, P * c:P * c + P], on[:, t % 2, P * c:P * c + P], ident[:, :])
                    last.then_inc(s["gp_bt"], 1)
                t = at(n, 14, 4, TILES)
                if t is not None:
                    pe.wait_ge(s["ga_bt"], t + 1)
                    for c in range(2):
                        last = mm(XB[:, T:2 * T], onT[:, t % 2, P * c:P * c + P], wf1[:, c, :], start=(c == 0), stop=(c == 1))
                    last.then_inc(s["gp_out"], 1)
                e = spread_at(n)
                if e is not None:
                    pe.wait_ge(s["g_lq"], e // 4 + 1)
                    if e == 0:
                        pe.wait_ge(s["dve_spread"], 1)
                        pe.wait_ge(s["fa_up"], 2 * FC)
                    else:
                        pe.wait_ge(*spread_read(e - 1))
                    for part in range(2):
                        last = mm(S[1][:, :], r32(spread[:, part, e % 4, :]), r32(hs[:, part, :]), start=(part == 0), stop=(part == 1))
                    last.then_inc(s["gp_e"], 1)
                for u in {2: (), 3: (n - 7, n - 6)}.get(n % 4, (n - 6,)):
                    if not 0 <= u < 4 * TILES:
                        continue
                    t, l = divmod(u, 4)
                    b, g = divmod(l, 2)
                    pe.wait_ge(s["ga_ex"], u + 1)
                    pe.wait_ge(s["ga_v"], t // 2 + 1)
                    if l == 0 and t >= 1:
                        pe.wait_ge(s["ga_o"], t)
                    for jp in range(2):
                        pr = 2 * g + jp
                        last = mm(O[32 * pr:32 * pr + 32, T * b:T * b + T], v1[:, t % 6, b, pr, :], e1(u)[:, T * jp:T * jp + T],
                                  start=True, stop=True)
                    last.then_inc(s["gp_pv"], 1)
                k = at(n, 3, 2, 2 * TILES)
                if k is not None:
                    pe.wait_ge(s["g_max"], 2 * k + 2)
                    if at(n, 21, 4, TILES) is not None:
                        pe.wait_ge(s["hl_xT"], at(n, 21, 4, TILES) + 1)
                    if k >= 1:
                        pe.wait_ge(s["ga_mt"], k)
                    for gi in range(4):
                        last = tr(MT[:, P * gi:P * gi + P], mw[:, k % 2, gi, :], ident[:, :])
                    last.then_inc(s["gp_mt"], 1)
                t = at(n, 20, 4, TILES)
                if t is not None:
                    pe.wait_ge(s["h_xn"], t + 1)
                    k = at(n, 4, 2, 2 * TILES)
                    if k is not None:
                        pe.wait_ge(s["ga_mt"], k + 1)
                    else:
                        pe.wait_ge(s["hl_xT"], t)
                    for k in range(2):
                        last = tr(MT[:, P * k:P * k + P], xn[:, t % 2, P * k:P * k + P], ident[:, :])
                    last.then_inc(s["hp_xT"], 1)
                f = at(n, 35, 1, FC)
                if f is not None:
                    moe_up(0, f)
                i = at(n, 44, 1, FC)
                if i is not None:
                    moe_down(i // 2, 4 * (i % 2), 4 * (i % 2) + 4)

            def moe_up(half, f):
                m = FC * half + f
                if m == 0:
                    pe.wait_ge(s["g_max"], 4 * TILES)
                    pe.wait_ge(*spread_read(4 * PAIRS - 1))
                if m == 0:
                    pe.wait_ge(s["hpool_w"], 4)
                if f == 0:
                    pe.wait_ge(s["hl_xT"], 4 * half + 4)
                if m >= 2:
                    pe.wait_ge(s["ha_up"], m - 1)
                for i, (k, a, b) in enumerate(PARTS):
                    last = mm(S[m % 2][:, :].rearrange("p (t c) -> p t c", t=4), r32(up2[:, a, k, P * f:P * f + P]),
                              r32(xq[half][:, :, b, k, :]), start=(i == 0), stop=(i == len(PARTS) - 1))
                last.then_inc(s["hp_up"], 1)

            def moe_down(t, f0, f1):
                half, m = divmod(t, 4)
                if f0 == 0:
                    if t == 0:
                        pe.wait_ge(s["ga_o"], TILES)
                        pe.wait_ge(s["ga_ex"], 4 * TILES)
                    if t == 1:
                        pe.wait_ge(s["ga_v"], PAIRS)
                    if t >= 2:
                        pe.wait_ge(s["h_y"], 2 * t - 3)
                    if t == 0:
                        pe.wait_ge(s["hpool_w"], 5)
                    for i, (k, a, b) in enumerate(PARTS):
                        last = mm((O, PJ)[t % 2][:, 0:T + NEXP], r32(xq[half][:, m, b, k, :]), r32(eg2[:, a, k, :]),
                                  start=(i == 0), stop=(i == len(PARTS) - 1))
                    last.then_inc(s["hp_eg"], 1)
                for f in range(f0, f1):
                    if m == 0:
                        pe.wait_ge(s["hpool_up" if half else "h_up"], f + 1)
                    last = mm(ST[t % 2][:, 0:T], hT[:, f, P * m:P * m + P], down[:, f, :], start=(f == 0), stop=(f == FC - 1))
                if f1 == FC:
                    last.then_inc(s["hp_dn"], 1)

            for n in SLOTS1:
                slot1(n)

            for f in range(FC):
                moe_up(1, f)
            for t in range(4, TILES):
                moe_down(t, 0, FC)

        @block.scalar
        def _(act):
            A = nc.scalar.activation

            def load(dst, src, name):
                act.dma_start(dst, src).then_inc(s[name], 16)
            load(w0[:, :, :], a["w0"], "ld_w0")
            load(b0[:, :], a["b0"], "ld_w0")
            load(kmask[:, :], a["kmask"], "ld_small")
            load(wv0[:, :], a["wv0"], "ld_small")

            def slot_(T_, l):
                t = T_ - 2
                if 0 <= t < TILES:
                    if l == 5:
                        act.wait_ge(s["pe_bt"], t + 1)
                        nc.scalar.copy(onT[:, t % 2, :], XB[:, 0:T]).then_inc(s["act_bt"], 1)
                    if l == 6:
                        act.wait_ge(s["pe_out"], t + 1)
                        if t == 0:
                            act.wait_ge(s["dve_w"], 5)
                        if t >= 1:
                            act.wait_ge(s["dve_y"], t)
                        A(yr[:, 0, :], XB[:, 0:T], ACT.Relu, bias=bcol[:, 3:4]).then_inc(s["act_relu"], 1)
                t = T_ - 3
                if l == 8 and 0 <= t < TILES:
                    act.wait_ge(s["fp_x"], t + 1)
                    nc.scalar.copy(selT(t), MT[:, 0:P])
                    nc.scalar.copy(xsT[:, :, 64 * t:64 * t + 64], MT[:, P:2 * P].rearrange("p (k c) -> p k c", k=2)).then_inc(s["fa_x"], 1)
                t, r = place(T_, l, 24)
                if l % 8 == 0 and live(t, r):
                    k = 2 * t + r // 8
                    act.wait_ge(s["pe_pv"], 8 * k + 8)
                    if k >= 2:
                        act.wait_ge(s["pe_ot"], k - 1)
                    nc.scalar.copy(osb[:, k % 2, :], O[:, :]).then_inc(s["act_o"], 1)
                t = T_ + 1
                if 0 <= t < TILES:
                    if l - 1 in PROJ:
                        n = PROJ[l - 1]
                        m = 4 * t + n
                        act.wait_ge(s["pe_proj"], m + 1)
                        if m == 0:
                            act.wait_ge(s["dve_w"], 4)
                        if m >= 2:
                            act.wait_ge(s["dve_mix"], m - 1)
                        A(r32(hs[:, m % 2, :]), proj_bank(t, n)[:, :], ACT.Identity, bias=sb0[:, n:n + 1], scale=cols[:, n // 2:n // 2 + 1])\
                            .then_inc(s["act_hs"], 1)
                for t, j in ((T_ + 1, KA.get(l)), (T_, KA.get(l + UNITS))):
                    if j is not None and 0 <= t < TILES:
                        if j == 0:
                            act.wait_ge(s["dve_mix"], 4 * t + 2)
                            if t == 0:
                                act.wait_ge(s["ld_small"], 64)
                            if t >= 2:
                                act.wait_ge(s["pe_st"], UNITS * (t - 1))
                        last = A(r32(kb[:, t % 2, 1, j, 1, :]), kp[:, 1, 1, :], ACT.Copy, scale=kmask[:, j:j + 1])
                        if j == 3:
                            last.then_inc(s["act_kb"], 1)
                if l == 0 and 0 <= T_ < TILES:
                    t = T_
                    act.wait_ge(s["pe_v"], t + 1)
                    if t >= 2:
                        act.wait_ge(s["pe_pv"], UNITS * (t - 1))
                    nc.scalar.copy(v0[:, t % 2, :, :, :, 0:8].rearrange("p c b h d -> p (c b) h d"),
                                   value_bank(t)[:, 0:T].rearrange("p (c h d) -> p c h d", c=4, h=8)).then_inc(s["act_v"], 1)
                t = T_ + 2
                if l == 14 and 0 <= t < TILES:
                    act.wait_ge(s["dve_xn"], t + 1)
                    if t >= 1:
                        act.wait_ge(s["pe_proj"], 4 * t)
                    A(r32(xs[0:64, 0, :]), xn[0:64, t % 2, :], ACT.Copy)
                    A(r32(xs[64:128, 1, :]), xn[64:128, t % 2, :], ACT.Copy).then_inc(s["act_xh"], 1)
                t, r = place(T_, l, ST_LAG)
                if live(t, r):
                    n = UNITS * t + r
                    b, g, c, w = parts(r)
                    act.wait_ge(s["pe_st"], n + 1)
                    if n >= 8:
                        act.wait_ge(s["pe_pv"], (n // 2 - 4) * 2 + 2)
                    A(ex[:, (n // 2) % 4, 2 * w:2 * w + 2, :], ST[n % 2][:, 0:2 * WIN].rearrange("p (h k) -> p h k", h=2),
                      ACT.Exp, scale=SCALE).then_inc(s["act_exp"], 1)
                t, r = place(T_, l, 9)
                if l % 8 == 1 and live(t, r):
                    k = 2 * t + r // 8
                    act.wait_ge(s["pe_mt"], k + 1)
                    A(r32(qp[96:128, t % 2, :, r // 8, :].rearrange("p g (c q) -> p c g q", c=2)),
                      MT[96:128, :].rearrange("p (c g q) -> p c g q", c=2, g=2), ACT.Copy, scale=-1.0)\
                        .then_inc(s["act_mt"], 1)
                if (T_, l) == (TILES + 2, 1):
                    keys1(0)
                if (T_, l) == (TILES + 2, 8):
                    values1(0)
                kind, n = tail(T_, l)
                if kind == "up":
                    gelu(0, n)

            def keys1(p):
                act.wait_ge(s["gp_k"], p + 1)
                if p >= 1:
                    act.wait_ge(s["g_mk"], p)
                A(r32(k1h), PJ[:, :], ACT.Identity, bias=0.0, scale=cols[:, 0:1]).then_inc(s["ga_hk"], 1)

            def values1(p):
                act.wait_ge(s["gp_v"], p + 1)
                if p == 0:
                    act.wait_ge(s["pool_zero"], 5)
                if p >= 3:
                    act.wait_ge(s["gp_pv"], 8 * (p - 2))
                for b in range(2):
                    for j2 in range(2):
                        last = nc.scalar.copy(v1[64 * j2:64 * j2 + 64, (2 * p) % 6:(2 * p) % 6 + 2, b, :, 16 * j2:16 * j2 + 8],
                                              PJ[64 * b:64 * b + 64, 0:128].rearrange("p (t r j d) -> p t r j d", t=2, r=4, j=2)[:, :, :, j2, :])
                last.then_inc(s["ga_v"], 1)

            def gelu(half, f):
                act.wait_ge(s["fp_up"], FC * half + f + 1)
                A(hT[:, f, T * half:T * half + T], up_bank(f), ACT.Gelu_apprx_tanh, bias=b1[:, f:f + 1]).then_inc(s["fa_up"], 1)

            act.wait_ge(s["pool_zero"], 1)
            A(warm[:, :], v0[:, 0, 0, 0, 0, 0:1], ACT.Exp)
            act.wait_ge(s["pool_zero"], 2)
            for T_, l in SLOTS_ALL:
                slot_(T_, l)

            def slot1(n):
                f = at(n, -16, 1, FC)
                if f is not None:
                    if f == 0:
                        act.wait_ge(s["fp_x"], TILES)
                    gelu(1, f)
                if n == 2:
                    A(warm[:, :], ident[:, 0:1], ACT.Exp)
                t = at(n, 10, 4, TILES)
                if t is not None:
                    act.wait_ge(s["gp_pv"], 4 * t + 4)
                    if t >= 2:
                        act.wait_ge(s["gp_ot"], t - 1)
                    nc.scalar.copy(osb[:, t % 2, :].rearrange("p (i b q) -> p b i q", b=2, i=4),
                                   O[:, :].rearrange("p (b i q) -> p b i q", b=2, i=4)).then_inc(s["ga_o"], 1)
                p = at(n, -5, 8, PAIRS)
                if p:
                    values1(p)
                p = at(n, -12, 8, PAIRS)
                if p is not None:
                    act.wait_ge(s["gp_xT"], p + 1)
                    act.wait_ge(*((s["fp_up"], FC * (p + 1)) if p < 2 else (s["fp_sc"], TILES)))
                    nc.scalar.copy(xT[:, :, T * p:T * p + T], PJ[:, :].rearrange("p (k c) -> p k c", k=2)).then_inc(s["ga_xT"], 1)
                p = at(n, -9, 8, PAIRS)
                if p is not None:
                    act.wait_ge(s["gp_q"], 2 * p + 2)
                    if p >= 1:
                        act.wait_ge(s["gp_e"], 4 * p)
                    A(r32(hs[:, 0, :]), PJ[:, :], ACT.Copy).then_inc(s["ga_hq"], 1)
                p = at(n, -7, 8, PAIRS)
                if p:
                    keys1(p)
                f = at(n, 36, 1, FC)
                if f is not None:
                    moe_relu(f)
                t = MOE_OUT.get(n)
                if t is not None:
                    moe_scale(t)
                i = at(n, 29, 1, 4)
                if i is not None:
                    act.wait_ge(s["gp_st"], 24)
                    k, c = divmod(i, 2)
                    nc.scalar.copy(r32(up2[:, 0, k, 512 * c:512 * c + 512]), up[:, k, 512 * c:512 * c + 512]).then_inc(s["ha_w"], 1)
                if n == 37:
                    act.wait_ge(s["gp_st"], 32)
                    nc.scalar.copy(r32(eg2[:, 0, :, :]), eg[:, :, :]).then_inc(s["ha_w"], 1)
                k = at(n, 4, 2, 2 * TILES)
                if k is not None:
                    t, b = divmod(k, 2)
                    act.wait_ge(s["gp_mt"], k + 1)
                    A(r32(q1[96:128, (t // 2) % 3, :, t % 2, b, :, :]), MT[96:128, :].rearrange("p (g i q) -> p g i q", g=2, i=4),
                      ACT.Copy, scale=-1.0).then_inc(s["ga_mt"], 1)
                t = at(n, 21, 4, TILES)
                if t is not None:
                    act.wait_ge(s["hp_xT"], t + 1)
                    if t % 4 == 0:
                        act.wait_ge(s["gp_st"], 16 * (1 + t // 4))
                    nc.scalar.copy(r32(xq[t // 4][:, t % 4, 0, :, :]), MT[:, 0:T].rearrange("p (k c) -> p k c", k=2)).then_inc(s["ha_xT"], 1)
                u = at(n, 5, 1, 4 * TILES)
                if u is not None:
                    act.wait_ge(s["gp_st"], u + 1)
                    if u >= 4:
                        act.wait_ge(s["gp_pv"], u - 3)
                    A(e1(u), ST[u % 2][:, :], ACT.Exp, scale=SCALE).then_inc(s["ga_ex"], 1)
                t = at(n, 13, 4, TILES)
                if t is not None:
                    act.wait_ge(s["gp_bt"], t + 1)
                    nc.scalar.copy(onT[:, t % 2, :], XB[:, 0:T]).then_inc(s["ga_bt"], 1)
                for i in (0, 3):
                    p = at(n, SPREAD[i] + 1, 8, PAIRS)
                    if p is not None:
                        act.wait_ge(s["gp_e"], 4 * p + i + 1)
                        if p >= 3:
                            act.wait_ge(s["gp_st"], 8 * (p - 2))
                        A(stacked(p, i), S[1][:, :].rearrange("p (g t q) -> p g t q", g=2, t=4), ACT.Copy).then_inc(s["ga_q"], 1)

            def moe_relu(m):
                act.wait_ge(s["hp_up"], m + 1)
                if m >= 2:
                    act.wait_ge(*((s["h_up"], m - 1) if m < FC + 2 else (s["hpool_up"], m - 1 - FC)))
                A(relu(m), S[m % 2][:, :], ACT.Relu).then_inc(s["ha_up"], 1)

            def moe_scale(t):
                act.wait_ge(s["h_tk"], 2 * t + 2)
                if t == 0:
                    act.wait_ge(s["gp_out"], TILES)
                if t >= 2:
                    act.wait_ge(s["h_y"], 2 * t - 3)
                A(onT[:, t % 2, :], (O, PJ)[t % 2][:, 0:T], ACT.Copy, scale=rk[:, t:t + 1]).then_inc(s["h_moe"], 1)

            for n in SLOTS1:
                slot1(n)

            for m in range(FC, 2 * FC):
                moe_relu(m)
                if m == FC + 3:
                    moe_scale(3)
            for t in range(4, TILES):
                moe_scale(t)

        @block.gpsimd
        def _(pool):
            G = nc.gpsimd
            G.memset(v0[:, :, :, :, :, :], 0.0).then_inc(s["pool_zero"], 1)
            pool.wait_ge(s["pool_zero"], 1)
            G.memset(v0[:, :, :, :, :, 8:9], 1.0).then_inc(s["pool_zero"], 1)
            G.memset(mw[:, :, :, :], 0.0).then_inc(s["pool_mw"], 1)
            pool.wait_ge(s["ld_first"], 32)

            variances = []

            def inv_std(t, ready, k, done):
                pool.wait_ge(s[ready], k)
                G.tensor_scalar(rstd[:, t:t + 1], mv[:, t, 1:2], EPS, None, ALU.add).then_inc(s["pool_var"], 1)
                variances.append(t)
                pool.wait_ge(s["pool_var"], len(variances))
                G.tensor_tensor(rstd[:, t:t + 1], rstd[:, t:t + 1], cols[:, 2:3], ALU.pow).then_inc(s[done], 1)

            def keys(t, b, g):
                pool.wait_ge(s["dve_mix"], 4 * t + g + 1)
                if t == 0 and (b, g) == (0, 0):
                    pool.wait_ge(s["ld_small"], 64)
                if t >= 2:
                    pool.wait_ge(s["pe_st"], UNITS * (t - 2) + 8 * b + 4 * g + 4)
                G.tensor_tensor(r32(kb[:, t % 2, g, :, b, :]), kp[:, g, b:b + 1, :].to_broadcast([P, 4, T]),
                                kmask[:, :, None].to_broadcast([P, 4, T]), ALU.mult).then_inc(s["pool_kb"], 1)

            def slot_(T_, l):
                t = T_ + 2
                if l == 3 and 0 <= t < TILES:
                    inv_std(t, "dve_ln", 2 * t + 2, "pool_rstd")
                t = T_ - 2
                if l == 13 and 0 <= t < TILES:
                    inv_std(t, "f_ln", 2 * t + 2, "f_rstd")
                if T_ >= 0:
                    t, r = place(T_, l, ST_LAG + 1)
                    if r % 2 == 0 and live(t, r):
                        n = UNITS * t + r
                        b, g, c, w = parts(r)
                        e = ex[:, (n // 2) % 4, :, :]
                        pool.wait_ge(s["act_exp"], n + 2)
                        if c == 0:
                            G.affine_select(out=e[:, :, 0:64], in_=e[:, :, 0:64], compare_op=ALU.is_ge, fill=0.0, base=BAND,
                                            pattern=[[0, 4], [1, 64]], channel_multiplier=-1)
                            G.affine_select(out=e[:, :, 64:WIN], in_=e[:, :, 64:WIN], compare_op=ALU.is_ge, fill=0.0, base=0,
                                            pattern=[[0, 4], [-1, 128]], channel_multiplier=1).then_inc(s["pool_sel"], 1)
                        else:
                            G.affine_select(out=e[:, :, 0:128], in_=e[:, :, 0:128], compare_op=ALU.is_ge, fill=0.0, base=0,
                                            pattern=[[0, 4], [1, 128]], channel_multiplier=-1)
                            G.affine_select(out=e[:, :, 128:WIN], in_=e[:, :, 128:WIN], compare_op=ALU.is_ge, fill=0.0, base=0,
                                            pattern=[[0, 4], [-1, 64]], channel_multiplier=1).then_inc(s["pool_sel"], 1)
                t = T_ + 1
                if l in KB and 0 <= t < TILES:
                    keys(t, *KB[l])
            for T_, l in SLOTS_ALL:
                slot_(T_, l)

            G.memset(v1[:, :, :, :, :], 0.0).then_inc(s["pool_zero"], 1)
            pool.wait_ge(s["pool_zero"], 3)
            for j2 in range(2):
                G.memset(v1[64 * j2:64 * j2 + 64, :, :, :, 16 * j2 + 8:16 * j2 + 9], 1.0).then_inc(s["pool_zero"], 1)
                pool.wait_ge(s["pool_zero"], 4 + j2)
            def keys1(p, tt):
                t = 2 * p + tt
                pool.wait_ge(s["g_mk"], p + 1)
                if t == 0:
                    pool.wait_ge(s["pe_st"], ALL_UNITS)
                if t >= 4:
                    pool.wait_ge(s["gp_st"], 4 * (t - 3))
                for g in range(2):
                    G.tensor_tensor(r32(k1[:, t % 4, g, :, :, :]),
                                    k1p.rearrange("p (g t b k) -> p g t b k", g=2, t=2, b=2)[:, g, tt, :, None, :].to_broadcast([P, 2, 4, 64]),
                                    kmask[:, None, :, None].to_broadcast([P, 2, 4, 64]), ALU.mult).then_inc(s["gpool_k"], 1)

            def slot1(n):
                for tt in range(2):
                    p = at(n, -17 + tt, 8, PAIRS)
                    if p is not None:
                        inv_std(2 * p + tt, "g_ln", 2 * (2 * p + tt) + 2, "g_rstd")
                i = at(n, 30, 1, 4)
                if i is not None:
                    k, c = divmod(i, 2)
                    pool.wait_ge(s["ha_w"], i + 1)
                    cs = slice(512 * c, 512 * c + 512)
                    G.tensor_tensor(r32(up2[:, 1, k, cs]), up[:, k, cs], up2[:, 0, k, cs], ALU.subtract).then_inc(s["hpool_w"], 1)
                if n == 38:
                    pool.wait_ge(s["ha_w"], 5)
                    G.tensor_tensor(r32(eg2[:, 1, :, :]), eg[:, :, :], eg2[:, 0, :, :], ALU.subtract).then_inc(s["hpool_w"], 1)
                t = at(n, 11, 4, TILES)
                if t is not None:
                    pool.wait_ge(s["f_x"], t + 1)
                    if t >= 2:
                        pool.wait_ge(s["g_x"], t - 1)
                    G.tensor_tensor(yr[:, t % 2, :], x[:, t, :], vecs[:, 2, :], ALU.add).then_inc(s["g_y"], 1)
                t = at(n, 18, 4, TILES)
                if t is not None:
                    inv_std(t, "h_ln", 2 * t + 2, "h_rstd")
                for tt in range(2):
                    p = at(n, -6 + 2 * tt, 8, PAIRS)
                    if p:
                        keys1(p, tt)
                    if n == -15 + tt:
                        keys1(0, tt)
            for n in SLOTS1:
                slot1(n)

            def moe_norm(t):
                pool.wait_ge(s["g_x"], t + 1)
                if t == 0:
                    pool.wait_ge(s["gp_bt"], TILES)
                if t >= 2:
                    pool.wait_ge(s["h_out"], t - 1)
                G.tensor_tensor(on[:, t % 2, :], x[:, t, :], vecs[:, 4, :], ALU.add).then_inc(s["h_xb"], 1)
                inv_std(t, "h_ln2", 2 * t + 2, "h_rstd2")

            for t in range(3):
                moe_norm(t)
            for f in range(FC):
                pool.wait_ge(s["ha_up"], FC + f + 1)
                if f == 0:
                    pool.wait_ge(s["hp_dn"], 4)
                G.tensor_tensor(hT[:, f, :], relu(FC + f), relu(FC + f), ALU.mult).then_inc(s["hpool_up"], 1)
            for t in range(3, TILES):
                moe_norm(t)

        @block.vector
        def _(dve):
            V = nc.vector

            def stats(t, src, name, k):
                V.bn_stats(st6[:, t % 2, :], src).then_inc(s[name], 1)
                dve.wait_ge(s[name], k + 1)
                V.bn_aggr(mv[:, t, :], st6[:, t % 2, :]).then_inc(s[name], 1)

            def normalise(dst, t, name):
                V.tensor_scalar(dst, x[:, t, :], mv[:, t, 0:1], rstd[:, t:t + 1], ALU.subtract, ALU.mult).then_inc(s[name], 1)

            V.memset(w0l[:, :, :, :], 0.0).then_inc(s["dve_zero"], 1)
            dve.wait_ge(s["ld_first"], 32)
            stats(0, x[:, 0, :], "dve_ln", 0)
            dve.wait_ge(s["ld_w0"], 32)
            V.tensor_copy(r32(w0h[:, :, :]), w0[:, :, :]).then_inc(s["dve_w"], 1)
            for n in range(4):
                last = V.tensor_tensor(sb0[:, n:n + 1], b0[:, n:n + 1], cols[:, n // 2:n // 2 + 1], ALU.mult)
            last.then_inc(s["dve_w"], 1)
            dve.wait_ge(s["pool_rstd"], 1)
            normalise(xn[:, 0, :], 0, "dve_xn")
            dve.wait_ge(s["dve_w"], 2)
            dve.wait_ge(s["dve_zero"], 1)
            for b in range(2):
                hp = slice(64 * b, 64 * b + 64)
                V.tensor_tensor(r32(w0l[hp, b, :, :]), w0[hp, :, :], w0h[hp, :, :], ALU.subtract).then_inc(s["dve_w"], 1)

            def slot_(T_, l):
                t, r = T_, l
                if live(t, r):
                    n = UNITS * t + r
                    b, g, c, w = parts(r)
                    dve.wait_ge(s["pe_s"], n + 1)
                    if n == 0:
                        dve.wait_ge(s["pool_mw"], 1)
                        dve.wait_ge(s["dve_band"], 1)
                    if r % 8 == 0 and n >= 16:
                        dve.wait_ge(s["pe_mt"], 2 * t + b - 1)
                    if n >= 2:
                        dve.wait_ge(s["dve_max"], n - 1)
                    for h in range(2):
                        last = V.tensor_tensor_reduce(out=masked[:, n % 2, h, :], in0=S[n % 2][:, WIN * h:WIN * h + WIN], in1=band[:, c, :], scale=1.0,
                                                      scalar=NEG, op0=ALU.add, op1=ALU.max,
                                                      accum_out=mw[:, b, 2 * c + g, 96 + 2 * w + h:97 + 2 * w + h])
                    last.then_inc(s["dve_max"], 1)
                t, r = place(T_, l, 27)
                if l % 8 == 3 and live(t, r):
                    k = 2 * t + r // 8
                    b = k % 2
                    dve.wait_ge(s["pe_ot"], k + 1)
                    ot = XB[:, :].rearrange("p (c g f) -> p c g f", c=2, f=32)
                    V.reciprocal(rc[:, b, 0:16].rearrange("p (c g) -> p c g", c=2), ot[:, :, :, 8]).then_inc(s["dve_rc"], 1)
                    dve.wait_ge(s["dve_rc"], k + 1)
                    if b == 0 and t >= 1:
                        dve.wait_ge(s["pe_bt"], t)
                    V.tensor_tensor(on[:, :, 64 * b:64 * b + 64].rearrange("p c (g d) -> p c g d", g=8), ot[:, :, :, 0:8],
                                    rc[:, b, 0:16].rearrange("p (c g) -> p c g", c=2)[:, :, :, None].to_broadcast([P, 2, 8, 8]),
                                    ALU.mult).then_inc(s["dve_on"], 1)
                t = T_ - 2
                if 0 <= t < TILES:
                    if l == 6:
                        dve.wait_ge(s["act_relu"], t + 1)
                        if t == 0:
                            dve.wait_ge(s["ld_rest"], 64)
                        if t >= 1:
                            dve.wait_ge(s["pe_wct"], t)
                        V.tensor_tensor(yr[:, 1, :], yr[:, 0, :], cx[:, t, :], ALU.mult).then_inc(s["dve_y"], 1)
                    if l == 8:
                        dve.wait_ge(s["pe_wct"], t + 1)
                        V.scalar_tensor_tensor(out=x[:, t, :], in0=XB[:, 0:T], scalar=bcol[:, 2:3], in1=x[:, t, :],
                                               op0=ALU.add, op1=ALU.add).then_inc(s["dve_x"], 1)
                    if l == 12:
                        dve.wait_ge(s["dve_x"], t + 1)
                        stats(t, x[:, t, :], "f_ln", 2 * t)
                    if l == 15:
                        dve.wait_ge(s["f_rstd"], t + 1)
                        if t == 0:
                            dve.wait_ge(s["ld_sel"], 96)
                            V.tensor_copy(r32(spread[:, :, :, :].rearrange("p a b c -> p (a b c)")), hT[:, 0:2, :].rearrange("p a b -> p (a b)"))\
                                .then_inc(s["dve_spread"], 1)
                            dve.wait_ge(s["dve_spread"], 1)
                        V.tensor_scalar(x_norm(t), x[:, t, :], mv[:, t, 0:1], rstd[:, t:t + 1], ALU.subtract, ALU.mult).then_inc(s["f_xn"], 1)
                t = T_ - 3
                if 0 <= t < TILES:
                    if l == 0:
                        dve.wait_ge(s["f_xn"], 2 * t + 1)
                        V.tensor_tensor_reduce(out=cmp[:, 0:2, :].rearrange("p a b -> p (a b)"), in0=x_norm(t), in1=vecs[:, 0, :], scale=1.0,
                                               scalar=0.0, op0=ALU.mult, op1=ALU.add, accum_out=sc[:, t:t + 1]).then_inc(s["f_xn"], 1)
                        dve.wait_ge(s["f_xn"], 2 * t + 2)
                        V.tensor_scalar(sc[:, t:t + 1], sc[:, t:t + 1], br[:, 0:1], None, ALU.add).then_inc(s["f_sc"], 1)
                if l == 5 and 0 <= t < TILES:
                    dve.wait_ge(s["fp_sT"], t + 1)
                    V.scalar_tensor_tensor(out=cmp[:, 0, :], in0=MT[:, 0:P], scalar=sc[:, t:t + 1], in1=blk[:, :], op0=ALU.is_gt, op1=ALU.mult,
                                           accum_out=rk[:, 0:1])
                    V.scalar_tensor_tensor(out=cmp[:, 1, :], in0=MT[:, 0:P], scalar=sc[:, t:t + 1], in1=tri[:, :], op0=ALU.is_equal, op1=ALU.mult,
                                           accum_out=rk[:, 1:2]).then_inc(s["f_cmp"], 1)
                    dve.wait_ge(s["f_cmp"], t + 1)
                    if t >= 2:
                        dve.wait_ge(s["fp_x"], t - 1)
                    V.tensor_scalar(sel[:, t % 2, :], slot[:, P * (t % 2):P * (t % 2) + P], rk[:, 0:1], rk[:, 1:2], ALU.subtract, ALU.is_equal)\
                        .then_inc(s["f_sel"], 1)
                if T_ == 1 and l == 2:
                    dve.wait_ge(s["pe_bias"], 1)
                    V.tensor_tensor(bcol[:, 3:4], XB[:, 0:1], bcol[:, 1:2], ALU.add).then_inc(s["dve_w"], 1)
                t = T_ + 2
                if 0 <= t < TILES:
                    if l == 2 and t >= 1:
                        if t == 1:
                            dve.wait_ge(s["ld_x1"], 16)
                        if t == 2:
                            dve.wait_ge(s["ld_x"], 16)
                        stats(t, x[:, t, :], "dve_ln", 2 * t)
                    if l == 9 and t >= 1:
                        dve.wait_ge(s["pool_rstd"], t + 1)
                        if t >= 2:
                            dve.wait_ge(s["pe_v"], t - 1)
                        normalise(xn[:, t % 2, :], t, "dve_xn")
                t = T_ + 1
                if l == 1 and 0 <= t < TILES:
                    dve.wait_ge(s["act_xh"], t + 1)
                    V.tensor_tensor(r32(xs[64:128, 0, :]), xn[0:64, t % 2, :], xs[0:64, 0, :], ALU.subtract)
                    V.tensor_tensor(r32(xs[0:64, 1, :]), xn[64:128, t % 2, :], xs[64:128, 1, :], ALU.subtract)\
                        .then_inc(s["dve_xl"], 1)
                if (T_, l) == (-1, 2):
                    dve.wait_ge(s["ld_small"], 64)
                    V.tensor_copy(band[:, :, :], exf[:, 0:2 * WIN].rearrange("p (c k) -> p c k", c=2)).then_inc(s["dve_band"], 1)
                t = T_ + 1
                if l - 1 in PROJ and 0 <= t < TILES:
                    n = PROJ[l - 1]
                    m, g = 4 * t + n, n % 2
                    dve.wait_ge(s["act_hs"], m + 1)
                    if n < 2 and t >= 1:
                        dve.wait_ge(s["pool_kb"], 3 * t)
                        if g == 1:
                            dve.wait_ge(s["act_kb"], t)
                    if n >= 2 and t >= 2:
                        dve.wait_ge(s["pe_st"], UNITS * (t - 2) + 8 + 4 * g + 4)
                    dst = (qp[:, t % 2, g, :, :] if n >= 2 else kp[:, g, :, :]).rearrange("p b q -> p (b q)")
                    V.scalar_tensor_tensor(out=r32(dst), in0=proj_bank(t, n)[:, :], scalar=b0[:, n:n + 1], in1=hs[:, m % 2, :],
                                           op0=ALU.add, op1=ALU.subtract).then_inc(s["dve_mix"], 1)
                if (T_, l) == (TILES + 2, 6):
                    keys1(0)
                if T_ == TILES + 1 and l in (13, 14):
                    ffn_out(l - 13)
                kind, n = tail(*place(T_, l, 1))
                if kind == "scatter":
                    ffn_add(n)

            def keys1(p):
                dve.wait_ge(s["ga_hk"], p + 1)
                if p >= 1:
                    dve.wait_ge(s["gpool_k"], 4 * p)
                V.scalar_tensor_tensor(out=r32(k1p), in0=PJ[:, :], scalar=cols[:, 3:4], in1=k1h,
                                       op0=ALU.add, op1=ALU.subtract).then_inc(s["g_mk"], 1)

            def ffn_out(c):
                dve.wait_ge(s["fp_dn"], c + 1)
                V.tensor_tensor(osel[:, c, :], down_bank(c), vecs[:, 1, :], ALU.add).then_inc(s["f_dn"], 1)

            def ffn_add(t):
                dve.wait_ge(s["fp_sc"], t + 1)
                V.tensor_tensor(x[:, t, :], scatter_bank(t), x[:, t, :], ALU.add).then_inc(s["f_x"], 1)

            for T_, l in SLOTS_ALL:
                slot_(T_, l)

            def slot1(n):
                c = at(n, -4, 8, 2)
                if c is not None:
                    ffn_out(2 + c)
                t = at(n, 21, 4, TILES)
                if t is not None:
                    dve.wait_ge(s["ha_xT"], t + 1)
                    V.tensor_tensor(r32(xq[t // 4][:, t % 4, 1, :, :]), MT[:, 0:T].rearrange("p (k c) -> p k c", k=2),
                                    xq[t // 4][:, t % 4, 0, :, :], ALU.subtract).then_inc(s["hl_xT"], 1)
                u = at(n, 0, 1, 4 * TILES)
                if u is not None:
                    k, g = divmod(u, 2)
                    dve.wait_ge(s["gp_s"], u + 1)
                    if k >= 2 and g == 0:
                        dve.wait_ge(s["gp_mt"], k - 1)
                    V.tensor_reduce(mw[:, k % 2, 2 * g:2 * g + 2, 96:100], S[0][:, :].rearrange("p (i j k) -> p i j k", i=2, j=4),
                                    AX, ALU.max).then_inc(s["g_max"], 1)
                for t in SCATTER1.get(n - 1, ()):
                    ffn_add(t)
                p = at(n, -9, 8, PAIRS)
                if p is not None:
                    dve.wait_ge(s["ga_hq"], p + 1)
                    V.tensor_tensor(r32(hs[:, 1, :]), PJ[:, :], hs[:, 0, :], ALU.subtract).then_inc(s["g_lq"], 1)
                p = at(n, -7, 8, PAIRS)
                if p:
                    keys1(p)
                for i in (1, 2):
                    p = at(n, SPREAD[i] + 1, 8, PAIRS)
                    if p is not None:
                        dve.wait_ge(s["gp_e"], 4 * p + i + 1)
                        if p >= 3:
                            dve.wait_ge(s["gp_st"], 8 * (p - 2))
                        V.tensor_copy(stacked(p, i), S[1][:, :].rearrange("p (g t q) -> p g t q", g=2, t=4)).then_inc(s["g_q"], 1)
                t = at(n, 15, 4, TILES)
                if t is not None:
                    dve.wait_ge(s["gp_out"], t + 1)
                    dve.wait_ge(s["g_y"], t + 1)
                    V.tensor_tensor(x[:, t, :], XB[:, T:2 * T], yr[:, t % 2, :], ALU.add).then_inc(s["g_x"], 1)
                t = at(n, 12, 4, TILES)
                if t is not None:
                    dve.wait_ge(s["gp_ot"], t + 1)
                    ot = XB[:, :].rearrange("p (i g f) -> p i g f", i=4, f=16)
                    rv = rc[:, t % 2, :].rearrange("p (i g) -> p i g", i=4)
                    V.reciprocal(rv, ot[:, :, :, 8]).then_inc(s["g_rc"], 1)
                    dve.wait_ge(s["g_rc"], t + 1)
                    if t >= 2:
                        dve.wait_ge(s["gp_bt"], t - 1)
                    V.tensor_tensor(on[:, t % 2, :].rearrange("p (g i d) -> p i g d", g=8, i=4), ot[:, :, :, 0:8],
                                    rv[:, :, :, None].to_broadcast([P, 4, 8, 8]), ALU.mult).then_inc(s["g_on"], 1)
                for tt in range(2):
                    p = at(n, -18 + tt, 8, PAIRS)
                    if p is not None:
                        t = 2 * p + tt
                        dve.wait_ge(s["f_x"], t + 1)
                        stats(t, x[:, t, :], "g_ln", 2 * t)
                    p = at(n, -16 + tt, 8, PAIRS)
                    if p is not None:
                        t = 2 * p + tt
                        dve.wait_ge(s["g_rstd"], t + 1)
                        if p >= 1:
                            dve.wait_ge(s["gp_xT"], p)
                        normalise(xn[:, tt, :], t, "g_xn")
                t = at(n, 17, 4, TILES)
                if t is not None:
                    dve.wait_ge(s["g_x"], t + 1)
                    stats(t, x[:, t, :], "h_ln", 2 * t)
                t = at(n, 18, 4, TILES)
                if t is not None:
                    dve.wait_ge(s["h_rstd"], t + 1)
                    if t >= 2:
                        dve.wait_ge(s["hp_xT"], t - 1)
                    elif t == 0:
                        dve.wait_ge(s["gp_xT"], PAIRS)
                    normalise(xn[:, t % 2, :], t, "h_xn")
                f = at(n, 36, 1, FC)
                if f is not None:
                    moe_square(f)
                t = MOE_OUT.get(n)
                if t is not None:
                    moe_out(t)

            def moe_square(m):
                dve.wait_ge(s["ha_up"], m + 1)
                V.tensor_tensor(hT[:, m, :], relu(m), relu(m), ALU.mult).then_inc(s["h_up"], 1)

            def moe_out(t):
                dve.wait_ge(s["hp_eg"], t + 1)
                gp = (O, PJ)[t % 2]
                V.max(out=tk[:, t % 2, :], in_=gp[:, T:T + NEXP]).then_inc(s["h_tk"], 1)
                dve.wait_ge(s["h_tk"], 2 * t + 1)
                V.tensor_tensor(rk[:, t:t + 1], tk[:, t % 2, 0:1], tk[:, t % 2, 1:2], ALU.add).then_inc(s["h_tk"], 1)
                dve.wait_ge(s["h_moe"], t + 1)
                dve.wait_ge(s["hp_dn"], t + 1)
                V.tensor_tensor(yr[:, 0, :], ST[t % 2][:, 0:T], onT[:, t % 2, :], ALU.add).then_inc(s["h_y"], 1)
                dve.wait_ge(s["h_y"], 2 * t + 1)
                stats(t, yr[:, 0, :], "h_ln2", 2 * t)
                dve.wait_ge(s["h_ln2"], 2 * t + 2)
                V.scalar_tensor_tensor(out=yr[:, 1, :], in0=yr[:, 0, :], scalar=mv[:, t, 0:1], in1=vecs[:, 3, :],
                                       op0=ALU.subtract, op1=ALU.mult).then_inc(s["h_y"], 1)
                dve.wait_ge(s["h_y"], 2 * t + 2)
                dve.wait_ge(s["h_xb"], t + 1)
                dve.wait_ge(s["h_rstd2"], t + 1)
                V.scalar_tensor_tensor(out=x[:, t, :], in0=yr[:, 1, :], scalar=rstd[:, t:t + 1], in1=on[:, t % 2, :],
                                       op0=ALU.mult, op1=ALU.add).then_inc(s["h_out"], 1)

            for n in SLOTS1:
                slot1(n)

            for t in range(3, TILES):
                moe_out(t)


def constants():
    i = np.arange(P)
    ident = np.eye(P, dtype=np.float32)
    c = {"ident": ident}
    band = np.zeros((P, 2, WIN), np.float32)
    for ch in range(2):
        q = P * ch + i[:, None]
        k = BAND * ch + np.arange(WIN)[None, :]
        band[:, ch] = np.where(np.abs(q - k) <= BAND, 0.0, NEG)
    c["band"] = band.reshape(P, 2 * WIN)
    kmask = np.zeros((P, 4), np.float32)
    for r in range(3):
        for j in range(4):
            kmask[32 * r + 8 * j:32 * r + 8 * j + 8, j] = 1
    for j in range(4):
        kmask[96 + j, j] = 1
    c["kmask"] = kmask
    cols = np.zeros((P, 4), np.float32)
    cols[32:64, 0] = 1
    cols[64:96, 1] = 1
    cols[:, 2] = -0.5
    cols[96:128, 3] = 1
    c["cols"] = cols
    same = (i[:, None] // 64) == (i[None, :] // 64)
    c["blk"] = same.astype(np.float32)
    c["tri"] = (same & (i[None, :] < i[:, None])).astype(np.float32)
    slot = np.full((P, 2, 2, 2, KEEP), -1, np.float32)
    for par in range(2):
        for b in range(2):
            slot[64 * b:64 * b + 64, par, par, b] = np.arange(KEEP)
    c["slot"] = slot.reshape(P, 2 * P)
    spread = np.zeros((4, 4, 8, 2, 4, 4, 4, 8), np.float32)
    for j in range(4):
        for i in range(4):
            for d in range(8):
                for r in range(3):
                    spread[j, i, d, r // 2, i, r, j, d] = 1
    c["spread"] = spread.reshape(P, -1)
    return c


def kernel(**inputs):
    import concourse.bacc as bacc
    from concourse.bass_utils import run_bass_kernel_spmd

    f = {k: np.asarray(v) for k, v in inputs.items()}
    arr = constants()
    arr["x"] = f["x"].reshape(N * E, T)
    arr["cx"] = f["ctx_2048"].reshape(N * E, T)
    arr["cxT"] = np.ascontiguousarray(arr["cx"].T)
    w_in, b_in = f["L0_xattn_w_in"], f["L0_xattn_b_in"]
    w0 = np.zeros((P, 4, 4, 32), np.float32)
    b0 = np.zeros((4, 32, 4), np.float32)
    for n, (typ, g) in enumerate(((1, 0), (1, 1), (0, 0), (0, 1))):
        rows = slice(64 * typ + 32 * g, 64 * typ + 32 * g + 32)
        for r in range(3):
            w0[0:64, n, r] = w_in[rows].T
            w0[64:128, n, r] = w_in[rows].T
            b0[r, :, n] = b_in[rows]
        if typ:
            b0[3, :, n] = 1
    arr["w0"] = w0.reshape(P, 4, P)
    arr["b0"] = b0.reshape(P, 4)

    def twice(w):
        out = np.zeros((P, P), np.float32)
        out[0:64, 0:64] = w
        out[64:128, 64:128] = w
        return out
    arr["wv0"] = twice(w_in[128:192].T)
    arr["wo0"] = twice(f["L0_xattn_w_out"].T)
    arr["wc0"] = twice(f["L0_xattn_w_ct"])
    bcol = np.zeros((P, 4), np.float32)
    for k, v in enumerate((b_in[128:192], f["L0_xattn_b_out"], f["L0_xattn_b_ct"])):
        bcol[0:64, k] = v
        bcol[64:128, k] = v
    arr["bcol"] = bcol
    arr["vecs"] = np.stack([f["L0_ffn_w_r"], f["L0_ffn_b2"], f["L1_xattn_bfc"], f["L1_ffn_ln_gamma"], f["L1_ffn_ln_beta"]])
    arr["br"] = f["L0_ffn_b_r"].reshape(1, 1)
    arr["b1"] = np.ascontiguousarray(f["L0_ffn_b1"].reshape(FC, P).T)
    arr["w1"], arr["w2"] = f["L0_ffn_w1"], f["L0_ffn_w2"]
    arr["wq1"] = np.ascontiguousarray(f["L1_xattn_Wq"].T)
    wk = f["L1_xattn_Wk"].reshape(2, 4, 8, 2, P)
    wk1 = np.zeros((P, 2, 2, 4, 4, 8), np.float32)
    for r in range(3):
        wk1[:, :, :, r] = wk.transpose(4, 3, 0, 1, 2)
    arr["wk1"] = wk1.reshape(P, -1)
    arr["wv1"] = np.ascontiguousarray(f["L1_xattn_Wv"].T)
    arr["wf1"] = np.ascontiguousarray(f["L1_xattn_Wfc"].T)
    arr["up"], arr["down"] = f["L1_ffn_up_w"], f["L1_ffn_down_w"]
    arr["ew"], arr["gw"] = f["L1_ffn_expert_weight"], f["L1_ffn_gate_w"]

    nc = bacc.Bacc("TRN2", target_bir_lowering=False, num_devices=1)
    aps, feed = {}, {}
    for name, v in arr.items():
        v = np.ascontiguousarray(v)
        feed[f"in_{name}"] = v
        aps[name] = nc.dram_tensor(f"in_{name}", v.shape, mybir.dt.from_np(v.dtype), kind="ExternalInput").ap()
    aps["out"] = nc.dram_tensor("out_0", (N * E, T), F32, kind="ExternalOutput").ap()
    build(nc, aps)
    res = run_bass_kernel_spmd(nc, [feed], core_ids=[0])
    return res.results[0]["out_0"].reshape(N, E, T)
```
